# Optimizing a Trainium2 kernel written in Bass

```python
import numpy as np
import jax
import jax.numpy as jnp

def _softmax(x, axis=-1):
    return jax.nn.softmax(x, axis=axis)

def _gelu(x):
    return jax.nn.gelu(x, approximate=True)

def _silu(x):
    return jax.nn.silu(x)

def _sigmoid(x):
    return jax.nn.sigmoid(x)

def _layernorm(x, axis=-1, eps=1e-05):
    m = jnp.mean(x, axis=axis, keepdims=True)
    v = jnp.var(x, axis=axis, keepdims=True)
    return (x - m) / jnp.sqrt(v + eps)

def _scatter_add(tgt, idx, src, axis=0):
    return tgt.at[idx].add(src)

def _segment_sum(src, seg, n):
    return jax.ops.segment_sum(src, seg, n)
kernel_name = 'mk_decoder_postln_d2_seqx_r8_31a823'

def setup_inputs(seed: int=0):
    np.random.seed(seed)
    _w = jnp.asarray

    def _rec_inputs():
        import jax
        import jax.numpy as jnp
        _rk = jax.random.key(seed)
        x = -0.000125 + 0.9999 * jax.random.normal(jax.random.fold_in(_rk, 1), (16, 128, 128), jnp.float32)
        _lenS = 128 - jax.random.randint(jax.random.fold_in(_rk, 7), (16,), 0, max(1, 128 // 4) + 1, jnp.int32)
        _lenS2 = 77 - jax.random.randint(jax.random.fold_in(_rk, 8), (16,), 0, max(1, 77 // 4) + 1, jnp.int32)
        _ctx_2048P = jax.random.normal(jax.random.fold_in(_rk, 11), (16, 16, 256), jnp.float32)
        _ctx_2048c = jax.random.dirichlet(jax.random.fold_in(_rk, 511), 0.3 * jnp.ones((16,), jnp.float32), (16, 77))
        _ctx_2048t = jnp.einsum('bsk,bkd->bsd', _ctx_2048c, _ctx_2048P)
        _ctx_2048t = _ctx_2048t * jax.lax.rsqrt(jnp.mean(jnp.square(_ctx_2048t)) + 1e-12) * 0.953939
        ctx_2048 = -1.39393e-06 + 0.999914 * (_ctx_2048t + 0.3 * jax.random.normal(jax.random.fold_in(_rk, 611), (16, 77, 256), jnp.float32))
        _validS = jnp.arange(128)[None, :] < _lenS[:, None]
        _validS2 = jnp.arange(77)[None, :] < _lenS2[:, None]
        _causal = jnp.tril(jnp.ones((128, 128), dtype=bool))
        mask_BxS2_if0 = jnp.where(jnp.ones((16, 77), dtype=bool), 4, 0).astype(jnp.int32)
        return (x, ctx_2048, mask_BxS2_if0)
    x, ctx_2048, mask_BxS2_if0 = _rec_inputs()

    def _L0_attn_setup():
        import jax, jax.numpy as jnp
        import numpy as np
        D_MODEL = 128
        N_HEAD = 16
        HEAD_DIM = D_MODEL // N_HEAD
        key = jax.random.key(seed)
        ks = jax.random.split(key, 5)
        x = jax.random.normal(ks[0], (4, 256, D_MODEL), dtype=jnp.float32)
        scale = 1.0 / np.sqrt(D_MODEL)
        W_qkv = jax.random.normal(ks[1], (D_MODEL, 3 * D_MODEL), dtype=jnp.float32) * scale
        b_qkv = jnp.zeros((3 * D_MODEL,), dtype=jnp.float32)
        W_proj = jax.random.normal(ks[2], (D_MODEL, D_MODEL), dtype=jnp.float32) * scale
        b_proj = jnp.zeros((D_MODEL,), dtype=jnp.float32)
        return {'x': x, 'W_qkv': W_qkv, 'b_qkv': b_qkv, 'W_proj': W_proj, 'b_proj': b_proj}
    _L0_attn_all = _L0_attn_setup()
    _L0_attn_in = {k: v for k, v in _L0_attn_all.items() if k in ('W_qkv', 'b_qkv', 'W_proj', 'b_proj')}
    del _L0_attn_all

    def _L0_xattn_setup():
        import jax, jax.numpy as jnp
        import numpy as np
        B, N, DIM = (8, 512, 128)
        M, CTX = (32, 256)
        HEADS, DH = (16, 64)
        INNER = HEADS * DH
        EPS = 1e-06

        def _split_heads(t):
            b, n, _ = t.shape
            return t.reshape(b, n, HEADS, DH).transpose(0, 2, 1, 3)
        key = jax.random.key(seed)
        ks = jax.random.split(key, 6)
        x = jax.random.normal(ks[0], (B, N, DIM), dtype=jnp.float32)
        context = jax.random.normal(ks[1], (B, M, CTX), dtype=jnp.float32)
        Wq = jax.random.normal(ks[2], (DIM, INNER), dtype=jnp.float32) / np.sqrt(DIM)
        Wkv = jax.random.normal(ks[3], (CTX, 2 * INNER), dtype=jnp.float32) / np.sqrt(CTX)
        null_kv = jax.random.normal(ks[4], (2, DH), dtype=jnp.float32) / np.sqrt(2.0)
        Wout = jax.random.normal(ks[5], (INNER, DIM), dtype=jnp.float32) / np.sqrt(INNER)
        ln_scale = jnp.ones((DIM,), dtype=jnp.float32)
        ln_bias = jnp.zeros((DIM,), dtype=jnp.float32)
        return {'x': x, 'context': context, 'Wq': Wq, 'Wkv': Wkv, 'null_kv': null_kv, 'Wout': Wout, 'ln_scale': ln_scale, 'ln_bias': ln_bias}
    _L0_xattn_all = _L0_xattn_setup()
    _L0_xattn_in = {k: v for k, v in _L0_xattn_all.items() if k in ('Wq', 'Wkv', 'null_kv', 'Wout', 'ln_scale', 'ln_bias')}
    del _L0_xattn_all

    def _L0_ffn_setup():
        import jax, jax.numpy as jnp
        import numpy as np
        B, S, D, H, E = (4, 256, 128, 256, 8)
        key = jax.random.key(seed)
        ks = jax.random.split(key, 8)
        scale = 0.02
        return {'x': jax.random.normal(ks[0], (B, S, D), dtype=jnp.float32), 'Wr': jax.random.normal(ks[1], (D, E), dtype=jnp.float32) * scale, 'br': jnp.zeros((E,), dtype=jnp.float32), 'W1': jax.random.normal(ks[2], (E, D, H), dtype=jnp.float32) * scale, 'b1': jnp.zeros((E, H), dtype=jnp.float32), 'W2': jax.random.normal(ks[3], (E, H, D), dtype=jnp.float32) * scale, 'b2': jnp.zeros((E, D), dtype=jnp.float32)}
    _L0_ffn_all = _L0_ffn_setup()
    _L0_ffn_in = {k: v for k, v in _L0_ffn_all.items() if k in ('Wr', 'br', 'W1', 'b1', 'W2', 'b2')}
    del _L0_ffn_all

    def _L1_attn_setup():
        import jax, jax.numpy as jnp
        import numpy as np
        D_MODEL = 128
        N_HEADS = 16
        SEQ = 64
        key = jax.random.key(seed)
        ks = jax.random.split(key, 12)
        B = 16
        x = jax.random.normal(ks[0], (B, SEQ, D_MODEL), dtype=jnp.float32)
        c = jax.random.normal(ks[1], (B, SEQ, 8), dtype=jnp.float32)
        s = 1.0 / np.sqrt(D_MODEL)
        Wq = jax.random.normal(ks[2], (D_MODEL, D_MODEL), dtype=jnp.float32) * s
        bq = jnp.zeros((D_MODEL,), dtype=jnp.float32)
        Wk = jax.random.normal(ks[3], (D_MODEL, D_MODEL), dtype=jnp.float32) * s
        bk = jnp.zeros((D_MODEL,), dtype=jnp.float32)
        Wv = jax.random.normal(ks[4], (D_MODEL, D_MODEL), dtype=jnp.float32) * s
        bv = jnp.zeros((D_MODEL,), dtype=jnp.float32)
        Wo = jax.random.normal(ks[5], (D_MODEL, D_MODEL), dtype=jnp.float32) * s
        bo = jnp.zeros((D_MODEL,), dtype=jnp.float32)
        rel_table = jax.random.normal(ks[6], (2 * SEQ - 1, N_HEADS), dtype=jnp.float32) * 0.02
        return {'x': x, 'c': c, 'Wq': Wq, 'bq': bq, 'Wk': Wk, 'bk': bk, 'Wv': Wv, 'bv': bv, 'Wo': Wo, 'bo': bo, 'rel_table': rel_table}
    _L1_attn_all = _L1_attn_setup()
    _L1_attn_in = {k: v for k, v in _L1_attn_all.items() if k in ('c', 'Wq', 'bq', 'Wk', 'bk', 'Wv', 'bv', 'Wo', 'bo', 'rel_table')}
    del _L1_attn_all

    def _L1_xattn_setup():
        import jax, jax.numpy as jnp
        import numpy as np
        B, L, P = (4, 512, 128)
        D_MODEL = 128
        D_GLOBAL = 256
        HEADDIM = 32
        EPSILON = 0.001
        RMS_EPS = 1e-05

        def rmsnorm(x, g, eps=RMS_EPS):
            var = jnp.mean(jnp.square(x), axis=-1, keepdims=True)
            return x * jax.lax.rsqrt(var + eps) * g

        def _hnet_depool(h, h_patch_full, patch_lens):
            h_patch = h_patch_full[..., :D_MODEL]
            bsz, plen = (h_patch.shape[0], h_patch.shape[1])
            seqlen = h.shape[1]
            logp = jnp.full((bsz, plen), -EPSILON, dtype=jnp.float32)
            bidx = jnp.cumsum(patch_lens, axis=1) - 1
            boundary_mask = jnp.zeros((bsz, seqlen), dtype=jnp.int32)
            boundary_mask = boundary_mask.at[jnp.arange(bsz)[:, None], bidx].set(1)
            dt = (-jnp.log(-jnp.expm1(logp))).astype(h_patch.dtype)
            x = h_patch / dt[..., None]
            n_heads = D_MODEL // HEADDIM
            A = -jnp.ones((n_heads,), dtype=jnp.float32)
            bcoef = jnp.exp(logp).astype(h_patch.dtype)
            x4 = x.reshape(bsz, plen, n_heads, HEADDIM)
            a = jnp.exp(dt[:, :, None] * A[None, None, :])
            u = (dt * bcoef)[:, :, None, None] * x4
            a_b = jnp.broadcast_to(a[..., None], u.shape)

            def comb(lft, rgt):
                aL, uL = lft
                aR, uR = rgt
                return (aL * aR, uL * aR + uR)
            _, s = jax.lax.associative_scan(comb, (a_b, u), axis=1)
            depool = s.reshape(bsz, plen, D_MODEL)
            plug = jnp.clip(jnp.cumsum(boundary_mask, axis=1) - 1, 0, plen - 1)
            depool_out = depool[jnp.arange(bsz)[:, None], plug]
            return depool_out + h
        key = jax.random.key(seed)
        k1, k2, k3, k4 = jax.random.split(key, 4)
        embeds = jax.random.normal(k1, (B, L, D_MODEL), dtype=jnp.float32)
        patch_embeds = jax.random.normal(k2, (B, P, D_GLOBAL), dtype=jnp.float32)
        patch_lens = jnp.full((B, P), L // P, dtype=jnp.int64)
        W_in = jax.random.normal(k3, (D_MODEL, D_MODEL), dtype=jnp.float32) * 0.02
        b_in = jnp.zeros((D_MODEL,), dtype=jnp.float32)
        g_res = jnp.ones((D_MODEL,), dtype=jnp.float32)
        g_init = jnp.ones((D_GLOBAL,), dtype=jnp.float32)
        return {'embeds': embeds, 'patch_embeds': patch_embeds, 'patch_lens': patch_lens, 'W_in': W_in, 'b_in': b_in, 'g_res': g_res, 'g_init': g_init}
    _L1_xattn_all = _L1_xattn_setup()
    _L1_xattn_in = {k: v for k, v in _L1_xattn_all.items() if k in ('W_in', 'b_in', 'g_res', 'g_init')}
    del _L1_xattn_all

    def _L1_ffn_setup():
        import jax, jax.numpy as jnp
        import numpy as np
        H = 8
        KD = 128
        TOPK = 8
        NUM_KEYS = 32
        N_EXPERTS = NUM_KEYS * NUM_KEYS
        N_DIM = 128
        BN_EPS = 1e-05

        def gelu_new(x):
            c = jnp.sqrt(jnp.asarray(2.0 / jnp.pi, x.dtype))
            return 0.5 * x * (1.0 + jnp.tanh(c * (x + 0.044715 * x * x * x)))
        key = jax.random.key(seed)
        ks = jax.random.split(key, 5)
        b, s = (2, 128)
        x = jax.random.normal(ks[0], (b, s, N_DIM), dtype=jnp.float32)
        w_q = jax.random.normal(ks[1], (N_DIM, 2 * H * KD), dtype=jnp.float32) * 0.02
        bn_gamma = jnp.ones((2 * H * KD,), dtype=jnp.float32)
        bn_beta = jnp.zeros((2 * H * KD,), dtype=jnp.float32)
        keys = jax.random.normal(ks[2], (H, NUM_KEYS, 2, KD), dtype=jnp.float32) * 0.02
        down_embed = jax.random.normal(ks[3], (N_EXPERTS, N_DIM), dtype=jnp.float32) * 0.02
        up_embed = jax.random.normal(ks[4], (N_EXPERTS, N_DIM), dtype=jnp.float32) * 0.02
        return {'x': x, 'w_q': w_q, 'bn_gamma': bn_gamma, 'bn_beta': bn_beta, 'keys': keys, 'down_embed': down_embed, 'up_embed': up_embed}
    _L1_ffn_all = _L1_ffn_setup()
    _L1_ffn_in = {k: v for k, v in _L1_ffn_all.items() if k in ('w_q', 'bn_gamma', 'bn_beta', 'keys', 'down_embed', 'up_embed')}
    del _L1_ffn_all
    return {'x': x, 'ctx_2048': ctx_2048, 'mask_BxS2_if0': mask_BxS2_if0, 'L0_attn_W_qkv': _L0_attn_in['W_qkv'], 'L0_attn_b_qkv': _L0_attn_in['b_qkv'], 'L0_attn_W_proj': _L0_attn_in['W_proj'], 'L0_attn_b_proj': _L0_attn_in['b_proj'], 'L0_xattn_Wq': _L0_xattn_in['Wq'], 'L0_xattn_Wkv': _L0_xattn_in['Wkv'], 'L0_xattn_null_kv': _L0_xattn_in['null_kv'], 'L0_xattn_Wout': _L0_xattn_in['Wout'], 'L0_xattn_ln_scale': _L0_xattn_in['ln_scale'], 'L0_xattn_ln_bias': _L0_xattn_in['ln_bias'], 'L0_ffn_Wr': _L0_ffn_in['Wr'], 'L0_ffn_br': _L0_ffn_in['br'], 'L0_ffn_W1': _L0_ffn_in['W1'], 'L0_ffn_b1': _L0_ffn_in['b1'], 'L0_ffn_W2': _L0_ffn_in['W2'], 'L0_ffn_b2': _L0_ffn_in['b2'], 'L1_attn_c': _L1_attn_in['c'], 'L1_attn_Wq': _L1_attn_in['Wq'], 'L1_attn_bq': _L1_attn_in['bq'], 'L1_attn_Wk': _L1_attn_in['Wk'], 'L1_attn_bk': _L1_attn_in['bk'], 'L1_attn_Wv': _L1_attn_in['Wv'], 'L1_attn_bv': _L1_attn_in['bv'], 'L1_attn_Wo': _L1_attn_in['Wo'], 'L1_attn_bo': _L1_attn_in['bo'], 'L1_attn_rel_table': _L1_attn_in['rel_table'], 'L1_xattn_W_in': _L1_xattn_in['W_in'], 'L1_xattn_b_in': _L1_xattn_in['b_in'], 'L1_xattn_g_res': _L1_xattn_in['g_res'], 'L1_xattn_g_init': _L1_xattn_in['g_init'], 'L1_ffn_w_q': _L1_ffn_in['w_q'], 'L1_ffn_bn_gamma': _L1_ffn_in['bn_gamma'], 'L1_ffn_bn_beta': _L1_ffn_in['bn_beta'], 'L1_ffn_keys': _L1_ffn_in['keys'], 'L1_ffn_down_embed': _L1_ffn_in['down_embed'], 'L1_ffn_up_embed': _L1_ffn_in['up_embed']}

def reference(x, ctx_2048, mask_BxS2_if0, L0_attn_W_qkv, L0_attn_b_qkv, L0_attn_W_proj, L0_attn_b_proj, L0_xattn_Wq, L0_xattn_Wkv, L0_xattn_null_kv, L0_xattn_Wout, L0_xattn_ln_scale, L0_xattn_ln_bias, L0_ffn_Wr, L0_ffn_br, L0_ffn_W1, L0_ffn_b1, L0_ffn_W2, L0_ffn_b2, L1_attn_c, L1_attn_Wq, L1_attn_bq, L1_attn_Wk, L1_attn_bk, L1_attn_Wv, L1_attn_bv, L1_attn_Wo, L1_attn_bo, L1_attn_rel_table, L1_xattn_W_in, L1_xattn_b_in, L1_xattn_g_res, L1_xattn_g_init, L1_ffn_w_q, L1_ffn_bn_gamma, L1_ffn_bn_beta, L1_ffn_keys, L1_ffn_down_embed, L1_ffn_up_embed):
    import jax
    import jax.numpy as jnp

    def _L0_attn_ref(x, W_qkv, b_qkv, W_proj, b_proj):
        import jax, jax.numpy as jnp
        import numpy as np
        D_MODEL = 128
        N_HEAD = 16
        HEAD_DIM = D_MODEL // N_HEAD
        B, T, C = x.shape
        qkv = x @ W_qkv + b_qkv
        q, k, v = jnp.split(qkv, 3, axis=-1)
        q = q.reshape(B, T, N_HEAD, HEAD_DIM).transpose(0, 2, 1, 3)
        k = k.reshape(B, T, N_HEAD, HEAD_DIM).transpose(0, 2, 1, 3)
        v = v.reshape(B, T, N_HEAD, HEAD_DIM).transpose(0, 2, 1, 3)
        att = jnp.einsum('bhqd,bhkd->bhqk', q, k) / jnp.sqrt(jnp.asarray(HEAD_DIM, x.dtype))
        causal = jnp.tril(jnp.ones((T, T), dtype=bool))
        att = jnp.where(causal[None, None], att, jnp.asarray(-jnp.inf, att.dtype))
        att = jax.nn.softmax(att, axis=-1)
        out = jnp.einsum('bhqk,bhkd->bhqd', att, v)
        out = out.transpose(0, 2, 1, 3).reshape(B, T, C)
        return out @ W_proj + b_proj

    def _L0_xattn_ref(x, context, Wq, Wkv, null_kv, Wout, ln_scale, ln_bias):
        import jax, jax.numpy as jnp
        import numpy as np
        B, N, DIM = (8, 512, 128)
        M, CTX = (32, 256)
        HEADS, DH = (16, 64)
        INNER = HEADS * DH
        EPS = 1e-06

        def _split_heads(t):
            b, n, _ = t.shape
            return t.reshape(b, n, HEADS, DH).transpose(0, 2, 1, 3)
        scale = DH ** (-0.5)
        b = x.shape[0]
        q = _split_heads(jnp.einsum('bnd,df->bnf', x, Wq))
        kv = jnp.einsum('bmc,cf->bmf', context, Wkv)
        k, v = jnp.split(kv, 2, axis=-1)
        k, v = (_split_heads(k), _split_heads(v))
        nk = jnp.broadcast_to(null_kv[0], (b, HEADS, 1, DH))
        nv = jnp.broadcast_to(null_kv[1], (b, HEADS, 1, DH))
        k = jnp.concatenate((nk, k), axis=-2)
        v = jnp.concatenate((nv, v), axis=-2)
        q = q * scale
        sim = jnp.einsum('bhid,bhjd->bhij', q, k)
        attn = jax.nn.softmax(sim, axis=-1)
        out = jnp.einsum('bhij,bhjd->bhid', attn, v)
        out = out.transpose(0, 2, 1, 3).reshape(b, -1, INNER)
        out = jnp.einsum('bnf,fd->bnd', out, Wout)
        mu = jnp.mean(out, axis=-1, keepdims=True)
        var = jnp.var(out, axis=-1, keepdims=True)
        out = (out - mu) * jax.lax.rsqrt(var + EPS) * ln_scale + ln_bias
        return out

    def _L0_ffn_ref(x, Wr, br, W1, b1, W2, b2):
        import jax, jax.numpy as jnp
        import numpy as np
        B, S, D, H, E = (4, 256, 128, 256, 8)
        d = x.shape[-1]
        tokens = x.reshape(-1, d)
        logits = tokens @ Wr + br
        probs = jax.nn.softmax(logits, axis=-1)
        expert = jnp.argmax(probs, axis=-1)
        max_prob = jnp.take_along_axis(probs, expert[:, None], axis=-1)
        h = jax.nn.relu(jnp.einsum('td,edh->teh', tokens, W1) + b1[None])
        y = jnp.einsum('teh,ehd->ted', h, W2) + b2[None]
        out = jnp.take_along_axis(y, expert[:, None, None], axis=1)[:, 0, :]
        return (out * max_prob).reshape(x.shape)

    def _L1_attn_ref(x, c, Wq, bq, Wk, bk, Wv, bv, Wo, bo, rel_table):
        import jax, jax.numpy as jnp
        import numpy as np
        D_MODEL = 128
        N_HEADS = 16
        SEQ = 64
        B, S, D = x.shape
        H = N_HEADS
        dk = D // H
        scale = 1.0 / np.sqrt(dk)
        q = (x @ Wq + bq).reshape(B, S, H, dk)
        k = (x @ Wk + bk).reshape(B, S, H, dk)
        v = (x @ Wv + bv).reshape(B, S, H, dk)
        scores = jnp.einsum('bihd,bjhd->bhij', q, k) * scale
        rel_index = jnp.arange(S)[:, None] + jnp.arange(S - 1, -1, -1)[None, :]
        bias = rel_table[rel_index]
        scores = scores + jnp.transpose(bias, (2, 0, 1))[None]
        probs = jax.nn.softmax(scores, axis=-1)
        out = jnp.einsum('bhij,bjhd->bihd', probs, v).reshape(B, S, D)
        return out @ Wo + bo

    def _L1_xattn_ref(embeds, patch_embeds, patch_lens, W_in, b_in, g_res, g_init):
        import jax, jax.numpy as jnp
        import numpy as np
        B, L, P = (4, 512, 128)
        D_MODEL = 128
        D_GLOBAL = 256
        HEADDIM = 32
        EPSILON = 0.001
        RMS_EPS = 1e-05

        def rmsnorm(x, g, eps=RMS_EPS):
            var = jnp.mean(jnp.square(x), axis=-1, keepdims=True)
            return x * jax.lax.rsqrt(var + eps) * g

        def _hnet_depool(h, h_patch_full, patch_lens):
            h_patch = h_patch_full[..., :D_MODEL]
            bsz, plen = (h_patch.shape[0], h_patch.shape[1])
            seqlen = h.shape[1]
            logp = jnp.full((bsz, plen), -EPSILON, dtype=jnp.float32)
            bidx = jnp.cumsum(patch_lens, axis=1) - 1
            boundary_mask = jnp.zeros((bsz, seqlen), dtype=jnp.int32)
            boundary_mask = boundary_mask.at[jnp.arange(bsz)[:, None], bidx].set(1)
            dt = (-jnp.log(-jnp.expm1(logp))).astype(h_patch.dtype)
            x = h_patch / dt[..., None]
            n_heads = D_MODEL // HEADDIM
            A = -jnp.ones((n_heads,), dtype=jnp.float32)
            bcoef = jnp.exp(logp).astype(h_patch.dtype)
            x4 = x.reshape(bsz, plen, n_heads, HEADDIM)
            a = jnp.exp(dt[:, :, None] * A[None, None, :])
            u = (dt * bcoef)[:, :, None, None] * x4
            a_b = jnp.broadcast_to(a[..., None], u.shape)

            def comb(lft, rgt):
                aL, uL = lft
                aR, uR = rgt
                return (aL * aR, uL * aR + uR)
            _, s = jax.lax.associative_scan(comb, (a_b, u), axis=1)
            depool = s.reshape(bsz, plen, D_MODEL)
            plug = jnp.clip(jnp.cumsum(boundary_mask, axis=1) - 1, 0, plen - 1)
            depool_out = depool[jnp.arange(bsz)[:, None], plug]
            return depool_out + h
        h = rmsnorm(embeds, g_res)
        h = jnp.einsum('bld,ed->ble', h, W_in) + b_in
        h_patch = rmsnorm(patch_embeds, g_init)
        return _hnet_depool(h, h_patch, patch_lens)

    def _L1_ffn_ref(x, w_q, bn_gamma, bn_beta, keys, down_embed, up_embed):
        import jax, jax.numpy as jnp
        import numpy as np
        H = 8
        KD = 128
        TOPK = 8
        NUM_KEYS = 32
        N_EXPERTS = NUM_KEYS * NUM_KEYS
        N_DIM = 128
        BN_EPS = 1e-05

        def gelu_new(x):
            c = jnp.sqrt(jnp.asarray(2.0 / jnp.pi, x.dtype))
            return 0.5 * x * (1.0 + jnp.tanh(c * (x + 0.044715 * x * x * x)))
        b, n, d = x.shape
        q = jnp.einsum('bnd,de->bne', x, w_q)
        mean = jnp.mean(q, axis=(0, 1))
        var = jnp.var(q, axis=(0, 1))
        q = (q - mean) * jax.lax.rsqrt(var + BN_EPS) * bn_gamma + bn_beta
        q = q.reshape(b, n, 2, H, KD).transpose(2, 0, 1, 3, 4)
        sim = jnp.einsum('pbnhd,hkpd->pbnhk', q, keys)
        sx, ix = jax.lax.top_k(sim[0], TOPK)
        sy, iy = jax.lax.top_k(sim[1], TOPK)
        all_scores = (sx[..., :, None] + sy[..., None, :]).reshape(b, n, H, TOPK * TOPK)
        all_indices = (ix[..., :, None] * NUM_KEYS + iy[..., None, :]).reshape(b, n, H, TOPK * TOPK)
        scores, pk = jax.lax.top_k(all_scores, TOPK)
        indices = jnp.take_along_axis(all_indices, pk, axis=-1)
        wd = down_embed[indices]
        wu = up_embed[indices]
        h = jnp.einsum('bnd,bnhkd->bnhk', x, wd)
        h = gelu_new(h)
        h = jax.nn.softmax(scores, axis=-1) * h
        out = jnp.einsum('bnhk,bnhkd->bnd', h, wu)
        return out
    x = _layernorm(x + _L0_attn_ref(x, L0_attn_W_qkv, L0_attn_b_qkv, L0_attn_W_proj, L0_attn_b_proj), axis=-1)
    x = _layernorm(x + _L0_xattn_ref(x, ctx_2048, L0_xattn_Wq, L0_xattn_Wkv, L0_xattn_null_kv, L0_xattn_Wout, L0_xattn_ln_scale, L0_xattn_ln_bias), axis=-1)
    x = _layernorm(x + _L0_ffn_ref(x, L0_ffn_Wr, L0_ffn_br, L0_ffn_W1, L0_ffn_b1, L0_ffn_W2, L0_ffn_b2), axis=-1)
    x = _layernorm(x + _L1_attn_ref(x, L1_attn_c, L1_attn_Wq, L1_attn_bq, L1_attn_Wk, L1_attn_bk, L1_attn_Wv, L1_attn_bv, L1_attn_Wo, L1_attn_bo, L1_attn_rel_table), axis=-1)
    x = _layernorm(x + _L1_xattn_ref(x, ctx_2048, mask_BxS2_if0, L1_xattn_W_in, L1_xattn_b_in, L1_xattn_g_res, L1_xattn_g_init), axis=-1)
    x = _layernorm(x + _L1_ffn_ref(x, L1_ffn_w_q, L1_ffn_bn_gamma, L1_ffn_bn_beta, L1_ffn_keys, L1_ffn_down_embed, L1_ffn_up_embed), axis=-1)
    return x

_drawn_inputs = setup_inputs


def setup_inputs(seed=0):
    import zlib

    import numpy as np

    out = dict(_drawn_inputs(seed))
    spreads = {'L0_attn_b_qkv': (0.0, 0.1),
     'L0_attn_b_proj': (0.0, 0.1),
     'L0_xattn_ln_scale': (1.0, 0.2),
     'L0_xattn_ln_bias': (0.0, 0.1),
     'L0_ffn_br': (0.0, 0.693),
     'L0_ffn_b1': (0.0, 0.8),
     'L0_ffn_b2': (0.0, 0.669),
     'L1_attn_bq': (0.0, 0.8),
     'L1_attn_bk': (0.0, 2.0),
     'L1_attn_bv': (0.0, 0.1),
     'L1_attn_bo': (0.0, 0.1),
     'L1_xattn_b_in': (0.0, 0.1),
     'L1_xattn_g_res': (1.0, 0.2),
     'L1_xattn_g_init': (1.0, 0.2),
     'L1_ffn_bn_gamma': (1.0, 0.6),
     'L1_ffn_bn_beta': (0.0, 0.8)}
    factors = {'L0_xattn_null_kv': 4.536,
     'L0_ffn_Wr': 4.758,
     'L0_ffn_W1': 8.0,
     'L0_ffn_W2': 7.998,
     'L1_attn_rel_table': 29.378,
     'L1_ffn_w_q': 8.0,
     'L1_ffn_keys': 8.0,
     'L1_ffn_down_embed': 8.0,
     'L1_ffn_up_embed': 8.0}
    for name, (base, spread) in spreads.items():
        noise = np.random.default_rng([zlib.crc32(name.encode()), seed]).standard_normal(out[name].shape)
        drawn = base * np.exp(spread * noise) if base else spread * noise
        out[name] = jnp.asarray(drawn.astype(out[name].dtype))
    for name, factor in factors.items():
        out[name] = (out[name] * factor).astype(out[name].dtype)
    return out
```

```python
from contextlib import ExitStack

import numpy as np

import concourse.bass as bass
from concourse import mybir

ALU = mybir.AluOpType
ACT = mybir.ActivationFunctionType
AX = mybir.AxisListType
F32 = mybir.dt.float32
BF16 = mybir.dt.bfloat16
I32 = mybir.dt.int32
U32 = mybir.dt.uint32

B, T, D = 16, 128, 128
SLOTS = 2
ROUNDS = B // SLOTS
HEADS, DH = 16, 8
XH, XDH = 16, 64
XC = XH * XDH // 128
M, CTX = 77, 256
MK = M + 1
E, HID = 8, 256
HC = HID // 128
PH, KD, NK = 8, 128, 32
TOP = 8
NE = NK * NK
LN_EPS = 1e-5
XLN_EPS = 1e-6
RMS_EPS = 1e-5
BN_EPS = 1e-5
MASKED = -1e30
LOGP = -0.001
DT = float(-np.log(-np.expm1(np.float32(LOGP))))
BCOEF = float(np.exp(np.float32(LOGP)))

VECTOR_LINKS = 84
FINAL_LINKS = 34
R_B1, R_GAMMA, R_BETA = 0, 16, 32
R_BQK0, R_BQK1, R_GRES, R_NULLK = 48, 50, 52, 53
NROWS = 54

RSTDS = 8


def bcast(ap, shape):
    return ap.broadcast_to(shape)


def build(nc, a, out):
    with ExitStack() as ctx:
        def sb(name, shape, dt=F32, where=ctx):
            return where.enter_context(nc.sbuf_tensor(name, shape, dt))

        def sem(name):
            return ctx.enter_context(nc.semaphore(name))

        ps = ctx.enter_context(nc.psum_tensor("ps", [128, 8, 512], F32))

        ident = sb("ident", [128, 128])
        neg_half = sb("neg_half", [128, 16])
        ones_col = sb("ones_col", [128, 128])
        cols = sb("cols", [128, NROWS])
        spare = sb("spare", [1, 1])
        x5 = sb("x5", [128, B, 128])
        x5T = sb("x5T", [128, B, 128])
        cov = sb("cov", [128, 129])
        pk_wq = sb("pk_wq", [128, 2 * PH, KD])
        pk_keys = sb("pk_keys", [128, 2, 2 * KD])
        pk_down = sb("pk_down", [128, NE // 128, 128])
        pk_up = sb("pk_up", [128, NE // 128, 128])

        loop1 = ctx.enter_context(ExitStack())

        def sb1(name, shape, dt=F32):
            return sb(name, shape, dt, loop1)

        ident16 = sb1("ident16", [128, 128], BF16)
        causal16 = sb1("causal16", [128, 4, 128], BF16)
        head_mask = sb1("head_mask", [128, HEADS])
        iota8 = sb1("iota8", [128, E])
        iota_col = sb1("iota_col", [128, 1])

        w_qkv = [sb1(f"w_qkv{l}", [128, 3, 128]) for l in range(2)]
        w_proj = [sb1(f"w_proj{l}", [128, 128]) for l in range(2)]
        b_v = [sb1(f"b_v{l}", [128, 128]) for l in range(2)]
        b_proj = [sb1(f"b_proj{l}", [128, 128]) for l in range(2)]
        rel_bias = sb1("rel_bias", [128, HEADS, 128])
        xw_q = sb1("xw_q", [128, XC * 128])
        xw_kv = sb1("xw_kv", [128, 2, 2 * XC * 128])
        xw_out = sb1("xw_out", [128, XC, 128])
        x_scale = sb1("x_scale", [128, 128])
        x_bias = sb1("x_bias", [128, 128])
        w_r = sb1("w_r", [128, E])
        b_r = sb1("b_r", [128, E])
        w_1 = sb1("w_1", [128, E, HID])
        w_2 = sb1("w_2", [128, E, HC, 128])
        b_2 = sb1("b_2", [E, 128])
        w_inT = sb1("w_inT", [128, 128])
        b_in = sb1("b_in", [128, 128])
        g_init = sb1("g_init", [128, 128])
        plug_T = sb1("plug_T", [M, B, 128])


        rel_dram = nc.dram_tensor("rel_scratch", [HEADS, 256], F32, kind="Internal").ap()
        plug_dram = nc.dram_tensor("plug_scratch", [B, 128], F32, kind="Internal").ap()

        s_w0 = sem("first_attention_weights_loaded")
        s_wx = sem("cross_attention_weights_loaded")
        s_we = sem("expert_weights_loaded")
        s_w1 = sem("second_attention_weights_loaded")
        s_wp = sem("patch_weights_loaded")
        s_rows = sem("rows_loaded")
        s_pk = sem("product_key_weights_loaded")
        s_rel = sem("relative_table_loaded")
        s_rel_ext = sem("relative_table_extended")
        s_rel_out = sem("relative_table_stored")
        s_rel_in = sem("relative_bias_loaded")
        s_rel_fl = sem("relative_bias_flipped")
        s_plen = sem("patch_lengths_loaded")
        s_plug = sem("plug_ready")
        s_plug_out = sem("plug_stored")
        s_plug_in = sem("plug_spread")
        s_const = sem("pool_constants_ready")
        s_zero = sem("vector_constants_ready")
        s_setup = sem("vector_setup_chain")
        s_pchain = sem("pool_chain")
        s_rowsT = sem("rows_turned")
        s_cols = sem("columns_ready")
        s_winT = sem("w_in_turned")
        s_setup_done = sem("vector_setup_done")
        s_ev = sem("plug_exp_ready")
        s_nullv = sem("null_value_loaded")
        s_vz = sem("value_zeros_ready")

        def pair(name, shape, dt=F32):
            return [sb(f"{name}{p}", shape, dt, loop1) for p in range(SLOTS)]

        x_in = pair("x_in", [128, 128])
        c_in = pair("c_in", [M, CTX])
        wide_a = pair("wide_a", [128, 2048])
        wide_p = pair("wide_p", [128, 2048])
        wide_t = pair("wide_t", [128, 2048])
        v_exp = pair("v_exp", [128, HEADS, 128])
        v_z = pair("v_z", [MK, XH, 128])
        k_exp = pair("k_exp", [128, XC, 2, MK])
        c_T = pair("c_T", [128, 2, M])
        x_T = pair("x_T", [128, 128])
        k_T = pair("k_T", [128, 128])
        att_T = pair("att_T", [128, 128])
        mx = pair("mx", [128, 16])
        sums = pair("sums", [128, 16])
        rsum = pair("rsum", [128, 16])
        z = pair("z", [128, 128])
        z2 = pair("z2", [128, 128])
        x_1 = pair("x_1", [128, 128])
        x_2 = pair("x_2", [128, 128])
        x_3 = pair("x_3", [128, 128])
        x_5 = pair("x_5", [128, 129])
        logit = pair("logit", [128, E])
        logit_e = pair("logit_e", [128, E])
        top8 = pair("top8", [128, 8])
        top8i = pair("top8i", [128, 8], U32)
        sm = pair("sm", [128, 8])
        w_one = pair("w_one", [128, E])
        w_oneT = pair("w_oneT", [E, 128])
        stats = sb("stats", [128, SLOTS * RSTDS, 6], F32, loop1)
        mv = sb("mv", [128, SLOTS * RSTDS, 2], F32, loop1)
        veps = sb("veps", [128, SLOTS * RSTDS], F32, loop1)
        rstd = sb("rstd", [128, SLOTS * RSTDS], F32, loop1)

        r_z = [wide_a[p][0:64, 0:256].rearrange("d (g q) -> d g q", g=2) for p in range(SLOTS)]
        x_4 = x_1
        patch = [att_T[p][0:M, :] for p in range(SLOTS)]
        plug_now = [k_T[p][0:M, :] for p in range(SLOTS)]
        c_sq = [wide_t[p][0:M, 0:CTX] for p in range(SLOTS)]
        plen_i = wide_t[0][0:B, 1152:1152 + M].bitcast(I32)
        flip = wide_t[1][:, 128:256]
        w_in = wide_t[1][:, 256:384]
        rows = wide_t[1][0:NROWS, 384:512]

        s_x = [sem(f"x{p}_loaded") for p in range(SLOTS)]
        s_c = [sem(f"context{p}_loaded") for p in range(SLOTS)]
        s_x_used = sem("x_used")
        s_c_used = sem("context_used")
        s_slot = sem("slot_free")
        A = [{n: sem(f"attention{l}_{n}") for n in (
            "x_turned", "xT_ready", "qkv_ready", "masked_q_ready", "v_ready", "scores_ready",
            "shifted", "probs_ready", "probs_turned", "probsT_ready", "mixed", "mixed_ready",
            "projected")} for l in range(2)]
        X = {n: sem(f"cross_{n}") for n in (
            "x_turned", "xT_ready", "q_ready", "q_copied", "c_turned", "cT_ready", "k_ready", "k_copied",
            "v_ready", "v_copied", "scores_ready", "shifted", "probs_ready", "normalized",
            "probs_turned", "probsT_ready", "mixed", "mixed_copied", "projected")}
        F = {n: sem(f"experts_{n}") for n in (
            "x_turned", "xT_ready", "logits_ready", "max_ready", "exp_ready", "gate_ready",
            "gate_turned", "gateT_ready", "hidden_ready", "biased", "relu_ready", "outputs_ready",
            "weighted")}
        G = {n: sem(f"patch_{n}") for n in (
            "x_turned", "xT_ready", "squares_ready", "rows_ready", "products_ready")}
        s_x1 = sem("x1_ready")
        s_x2 = sem("x2_ready")
        s_x3 = sem("x3_ready")
        s_x4 = sem("x4_ready")
        s_x5 = sem("x5_ready")
        s_x5T = sem("x5_turned")
        s_x5T_ready = sem("x5T_stored")
        s_var = sem("variance_ready")
        s_rstd = sem("rstd_ready")
        s_chain = sem("vector_chain")
        s_cov = sem("covariance_summed")

        def v_blocks(p):
            base = v_exp[p][:]
            return bass.AP(tensor=base.tensor, offset=base.offset,
                           ap=[base.ap[0], [8 * 128, 2], [128 + DH, 8], [1, DH]])

        bank = lambda p, k: ps[:, 4 * p + k, :]
        banks = lambda p: ps[:, 4 * p:4 * p + 4, :]

        def weights_dma(q, names):
            for dst, src, s in names:
                q.dma_start(dst, src).then_inc(s, 16)

        def pbc(ap1d, n=128):
            return ap1d.partition_broadcast(n)

        row_sources = [
            (R_B1, 16, a["L0_ffn_b1"].rearrange("e (j h) -> (e j) h", h=128)),
            (R_GAMMA, 16, a["L1_ffn_bn_gamma"].rearrange("(r d) -> r d", d=128)),
            (R_BETA, 16, a["L1_ffn_bn_beta"].rearrange("(r d) -> r d", d=128)),
            (R_BQK0, 2, a["L0_attn_b_qkv"].rearrange("(r d) -> r d", d=128)[0:2]),
            (R_BQK1, 1, a["L1_attn_bq"].unsqueeze(0)),
            (R_BQK1 + 1, 1, a["L1_attn_bk"].unsqueeze(0)),
            (R_GRES, 1, a["L1_xattn_g_res"].unsqueeze(0)),
        ]
        N_ROWS_DMA = len(row_sources) + 2

        first = ctx.enter_context(ExitStack())
        block = first.enter_context(nc.Block())

        @block.sync
        def _(sp):
            for p in range(SLOTS):
                sp.dma_start(x_in[p][:], a["x"][p]).then_inc(s_x[p], 16)
                sp.dma_start(c_in[p][:], a["ctx_2048"][p]).then_inc(s_c[p], 16)
            weights_dma(sp, [
                (w_qkv[0][:], a["L0_attn_W_qkv"].rearrange("k (t n) -> k t n", t=3), s_w0),
                (w_proj[0][:], a["L0_attn_W_proj"], s_w0),
                (b_v[0][:], pbc(a["L0_attn_b_qkv"][2 * D:3 * D]), s_w0),
                (b_proj[0][:], pbc(a["L0_attn_b_proj"]), s_w0),
            ])
            for r, n, src in row_sources:
                sp.dma_start(rows[r:r + n, :], src).then_inc(s_rows, 16)
            for j in range(2):
                sp.dma_start(rows[R_NULLK:R_NULLK + 1, 64 * j:64 * j + 64],
                             a["L0_xattn_null_kv"][0:1, :]).then_inc(s_rows, 16)
            weights_dma(sp, [
                (xw_q[:], a["L0_xattn_Wq"], s_wx),
                (xw_kv[:], a["L0_xattn_Wkv"].rearrange("(c k) n -> k c n", k=128), s_wx),
                (xw_out[:], a["L0_xattn_Wout"].rearrange("(c k) n -> k c n", k=128), s_wx),
                (x_scale[:], pbc(a["L0_xattn_ln_scale"]), s_wx),
                (x_bias[:], pbc(a["L0_xattn_ln_bias"]), s_wx),
            ])
            for p in range(SLOTS):
                sp.wait_ge(s_vz, p + 1)
                for hp in range(2):
                    sp.dma_start(
                        v_z[p][M:M + 1].rearrange("k (c g) d -> k c g d", g=2)[:, :, hp, 64 * hp:64 * hp + 64],
                        a["L0_xattn_null_kv"][1:2, :].unsqueeze(1).broadcast_to([1, XC, 64]),
                    ).then_inc(s_nullv, 16)
            sp.wait_ge(s_rel_ext, 1)
            sp.dma_start(rel_dram[:, 0:255], wide_p[0][0:HEADS, 0:255]).then_inc(s_rel_out, 16)
            sp.wait_ge(s_rel_out, 16)
            sp.dma_start(wide_p[1][:].rearrange("i (h j) -> i h j", h=HEADS),
                         bass.AP(tensor=rel_dram.tensor, offset=0, ap=[[1, 128], [256, HEADS], [1, 128]])
                         ).then_inc(s_rel_in, 16)
            sp.wait_ge(s_plug, 1)
            sp.dma_start(plug_dram, wide_t[0][0:B, 0:128]).then_inc(s_plug_out, 16)
            sp.wait_ge(s_plug_out, 16)
            sp.dma_start(plug_T[:], plug_dram.partition_broadcast(M)).then_inc(s_plug_in, 16)

            weights_dma(sp, [
                (pk_wq[:], a["L1_ffn_w_q"].rearrange("k (r d) -> k r d", d=KD), s_pk),
                (pk_keys[:], a["L1_ffn_keys"].rearrange("(t h) k p d -> (h k) t (p d)", t=2), s_pk),
                (pk_down[:], a["L1_ffn_down_embed"].rearrange("(c k) n -> k c n", k=128), s_pk),
                (pk_up[:], a["L1_ffn_up_embed"].rearrange("(c k) n -> k c n", k=128), s_pk),
            ])
            with sp.Fori(0, ROUNDS - 1) as i:
                for p in range(SLOTS):
                    u = SLOTS * i + p
                    sp.wait_ge(s_x_used, u + 1)
                    sp.dma_start(x_in[p][:], a["x"][bass.ds(u + SLOTS, 1)].rearrange("o t d -> t (o d)")
                                 ).then_inc(s_x[p], 16)
                for p in range(SLOTS):
                    u = SLOTS * i + p
                    sp.wait_ge(s_c_used, u + 1)
                    sp.dma_start(c_in[p][:], a["ctx_2048"][bass.ds(u + SLOTS, 1)].rearrange("o t d -> t (o d)")
                                 ).then_inc(s_c[p], 16)

        @block.gpsimd
        def _(pool):
            n = [0]

            def link(ins):
                n[0] += 1
                ins.then_inc(s_pchain, 1)
                pool.wait_ge(s_pchain, n[0])

            link(nc.gpsimd.memset(ident[:], 1.0))
            link(nc.gpsimd.affine_select(out=ident[:], in_=ident[:], compare_op=ALU.is_equal, fill=0.0,
                                         base=0, pattern=[[-1, 128]], channel_multiplier=1))
            link(nc.gpsimd.memset(flip[:], 1.0))
            link(nc.gpsimd.affine_select(out=flip[:], in_=flip[:], compare_op=ALU.is_equal, fill=0.0,
                                         base=-127, pattern=[[1, 128]], channel_multiplier=1))
            link(nc.gpsimd.tensor_copy(ident16[:], ident[:]))
            link(nc.gpsimd.memset(causal16[:], 0.0))
            link(nc.gpsimd.affine_select(out=causal16[:], in_=causal16[:], compare_op=ALU.is_ge, fill=MASKED,
                                         base=0, pattern=[[0, 4], [-1, 128]], channel_multiplier=1))
            link(nc.gpsimd.memset(head_mask[:], float(DH) ** -0.5))
            link(nc.gpsimd.affine_select(out=head_mask[:], in_=head_mask[:], compare_op=ALU.is_ge, fill=0.0,
                                         base=0, pattern=[[-DH, HEADS]], channel_multiplier=1))
            link(nc.gpsimd.affine_select(out=head_mask[:], in_=head_mask[:], compare_op=ALU.is_ge, fill=0.0,
                                         base=DH - 1, pattern=[[DH, HEADS]], channel_multiplier=-1))
            link(nc.gpsimd.iota(iota8[:], pattern=[[1, E]], base=0, channel_multiplier=0,
                                allow_small_or_imprecise_dtypes=True))
            link(nc.gpsimd.iota(iota_col[:], pattern=[[1, 1]], base=0, channel_multiplier=1,
                                allow_small_or_imprecise_dtypes=True))
            link(nc.gpsimd.memset(neg_half[:], -0.5))
            nc.gpsimd.memset(ones_col[:], 1.0).then_inc(s_const, 1)

            with pool.Fori(0, ROUNDS) as i:
                for k in range(SLOTS * RSTDS):
                    pool.wait_ge(s_var, SLOTS * RSTDS * i + k + 1)
                    nc.gpsimd.tensor_tensor(out=rstd[:, k:k + 1], in0=veps[:, k:k + 1],
                                            in1=neg_half[:, 0:1], op=ALU.pow).then_inc(s_rstd, 1)

        @block.tensor
        def _(pe):
            pe.wait_ge(s_const, 1)
            pe.wait_ge(s_rows, 16 * N_ROWS_DMA)
            nc.tensor.transpose(ps[:, 0, 0:NROWS], rows[:], ident[0:NROWS, 0:NROWS]).then_inc(s_rowsT, 1)
            pe.wait_ge(s_wp, 16 * 3)
            nc.tensor.transpose(ps[:, 1, 0:128], w_in[:], ident[:]).then_inc(s_winT, 1)
            pe.wait_ge(s_rel_in, 16)
            for c in range(4):
                mm = nc.tensor.matmul(ps[:, 4 + c, :], flip[:], wide_p[1][:, 512 * c:512 * c + 512],
                                      start=True, stop=True)
            mm.then_inc(s_rel_fl, 1)
            pe.wait_ge(s_w0, 16 * 4)
            pe.wait_ge(s_wx, 16 * 5)
            pe.wait_ge(s_we, 16 * 5)
            pe.wait_ge(s_w1, 16 * 6)
            pe.wait_ge(s_setup_done, 1)
            pe.wait_ge(s_nullv, 64)

            def attention(l, i, x_ready, xt):
                S = A[l]
                for p in range(SLOTS):
                    u1 = SLOTS * i + p + 1
                    if l == 0:
                        pe.wait_ge(s_slot, u1)
                        pe.wait_ge(s_x[p], 16 * i + 16)
                    else:
                        pe.wait_ge(x_ready, u1)
                    nc.tensor.transpose(bank(p, 0)[:, 0:128], xt[p][:], ident[:]).then_inc(S["x_turned"], 1)
                for p in range(SLOTS):
                    u1 = SLOTS * i + p + 1
                    pe.wait_ge(S["xT_ready"], u1)
                    nc.tensor.matmul(bank(p, 0)[:, 0:128], w_qkv[l][:, 0, :], x_T[p][:], start=True, stop=True)
                    nc.tensor.matmul(bank(p, 0)[:, 128:256], w_qkv[l][:, 1, :], x_T[p][:], start=True, stop=True)
                    nc.tensor.matmul(bank(p, 0)[:, 256:384], x_T[p][:], w_qkv[l][:, 2, :], start=True,
                                     stop=True).then_inc(S["qkv_ready"], 1)
                for p in range(SLOTS):
                    u1 = SLOTS * i + p + 1
                    pe.wait_ge(S["masked_q_ready"], u1)
                    q = wide_a[p][:].rearrange("d (h t) -> d h t", h=HEADS)
                    for c in range(4):
                        if l == 0:
                            nc.tensor.matmul(bank(p, c), ident16[:], causal16[:].rearrange("k h j -> k (h j)"),
                                             start=True, stop=False, skip_group_check=True)
                        for k in range(4):
                            mm = nc.tensor.matmul(bank(p, c)[:, 128 * k:128 * k + 128], q[:, 4 * c + k, :], k_T[p][:],
                                                  start=(l == 1), stop=True, skip_group_check=True)
                    mm.then_inc(S["scores_ready"], 1)
                for p in range(SLOTS):
                    u1 = SLOTS * i + p + 1
                    pe.wait_ge(S["probs_ready"], u1)
                    pr = wide_p[p][:].rearrange("q (h k) -> q h k", h=HEADS)
                    for h in range(HEADS):
                        mm = nc.tensor.transpose(bank(p, h // 4)[:, 128 * (h % 4):128 * (h % 4) + 128],
                                                 pr[:, h, :], ident[:])
                    mm.then_inc(S["probs_turned"], 1)
                for p in range(SLOTS):
                    u1 = SLOTS * i + p + 1
                    pe.wait_ge(S["probsT_ready"], u1)
                    pe.wait_ge(S["v_ready"], u1)
                    pt = wide_t[p][:].rearrange("k (h q) -> k h q", h=HEADS)
                    for h in range(HEADS):
                        mm = nc.tensor.matmul(bank(p, 0)[:, 128 * (h // 8):128 * (h // 8) + 128], v_exp[p][:, h, :],
                                              pt[:, h, :], start=(h % 8 == 0), stop=(h % 8 == 7),
                                              skip_group_check=True)
                    mm.then_inc(S["mixed"], 1)
                for p in range(SLOTS):
                    u1 = SLOTS * i + p + 1
                    pe.wait_ge(S["mixed_ready"], u1)
                    nc.tensor.matmul(bank(p, 0)[:, 0:128], att_T[p][:], w_proj[l][:], start=True,
                                     stop=True).then_inc(S["projected"], 1)

            def cross(i):
                for p in range(SLOTS):
                    u1 = SLOTS * i + p + 1
                    pe.wait_ge(s_x1, u1)
                    nc.tensor.transpose(bank(p, 0)[:, 0:128], x_1[p][:], ident[:]).then_inc(X["x_turned"], 1)
                    pe.wait_ge(s_c[p], 16 * i + 16)
                    for c in range(2):
                        mm = nc.tensor.transpose(bank(p, 3)[:, 128 * c:128 * c + M], c_in[p][:, 128 * c:128 * c + 128],
                                                 ident[0:M, 0:M])
                    mm.then_inc(X["c_turned"], 1)
                for p in range(SLOTS):
                    u1 = SLOTS * i + p + 1
                    pe.wait_ge(X["xT_ready"], u1)
                    for c in range(XC):
                        mm = nc.tensor.matmul(bank(p, c // 4)[:, 128 * (c % 4):128 * (c % 4) + 128],
                                              xw_q[:, 128 * c:128 * c + 128], x_T[p][:], start=True, stop=True)
                    mm.then_inc(X["q_ready"], 1)
                    pe.wait_ge(X["cT_ready"], u1)
                    for c in range(XC):
                        for k in range(2):
                            mm = nc.tensor.matmul(bank(p, 2 + c // 4)[:, 128 * (c % 4):128 * (c % 4) + M],
                                                  xw_kv[:, k, 128 * c:128 * c + 128], c_T[p][:, k, :],
                                                  start=(k == 0), stop=(k == 1))
                    mm.then_inc(X["k_ready"], 1)
                for p in range(SLOTS):
                    u1 = SLOTS * i + p + 1
                    pe.wait_ge(X["q_copied"], u1)
                    for n in range(2):
                        for k in range(2):
                            mm = nc.tensor.matmul(bank(p, n)[0:M, :], c_T[p][:, k, :],
                                                  xw_kv[:, k, 1024 + 512 * n:1536 + 512 * n],
                                                  start=(k == 0), stop=(k == 1))
                    mm.then_inc(X["v_ready"], 1)
                for p in range(SLOTS):
                    u1 = SLOTS * i + p + 1
                    pe.wait_ge(X["k_copied"], u1)
                    pe.wait_ge(X["v_copied"], u1)
                    for c in range(XC):
                        mm = nc.tensor.matmul(bank(p, c // 2)[:, 2 * MK * (c % 2):2 * MK * (c % 2 + 1)],
                                              wide_a[p][:, 128 * c:128 * c + 128],
                                              k_exp[p][:, c].rearrange("d g k -> d (g k)"), start=True, stop=True)
                    mm.then_inc(X["scores_ready"], 1)
                for p in range(SLOTS):
                    u1 = SLOTS * i + p + 1
                    pe.wait_ge(X["normalized"], u1)
                    pr = wide_p[p][:, 0:XH * MK].rearrange("q (h k) -> q h k", h=XH)
                    for h in range(XH):
                        mm = nc.tensor.transpose(bank(p, h // 4)[0:MK, 128 * (h % 4):128 * (h % 4) + 128],
                                                 pr[:, h, :], ident[:])
                    mm.then_inc(X["probs_turned"], 1)
                for p in range(SLOTS):
                    u1 = SLOTS * i + p + 1
                    pe.wait_ge(X["probsT_ready"], u1)
                    pt = wide_t[p][:].rearrange("k (h q) -> k h q", h=XH)
                    for c in range(XC):
                        for g in range(2):
                            mm = nc.tensor.matmul(bank(p, c // 4)[:, 128 * (c % 4):128 * (c % 4) + 128],
                                                  v_z[p][:, 2 * c + g, :], pt[0:MK, 2 * c + g, :],
                                                  start=(g == 0), stop=(g == 1))
                    mm.then_inc(X["mixed"], 1)
                for p in range(SLOTS):
                    u1 = SLOTS * i + p + 1
                    pe.wait_ge(X["mixed_copied"], u1)
                    for c in range(XC):
                        mm = nc.tensor.matmul(bank(p, 2)[:, 0:128], wide_a[p][:, 128 * c:128 * c + 128],
                                              xw_out[:, c, :], start=(c == 0), stop=(c == XC - 1))
                    mm.then_inc(X["projected"], 1)

            def experts(i):
                for p in range(SLOTS):
                    u1 = SLOTS * i + p + 1
                    pe.wait_ge(s_x2, u1)
                    nc.tensor.transpose(bank(p, 0)[:, 0:128], x_2[p][:], ident[:]).then_inc(F["x_turned"], 1)
                for p in range(SLOTS):
                    u1 = SLOTS * i + p + 1
                    pe.wait_ge(F["xT_ready"], u1)
                    nc.tensor.matmul(bank(p, 0)[:, 0:E], x_T[p][:], w_r[:], start=True,
                                     stop=True).then_inc(F["logits_ready"], 1)
                for p in range(SLOTS):
                    u1 = SLOTS * i + p + 1
                    pe.wait_ge(F["max_ready"], u1)
                    for e in range(E):
                        for j in range(HC):
                            k = HC * e + j
                            mm = nc.tensor.matmul(bank(p, k // 4)[:, 128 * (k % 4):128 * (k % 4) + 128],
                                                  w_1[:, e, 128 * j:128 * j + 128], x_T[p][:], start=True, stop=True)
                    mm.then_inc(F["hidden_ready"], 1)
                for p in range(SLOTS):
                    u1 = SLOTS * i + p + 1
                    pe.wait_ge(F["relu_ready"], u1)
                    for e in range(E):
                        for j in range(HC):
                            mm = nc.tensor.matmul(bank(p, e // 4)[:, 128 * (e % 4):128 * (e % 4) + 128],
                                                  wide_a[p][:, 128 * (HC * e + j):128 * (HC * e + j) + 128],
                                                  w_2[:, e, j, :], start=(j == 0), stop=(j == HC - 1))
                    mm.then_inc(F["outputs_ready"], 1)
                    pe.wait_ge(F["gate_ready"], u1)
                    nc.tensor.transpose(bank(p, 2)[0:E, 0:128], w_one[p][:], ident[:]).then_inc(F["gate_turned"], 1)
                for p in range(SLOTS):
                    u1 = SLOTS * i + p + 1
                    pe.wait_ge(F["gateT_ready"], u1)
                    nc.tensor.matmul(bank(p, 3)[:, 0:128], w_oneT[p][:], b_2[:], start=True,
                                     stop=True).then_inc(F["weighted"], 1)

            def patches(i):
                for p in range(SLOTS):
                    u1 = SLOTS * i + p + 1
                    pe.wait_ge(s_x4, u1)
                    nc.tensor.transpose(bank(p, 0)[:, 0:128], x_4[p][:], ident[:]).then_inc(G["x_turned"], 1)
                for p in range(SLOTS):
                    u1 = SLOTS * i + p + 1
                    pe.wait_ge(G["xT_ready"], u1)
                    nc.tensor.matmul(bank(p, 1)[:, 0:128], x_T[p][:], w_inT[:], start=True, stop=True)
                    pe.wait_ge(G["rows_ready"], u1)
                    nc.tensor.matmul(bank(p, 2)[:, 0:128], plug_now[p][:], patch[p][:], start=True,
                                     stop=True).then_inc(G["products_ready"], 1)
                for p in range(SLOTS):
                    u1 = SLOTS * i + p + 1
                    pe.wait_ge(s_x5, u1)
                    nc.tensor.transpose(bank(p, 0)[:, 0:128], x_5[p][:, 0:128], ident[:])
                    nc.tensor.matmul(bank(p, 3)[:, 0:129], x_5[p][:, 0:128], x_5[p][:], start=True,
                                     stop=True).then_inc(s_x5T, 1)

            with pe.Fori(0, ROUNDS) as i:
                attention(0, i, None, x_in)
                cross(i)
                experts(i)
                attention(1, i, s_x3, x_3)
                patches(i)

        @block.scalar
        def _(act):
            weights_dma(act, [
                (w_in[:], a["L1_xattn_W_in"], s_wp),
                (b_in[:], pbc(a["L1_xattn_b_in"]), s_wp),
                (g_init[:], pbc(a["L1_xattn_g_init"][0:128]), s_wp),
                (w_r[:], a["L0_ffn_Wr"], s_we),
                (b_r[:], pbc(a["L0_ffn_br"]), s_we),
                (w_1[:], a["L0_ffn_W1"].rearrange("e k n -> k e n"), s_we),
                (w_2[:], a["L0_ffn_W2"].rearrange("e (j k) n -> k e j n", k=128), s_we),
                (b_2[:], a["L0_ffn_b2"], s_we),
                (w_qkv[1][:, 0, :], a["L1_attn_Wq"], s_w1),
                (w_qkv[1][:, 1, :], a["L1_attn_Wk"], s_w1),
                (w_qkv[1][:, 2, :], a["L1_attn_Wv"], s_w1),
                (w_proj[1][:], a["L1_attn_Wo"], s_w1),
                (b_v[1][:], pbc(a["L1_attn_bv"]), s_w1),
                (b_proj[1][:], pbc(a["L1_attn_bo"]), s_w1),
                (wide_p[0][0:HEADS, 128:255], a["rel_rev"], s_rel),
                (plen_i, a["mask_BxS2_if0"], s_plen),
            ])
            act.wait_ge(s_ev, 1)
            nc.scalar.activation(plug_T[:], plug_T[:], ACT.Exp, scale=-DT).then_inc(s_ev, 1)

            def copy_all(i, ready, done, dst, src):
                for p in range(SLOTS):
                    act.wait_ge(ready, SLOTS * i + p + 1)
                    nc.scalar.copy(dst(p), src(p)).then_inc(done, 1)

            def attention(l, i):
                S = A[l]
                copy_all(i, S["x_turned"], S["xT_ready"], lambda p: x_T[p][:], lambda p: bank(p, 0)[:, 0:128])
                for p in range(SLOTS):
                    act.wait_ge(S["shifted"], SLOTS * i + p + 1)
                    nc.scalar.activation(wide_p[p][:], wide_p[p][:], ACT.Exp).then_inc(S["probs_ready"], 1)
                copy_all(i, S["probs_turned"], S["probsT_ready"],
                         lambda p: wide_t[p][:].rearrange("k (b n) -> k b n", b=4), lambda p: banks(p))

            with act.Fori(0, ROUNDS) as i:
                attention(0, i)
                for p in range(SLOTS):
                    u1 = SLOTS * i + p + 1
                    act.wait_ge(X["x_turned"], u1)
                    nc.scalar.copy(x_T[p][:], bank(p, 0)[:, 0:128]).then_inc(X["xT_ready"], 1)
                    act.wait_ge(X["c_turned"], u1)
                    nc.scalar.copy(c_T[p][:], bank(p, 3)[:, 0:256].rearrange("d (c k) -> d c k", c=2)[:, :, 0:M]
                                   ).then_inc(X["cT_ready"], 1)
                for p in range(SLOTS):
                    u1 = SLOTS * i + p + 1
                    act.wait_ge(X["q_ready"], u1)
                    nc.scalar.copy(wide_a[p][:, 0:1024].rearrange("d (b n) -> d b n", b=2),
                                   ps[:, 4 * p:4 * p + 2, :]).then_inc(X["q_copied"], 1)
                for p in range(SLOTS):
                    u1 = SLOTS * i + p + 1
                    act.wait_ge(X["v_ready"], u1)
                    for hp in range(2):
                        ins = nc.scalar.copy(
                            v_z[p][0:M].rearrange("k (c g) d -> k c g d", g=2)[:, :, hp, 64 * hp:64 * hp + 64],
                            ps[0:M, 4 * p:4 * p + 2, :].rearrange("k b (c g d) -> k (b c) g d", g=2, d=64)[:, :, hp, :])
                    ins.then_inc(X["v_copied"], 1)
                for p in range(SLOTS):
                    act.wait_ge(X["shifted"], SLOTS * i + p + 1)
                    nc.scalar.activation(wide_p[p][:, 0:XH * MK], wide_p[p][:, 0:XH * MK], ACT.Exp,
                                         scale=float(XDH) ** -0.5).then_inc(X["probs_ready"], 1)
                copy_all(i, X["probs_turned"], X["probsT_ready"],
                         lambda p: wide_t[p][0:MK, :].rearrange("k (b n) -> k b n", b=4),
                         lambda p: ps[0:MK, 4 * p:4 * p + 4, :])
                copy_all(i, X["mixed"], X["mixed_copied"],
                         lambda p: wide_a[p][:, 0:1024].rearrange("d (b n) -> d b n", b=2),
                         lambda p: ps[:, 4 * p:4 * p + 2, :])
                copy_all(i, F["x_turned"], F["xT_ready"], lambda p: x_T[p][:], lambda p: bank(p, 0)[:, 0:128])
                for p in range(SLOTS):
                    act.wait_ge(F["max_ready"], SLOTS * i + p + 1)
                    nc.scalar.activation(logit_e[p][:], logit[p][:], ACT.Exp, bias=sm[p][:, 0:1],
                                         accum_out=sm[p][:, 1:2]).then_inc(F["exp_ready"], 1)
                for p in range(SLOTS):
                    act.wait_ge(F["biased"], SLOTS * i + p + 1)
                    nc.scalar.activation(wide_a[p][:], wide_a[p][:], ACT.Relu).then_inc(F["relu_ready"], 1)
                copy_all(i, F["gate_turned"], F["gateT_ready"], lambda p: w_oneT[p][:],
                         lambda p: bank(p, 2)[0:E, 0:128])
                attention(1, i)
                copy_all(i, G["x_turned"], G["xT_ready"], lambda p: x_T[p][:], lambda p: bank(p, 0)[:, 0:128])
                for p in range(SLOTS):
                    u = SLOTS * i + p
                    act.wait_ge(s_x5T, u + 1)
                    nc.scalar.copy(x5T[:, bass.ds(u, 1), :], bank(p, 0)[:, 0:128].unsqueeze(1)
                                   ).then_inc(s_x5T_ready, 1)

        @block.vector
        def _(dve):
            V = nc.vector
            n = [0]

            def link(ins):
                n[0] += 1
                ins.then_inc(s_setup, 1)
                dve.wait_ge(s_setup, n[0])

            for p in range(SLOTS):
                V.memset(v_z[p][:], 0.0).then_inc(s_vz, 1)
                link(V.memset(k_exp[p][:], 0.0))
                link(V.memset(v_exp[p][:], 0.0))
                for h in range(HEADS):
                    ins = V.memset(v_exp[p][:, h, 64 + DH * (h % 8):64 + DH * (h % 8) + DH], 1.0)
                link(ins)
                link(V.memset(x_5[p][:], 1.0))
            link(V.memset(cov[:], 0.0))
            link(V.memset(veps[:], 1.0))
            dve.wait_ge(s_const, 1)
            dve.wait_ge(s_rel, 16)
            link(V.tensor_copy(wide_p[0][0:HEADS, 0:128],
                               bcast(wide_p[0][0:HEADS, 128:129], [HEADS, 128])))
            V.tensor_copy(wide_t[1][0:HEADS, 0:8], wide_p[0][0:HEADS, 0:8]).then_inc(s_rel_ext, 1)
            dve.wait_ge(s_plen, 16)
            plen = wide_t[0][0:B, 256:256 + M]
            edge = wide_t[0][0:B, 384:384 + M]
            wrap = wide_t[0][0:B, 512:512 + M]
            hit = wide_t[0][0:B, 640:768]
            zero = wide_t[0][0:B, 768:1024]
            tok = wide_t[0][0:B, 1024:1152]
            link(V.memset(zero, 0.0))
            link(V.tensor_copy(plen, plen_i))
            link(V.tensor_tensor_scan(edge, plen, zero[:, 0:M], 0.0, ALU.add, ALU.add))
            link(V.tensor_scalar(edge, edge, 1.0, None, ALU.subtract))
            link(V.tensor_scalar(wrap, edge, 0.0, float(T), ALU.is_lt, ALU.mult))
            link(V.tensor_tensor(edge, edge, wrap, ALU.add))
            link(V.memset(tok, 1.0))
            link(V.tensor_tensor_scan(hit, tok, zero[:, 0:128], -1.0, ALU.add, ALU.add))
            link(V.tensor_copy(tok, hit))
            CH = 16
            for c in range(T // CH):
                cmp = wide_a[0][0:B, 0:CH * M].rearrange("b (t k) -> b t k", t=CH)
                link(V.tensor_tensor(cmp, bcast(edge.unsqueeze(1), [B, CH, M]),
                                     bcast(tok[:, CH * c:CH * c + CH].unsqueeze(2), [B, CH, M]), ALU.is_equal))
                link(V.tensor_reduce(hit[:, CH * c:CH * c + CH], cmp, AX.X, ALU.max))
            link(V.tensor_tensor_scan(tok, hit, zero[:, 0:128], -1.0, ALU.add, ALU.add))
            V.tensor_scalar(wide_t[0][0:B, 0:128], tok, 0.0, float(M - 1), ALU.max, ALU.min).then_inc(s_plug, 1)
            dve.wait_ge(s_plug_in, 16)
            flat = plug_T[:]
            sign = wide_a[1][0:M, :].rearrange("k (b t) -> k b t", b=B)
            link(V.tensor_scalar(flat, flat, iota_col[0:M, 0:1], None, ALU.subtract))
            link(V.tensor_scalar(sign, flat, 0.0, None, ALU.is_ge))
            V.tensor_scalar(flat, flat, 0.0, None, ALU.max).then_inc(s_ev, 1)
            dve.wait_ge(s_ev, 2)
            link(V.tensor_tensor(flat, flat, sign, ALU.mult))
            dve.wait_ge(s_rowsT, 1)
            link(V.tensor_copy(cols[:], ps[:, 0, 0:NROWS]))
            dve.wait_ge(s_winT, 1)
            link(V.tensor_scalar(w_inT[:], ps[:, 1, 0:128], cols[:, R_GRES:R_GRES + 1], None, ALU.mult))
            for p in range(SLOTS):
                for hp in range(2):
                    r = slice(64 * hp, 64 * hp + 64)
                    link(V.tensor_copy(k_exp[p][r, :, hp, M:MK],
                                       bcast(cols[r, R_NULLK:R_NULLK + 1].unsqueeze(1), [64, XC, 1])))
            dve.wait_ge(s_rel_fl, 1)
            link(V.tensor_copy(rel_bias[:].rearrange("i (b h) j -> i b (h j)", b=4), ps[:, 4:8, :]))
            dve.wait_ge(s_w0, 16 * 4)
            dve.wait_ge(s_wx, 16 * 5)
            dve.wait_ge(s_we, 16 * 5)
            dve.wait_ge(s_w1, 16 * 6)
            dve.wait_ge(s_wp, 16 * 3)
            dve.wait_ge(s_nullv, 64)
            V.memset(z[0][:, 0:1], 0.0).then_inc(s_setup_done, 1)
            for p in range(SLOTS):
                V.memset(z2[p][:, 0:1], 0.0).then_inc(s_slot, 1)

            LINKS = VECTOR_LINKS
            state = {}

            def settle():
                V.memset(spare[:], 0.0)

            def chain(ins):
                state["links"] += 1
                ins.then_inc(s_chain, 1)
                dve.wait_ge(s_chain, LINKS * state["i"] + state["links"])

            def variance(eps):
                k = state["roots"]
                state["roots"] += 1
                return k

            def wait_rstd(k):
                dve.wait_ge(s_rstd, SLOTS * RSTDS * state["i"] + k + 1)

            def norm_begin(zp, eps):
                k = variance(eps)
                chain(V.bn_stats(stats[:, k, :], zp))
                settle()
                chain(V.bn_aggr(mv[:, k, :], stats[:, k, :]))
                V.tensor_scalar(veps[:, k:k + 1], mv[:, k, 1:2], eps, None, ALU.add).then_inc(s_var, 1)
                return k

            def norm_end(k, outp, zp):
                wait_rstd(k)
                return V.tensor_scalar(outp, zp, mv[:, k, 0:1], rstd[:, k:k + 1], ALU.subtract, ALU.mult)

            def attention(l, i, xs, done, outs):
                S = A[l]
                bq = R_BQK0 if l == 0 else R_BQK1
                for p in range(SLOTS):
                    u1 = SLOTS * i + p + 1
                    dve.wait_ge(S["qkv_ready"], u1)
                    V.tensor_scalar(k_T[p][:], bank(p, 0)[:, 128:256], cols[:, bq + 1:bq + 2], None, ALU.add)
                    V.tensor_tensor(
                        v_blocks(p),
                        bank(p, 0)[:, 256:384].rearrange("k (g h d) -> k g h d", g=2, h=8),
                        b_v[l][:].rearrange("k (g h d) -> k g h d", g=2, h=8), ALU.add).then_inc(S["v_ready"], 1)
                    V.scalar_tensor_tensor(
                        out=wide_a[p][:].rearrange("d (h t) -> d h t", h=HEADS),
                        in0=bcast(bank(p, 0)[:, 0:128].unsqueeze(1), [128, HEADS, 128]),
                        scalar=cols[:, bq:bq + 1],
                        in1=bcast(head_mask[:].unsqueeze(2), [128, HEADS, 128]),
                        op0=ALU.add, op1=ALU.mult).then_inc(S["masked_q_ready"], 1)
                for p in range(SLOTS):
                    u1 = SLOTS * i + p + 1
                    dve.wait_ge(S["scores_ready"], u1)
                    pr = wide_p[p][:].rearrange("q (b h k) -> q b h k", b=4, h=4)
                    sc = banks(p).rearrange("q b (h k) -> q b h k", h=4)
                    if l == 1:
                        chain(V.tensor_tensor(wide_p[p][:].rearrange("q (b n) -> q b n", b=4), banks(p),
                                              rel_bias[:].rearrange("i (b h) j -> i b (h j)", b=4), ALU.add))
                        sc = pr
                    chain(V.tensor_reduce(mx[p][:].rearrange("q (b h) -> q b h", b=4), sc, AX.X, ALU.max))
                    V.tensor_tensor(pr, sc, bcast(mx[p][:].rearrange("q (b h) -> q b h", b=4).unsqueeze(3),
                                                  [128, 4, 4, 128]), ALU.subtract).then_inc(S["shifted"], 1)
                for p in range(SLOTS):
                    u1 = SLOTS * i + p + 1
                    dve.wait_ge(S["mixed"], u1)
                    chain(V.reciprocal(r_z[p][:], ps[64:128, 4 * p, 0:256].rearrange("d (g q) -> d g q", g=2)))
                    for g in range(2):
                        ins = V.tensor_tensor(att_T[p][64 * g:64 * g + 64, :],
                                              ps[0:64, 4 * p, 128 * g:128 * g + 128], r_z[p][:, g, :], ALU.mult)
                    ins.then_inc(S["mixed_ready"], 1)
                ks = []
                for p in range(SLOTS):
                    u1 = SLOTS * i + p + 1
                    dve.wait_ge(S["projected"], u1)
                    ins = V.tensor_tensor(z2[p][:], xs[p][:], b_proj[l][:], ALU.add)
                    if l == 0:
                        ins.then_inc(s_x_used, 1)
                        dve.wait_ge(s_x_used, u1)
                    else:
                        chain(ins)
                    chain(V.tensor_tensor(z[p][:], bank(p, 0)[:, 0:128], z2[p][:], ALU.add))
                    ks.append(norm_begin(z[p][:], LN_EPS))
                for p in range(SLOTS):
                    norm_end(ks[p], outs[p][:], z[p][:]).then_inc(done, 1)

            def cross(i):
                for p in range(SLOTS):
                    u1 = SLOTS * i + p + 1
                    dve.wait_ge(X["k_ready"], u1)
                    for hp in range(2):
                        r = slice(64 * hp, 64 * hp + 64)
                        ins = V.tensor_copy(k_exp[p][r, :, hp, 0:M],
                                            ps[r, 4 * p + 2:4 * p + 4, :].rearrange("d b (c k) -> d (b c) k", k=128)
                                            [:, :, 0:M])
                    ins.then_inc(X["k_copied"], 1)
                for p in range(SLOTS):
                    u1 = SLOTS * i + p + 1
                    dve.wait_ge(X["scores_ready"], u1)
                    sc = banks(p)[:, :, 0:4 * MK].rearrange("q b (h k) -> q b h k", h=4)
                    pr = wide_p[p][:, 0:XH * MK].rearrange("q (b h k) -> q b h k", b=4, h=4)
                    chain(V.tensor_reduce(mx[p][:].rearrange("q (b h) -> q b h", b=4), sc, AX.X, ALU.max))
                    V.tensor_tensor(pr, sc, bcast(mx[p][:].rearrange("q (b h) -> q b h", b=4).unsqueeze(3),
                                                  [128, 4, 4, MK]), ALU.subtract).then_inc(X["shifted"], 1)
                for p in range(SLOTS):
                    u1 = SLOTS * i + p + 1
                    dve.wait_ge(X["probs_ready"], u1)
                    pr = wide_p[p][:, 0:XH * MK].rearrange("q (h k) -> q h k", h=XH)
                    chain(V.tensor_reduce(sums[p][:], pr, AX.X, ALU.add))
                    chain(V.reciprocal(rsum[p][:], sums[p][:]))
                    V.tensor_tensor(pr, pr, bcast(rsum[p][:].unsqueeze(2), [128, XH, MK]),
                                    ALU.mult).then_inc(X["normalized"], 1)
                ks = []
                for p in range(SLOTS):
                    dve.wait_ge(X["projected"], SLOTS * i + p + 1)
                    chain(V.tensor_copy(z[p][:], bank(p, 2)[:, 0:128]))
                    ks.append(norm_begin(z[p][:], XLN_EPS))
                for p in range(SLOTS):
                    chain(norm_end(ks[p], z2[p][:], z[p][:]))
                    chain(V.tensor_tensor(z2[p][:], z2[p][:], x_scale[:], ALU.mult))
                    chain(V.tensor_tensor(z[p][:], x_1[p][:], x_bias[:], ALU.add))
                    chain(V.tensor_tensor(z[p][:], z[p][:], z2[p][:], ALU.add))
                    ks[p] = norm_begin(z[p][:], LN_EPS)
                for p in range(SLOTS):
                    norm_end(ks[p], x_2[p][:], z[p][:]).then_inc(s_x2, 1)

            def experts(i):
                for p in range(SLOTS):
                    u1 = SLOTS * i + p + 1
                    dve.wait_ge(F["logits_ready"], u1)
                    chain(V.tensor_tensor(logit[p][:], bank(p, 0)[:, 0:E], b_r[:], ALU.add))
                    settle()
                    chain(V.max(top8[p][:], logit[p][:]))
                    settle()
                    V.max_index(top8i[p][:], top8[p][:], logit[p][:])
                    V.tensor_scalar(sm[p][:, 0:1], top8[p][:, 0:1], -1.0, None, ALU.mult).then_inc(F["max_ready"], 1)
                for p in range(SLOTS):
                    u1 = SLOTS * i + p + 1
                    dve.wait_ge(F["exp_ready"], u1)
                    chain(V.tensor_copy(sm[p][:, 2:3], top8i[p][:, 0:1]))
                    chain(V.reciprocal(sm[p][:, 3:4], sm[p][:, 1:2]))
                    V.tensor_scalar(w_one[p][:], iota8[:], sm[p][:, 2:3], sm[p][:, 3:4], ALU.is_equal,
                                    ALU.mult).then_inc(F["gate_ready"], 1)
                for p in range(SLOTS):
                    u1 = SLOTS * i + p + 1
                    dve.wait_ge(F["hidden_ready"], u1)
                    V.tensor_tensor(wide_a[p][:].rearrange("h (b k t) -> h b k t", b=4, k=4),
                                    banks(p).rearrange("h b (k t) -> h b k t", k=4),
                                    bcast(cols[:, R_B1:R_B1 + 16].rearrange("h (b k) -> h b k", b=4).unsqueeze(3),
                                          [128, 4, 4, 128]), ALU.add).then_inc(F["biased"], 1)
                ks = []
                for p in range(SLOTS):
                    u1 = SLOTS * i + p + 1
                    dve.wait_ge(F["outputs_ready"], u1)
                    dve.wait_ge(F["gate_ready"], u1)
                    y = wide_p[p][:, 0:1024].rearrange("t (e d) -> t e d", e=E)
                    chain(V.tensor_tensor(y, ps[:, 4 * p:4 * p + 2, :].rearrange("t b (e d) -> t (b e) d", d=128),
                                          bcast(w_one[p][:].unsqueeze(2), [128, E, 128]), ALU.mult))
                    chain(V.tensor_reduce(z[p][:], y.rearrange("t e d -> t d e"), AX.X, ALU.add))
                    chain(V.tensor_tensor(z2[p][:], z[p][:], x_2[p][:], ALU.add))
                    dve.wait_ge(F["weighted"], u1)
                    chain(V.tensor_tensor(z[p][:], bank(p, 3)[:, 0:128], z2[p][:], ALU.add))
                    ks.append(norm_begin(z[p][:], LN_EPS))
                for p in range(SLOTS):
                    norm_end(ks[p], x_3[p][:], z[p][:]).then_inc(s_x3, 1)

            def patches(i):
                kx, kc = [], []
                for p in range(SLOTS):
                    u1 = SLOTS * i + p + 1
                    dve.wait_ge(s_x4, u1)
                    k = variance(RMS_EPS)
                    V.tensor_tensor(z[p][:], x_4[p][:], x_4[p][:], ALU.mult)
                    chain(V.tensor_tensor(c_sq[p][:], c_in[p][:], c_in[p][:], ALU.mult))
                    V.tensor_reduce(sm[p][:, 4:5], z[p][:], AX.X, ALU.add)
                    chain(V.tensor_reduce(sm[p][0:M, 5:6], c_sq[p][:], AX.X, ALU.add))
                    V.tensor_scalar(veps[:, k:k + 1], sm[p][:, 4:5], 1.0 / D, RMS_EPS, ALU.mult,
                                    ALU.add).then_inc(s_var, 1)
                    kx.append(k)
                    k = variance(RMS_EPS)
                    V.tensor_scalar(veps[0:M, k:k + 1], sm[p][0:M, 5:6], 1.0 / CTX, RMS_EPS, ALU.mult,
                                    ALU.add).then_inc(s_var, 1)
                    kc.append(k)
                for p in range(SLOTS):
                    u = SLOTS * i + p
                    V.tensor_copy(plug_now[p][:].unsqueeze(1), plug_T[:, bass.ds(u, 1), :])
                    wait_rstd(kc[p])
                    ins = V.tensor_scalar(patch[p][:], c_in[p][:, 0:128], rstd[0:M, kc[p]:kc[p] + 1], BCOEF,
                                          ALU.mult, ALU.mult)
                    ins.then_inc(s_c_used, 1)
                    dve.wait_ge(s_c_used, u + 1)
                    V.tensor_tensor(patch[p][:], patch[p][:], g_init[0:M, :], ALU.mult).then_inc(G["rows_ready"], 1)
                ks = []
                for p in range(SLOTS):
                    u1 = SLOTS * i + p + 1
                    chain(V.tensor_tensor(z2[p][:], x_4[p][:], b_in[:], ALU.add))
                    dve.wait_ge(G["products_ready"], u1)
                    chain(V.scalar_tensor_tensor(out=z[p][:], in0=bank(p, 1)[:, 0:128],
                                                 scalar=rstd[:, kx[p]:kx[p] + 1], in1=z2[p][:],
                                                 op0=ALU.mult, op1=ALU.add))
                    chain(V.tensor_tensor(z[p][:], bank(p, 2)[:, 0:128], z[p][:], ALU.add))
                    ks.append(norm_begin(z[p][:], LN_EPS))
                for p in range(SLOTS):
                    u = SLOTS * i + p
                    norm_end(ks[p], x_5[p][:, 0:128], z[p][:]).then_inc(s_x5, 1)
                for p in range(SLOTS):
                    u = SLOTS * i + p
                    dve.wait_ge(s_x5, u + 1)
                    V.tensor_copy(x5[:, bass.ds(u, 1), :], x_5[p][:, 0:128].unsqueeze(1))
                    dve.wait_ge(s_x5T, u + 1)
                    chain(V.tensor_tensor(cov[:], cov[:], bank(p, 3)[:, 0:129], ALU.add))
                for p in range(SLOTS):
                    u = SLOTS * i + p
                    dve.wait_ge(s_x5T_ready, u + 1)
                    V.memset(sums[p][:, 0:1], 0.0).then_inc(s_slot, 1)

            with dve.Fori(0, ROUNDS) as i:
                state.update(i=i, links=0, roots=0)
                attention(0, i, x_in, s_x1, x_1)
                cross(i)
                experts(i)
                attention(1, i, x_3, s_x4, x_4)
                patches(i)
                assert state["links"] == LINKS, state["links"]
                assert state["roots"] == SLOTS * RSTDS

        first.close()
        loop1.close()
        product_keys(nc, ctx, ps, out, dict(
            ident=ident, ones=ones_col, neg_half=neg_half, cols=cols, spare=spare, x5=x5, x5T=x5T, cov=cov,
            w_q=pk_wq, keys=pk_keys, down=pk_down, up=pk_up, loaded=s_pk))


def product_keys(nc, ctx, ps, out, c):
    ident, ones, cols, x5, x5T, cov = c["ident"], c["ones"], c["cols"], c["x5"], c["x5T"], c["cov"]
    spare = c["spare"]
    N = B * T
    SEG = NK + TOP

    def sb(name, shape, dt=F32):
        return ctx.enter_context(nc.sbuf_tensor(name, shape, dt))

    def pair(name, shape, dt=F32):
        return [sb(f"{name}{p}", shape, dt) for p in range(SLOTS)]

    def sem(name):
        return ctx.enter_context(nc.semaphore(name))

    wqT = sb("wqT", [128, 2 * PH, 128])
    keysT = sb("keysT", [128, 2 * PH, NK])
    downT = sb("downT", [128, NE])
    covn = sb("covn", [128, 129])
    mean_row = sb("mean_row", [1, 128])
    wu = sb("wu", [128, 2 * PH, KD])
    fold = sb("fold", [128, 4, 2 * PH])
    means = sb("means", [128, 2 * PH])
    keys_s = sb("keys_s", [128, 2 * PH, NK])
    keys_b = sb("keys_b", [128, 2 * PH, NK])
    w_sim = sb("w_sim", [128, 512])
    b_sim = sb("b_sim", [128, 512])
    act_all = sb("act_all", [128, B, NE])
    xg = pair("xg", [128, 128])
    xs = pair("xs", [128, 128])
    halves = pair("halves", [128, 2 * PH, SEG])
    cand = pair("cand", [128, PH, TOP * TOP])
    mxs = pair("mxs", [128, 2 * PH])
    best = pair("best", [128, PH, TOP])
    total = pair("total", [128, PH])
    inv = pair("inv", [128, PH])
    outer = [[sb(f"outer{p}{k}", [128, NE]) for k in range(2)] for p in range(SLOTS)]
    kept = sb("kept", [128, NE])
    mix = pair("mix", [128, NE])
    mixT = pair("mixT", [128, NE])
    z = pair("fz", [128, 128])
    y = pair("fy", [128, 128])
    stats = sb("fstats", [128, SLOTS, 6])
    mv = sb("fmv", [128, SLOTS, 2])
    veps = sb("fveps", [128, SLOTS])
    rstd = sb("frstd", [128, SLOTS])

    s_turn = sem("pk_weights_turned")
    s_turned = sem("pk_turned_copied")
    s_mean = sem("pk_mean_ready")
    s_meanT = sem("pk_mean_turned")
    s_mrow = sem("pk_mean_row_ready")
    s_outer = sem("pk_mean_product_ready")
    s_covc = sem("pk_covariance_ready")
    s_u = sem("pk_covariance_times_weights")
    s_wu = sem("pk_squares_ready")
    s_vm = sem("pk_variance_and_mean_ready")
    s_veps = sem("pk_variance_copied")
    s_root = sem("pk_root_ready")
    s_ks = sem("pk_scaled_keys_ready")
    s_fold = sem("pk_folded_weights_ready")
    s_folded = sem("pk_folded_weights_copied")
    s_mid = sem("pk_fold_chain")
    s_xg = sem("gelu_x_copied")
    s_gp = sem("gelu_products_ready")
    s_g = sem("gelu_ready")
    s_xs = sem("score_x_copied")
    s_sim = sem("half_scores_ready")
    s_simc = sem("half_scores_shifted")
    s_exp = sem("half_exps_ready")
    s_cut = sem("cut_ready")
    s_pr = sem("outer_product_ready")
    s_used = sem("outer_product_used")
    s_mix = sem("mix_ready")
    s_mixT = sem("mix_turned")
    s_mixTc = sem("mixT_ready")
    s_y = sem("experts_summed")
    s_v = sem("final_variance_ready")
    s_r = sem("final_root_ready")
    s_fin = sem("result_ready")
    s_out = [sem(f"result{p}_stored") for p in range(SLOTS)]
    s_ch = sem("final_vector_chain")

    with nc.Block() as block:

        @block.sync
        def _(sp):
            with sp.Fori(0, ROUNDS) as i:
                for p in range(SLOTS):
                    u = SLOTS * i + p
                    sp.wait_ge(s_fin, u + 1)
                    sp.dma_start(out[bass.ds(u, 1)].rearrange("o t d -> t (o d)"), y[p][:]).then_inc(s_out[p], 16)
            for p in range(SLOTS):
                sp.wait_ge(s_out[p], 16 * (ROUNDS + 1))

        @block.tensor
        def _(pe):
            pe.wait_ge(c["loaded"], 64)
            for k in range(2 * PH):
                nc.tensor.transpose(ps[:, k // 4, 128 * (k % 4):128 * (k % 4) + 128], c["w_q"][:, k, :], ident[:])
            for half in range(2):
                for t in range(2):
                    nc.tensor.transpose(ps[:, 4, 256 * half + 128 * t:256 * half + 128 * t + 128],
                                        c["keys"][:, t, KD * half:KD * half + KD], ident[:])
            for k in range(NE // 128):
                mm = nc.tensor.transpose(ps[:, 5 + k // 4, 128 * (k % 4):128 * (k % 4) + 128],
                                         c["down"][:, k, :], ident[:])
            mm.then_inc(s_turn, 1)
            pe.wait_ge(s_mean, 1)
            nc.tensor.transpose(ps[0:1, 7, 0:128], covn[:, 128:129], ident[:]).then_inc(s_meanT, 1)
            pe.wait_ge(s_mrow, 1)
            nc.tensor.matmul(ps[:, 7, 0:128], mean_row[:], mean_row[:], start=True, stop=True).then_inc(s_outer, 1)
            pe.wait_ge(s_covc, 1)
            pe.wait_ge(s_turned, 1)
            for k in range(4):
                mm = nc.tensor.matmul(ps[:, k, :], covn[:, 0:128],
                                      c["w_q"][:, 4 * k:4 * k + 4, :].rearrange("k r d -> k (r d)"),
                                      start=True, stop=True)
            mm.then_inc(s_u, 1)
            pe.wait_ge(s_wu, 1)
            for k in range(2 * PH):
                nc.tensor.matmul(ps[:, 7, k:k + 1], wu[:, k, :], ones[:, 0:1], start=True, stop=True)
                mm = nc.tensor.matmul(ps[:, 7, 16 + k:17 + k], c["w_q"][:, k, :], covn[:, 128:129],
                                      start=True, stop=True)
            mm.then_inc(s_vm, 1)
            pe.wait_ge(s_ks, 1)
            for k in range(2 * PH):
                nc.tensor.matmul(ps[:, 5, NK * k:NK * k + NK], wqT[:, k, :], keys_s[:, k, :], start=True, stop=True)
            nc.tensor.matmul(ps[:, 6, :], ones[:], keys_b[:].rearrange("d r k -> d (r k)"), start=True,
                             stop=True).then_inc(s_fold, 1)

            with pe.Fori(0, ROUNDS) as i:
                for p in range(SLOTS):
                    u1 = SLOTS * i + p + 1
                    pe.wait_ge(s_xg, u1)
                    pe.wait_ge(s_g, u1)
                    for k in range(2):
                        mm = nc.tensor.matmul(ps[:, 2 * p + k, :], xg[p][:], downT[:, 512 * k:512 * k + 512],
                                              start=True, stop=True)
                    mm.then_inc(s_gp, 1)

            pe.wait_ge(s_folded, 1)
            with pe.Fori(0, ROUNDS) as i:
                for p in range(SLOTS):
                    u1 = SLOTS * i + p + 1
                    pe.wait_ge(s_xs, u1)
                    nc.tensor.matmul(ps[:, 4 * p, :], xs[p][:], w_sim[:], start=True, stop=True).then_inc(s_sim, 1)
                for p in range(SLOTS):
                    u1 = SLOTS * i + p + 1
                    pe.wait_ge(s_mix, u1)
                    for k in range(NE // 128):
                        mm = nc.tensor.transpose(ps[:, 4 * p + 1 + k // 4, 128 * (k % 4):128 * (k % 4) + 128],
                                                 mix[p][:, 128 * k:128 * k + 128], ident[:])
                    mm.then_inc(s_mixT, 1)
                    pe.wait_ge(s_mixTc, u1)
                    for k in range(NE // 128):
                        mm = nc.tensor.matmul(ps[:, 4 * p + 3, 0:128], mixT[p][:, 128 * k:128 * k + 128],
                                              c["up"][:, k, :], start=(k == 0), stop=(k == NE // 128 - 1))
                    mm.then_inc(s_y, 1)

        @block.scalar
        def _(act):
            act.wait_ge(s_turn, 1)
            nc.scalar.copy(wqT[:].rearrange("d (b r) k -> d b (r k)", b=4), ps[:, 0:4, :])
            nc.scalar.copy(keysT[:].rearrange("d r k -> d (r k)"), ps[:, 4, :])
            nc.scalar.copy(downT[:].rearrange("d (b n) -> d b n", b=2), ps[:, 5:7, :]).then_inc(s_turned, 1)
            for p in range(SLOTS):
                nc.scalar.copy(xg[p][:], ones[:]).then_inc(s_g, 1)
            act.wait_ge(s_folded, 1)
            act.wait_ge(s_g, 2)
            with act.Fori(0, ROUNDS) as i:
                for p in range(SLOTS):
                    u = SLOTS * i + p
                    nc.scalar.copy(xg[p][:].unsqueeze(1), x5T[:, bass.ds(u, 1), :]).then_inc(s_xg, 1)
                for p in range(SLOTS):
                    u = SLOTS * i + p
                    act.wait_ge(s_gp, u + 1)
                    nc.scalar.activation(act_all[:, bass.ds(u, 1), :].rearrange("t o (b n) -> t (o b) n", b=2),
                                         ps[:, 2 * p:2 * p + 2, :], ACT.Gelu_apprx_tanh).then_inc(s_g, 1)
            for p in range(SLOTS):
                nc.scalar.copy(xs[p][:].unsqueeze(1), x5T[:, p:p + 1, :]).then_inc(s_xs, 1)
            with act.Fori(0, ROUNDS) as i:
                for p in range(SLOTS):
                    u1 = SLOTS * i + p + 1
                    act.wait_ge(s_simc, u1)
                    nc.scalar.activation(halves[p][:], halves[p][:], ACT.Exp).then_inc(s_exp, 1)
                for p in range(SLOTS):
                    u1 = SLOTS * i + p + 1
                    act.wait_ge(s_mixT, u1)
                    nc.scalar.copy(mixT[p][:].rearrange("d (b n) -> d b n", b=2),
                                   ps[:, 4 * p + 1:4 * p + 3, :]).then_inc(s_mixTc, 1)
                    nxt = (SLOTS * i + p + SLOTS) % B
                    nc.scalar.copy(xs[p][:].unsqueeze(1), x5T[:, bass.ds(nxt, 1), :]).then_inc(s_xs, 1)

        @block.gpsimd
        def _(pool):
            pool.wait_ge(s_veps, 1)
            nc.gpsimd.tensor_tensor(out=fold[:, 1, :], in0=fold[:, 0, :], in1=c["neg_half"][:], op=ALU.pow
                                    ).then_inc(s_root, 1)
            with pool.Fori(0, ROUNDS) as i:
                for p in range(SLOTS):
                    pool.wait_ge(s_cut, SLOTS * i + p + 1)
                    for h in range(PH):
                        pool.wait_ge(s_used, PH * (SLOTS * i + p) + h + 1)
                        nc.gpsimd.tensor_tensor(
                            out=outer[0][h % 2][:].rearrange("t (a b) -> t a b", a=NK),
                            in0=bcast(halves[p][:, h, 0:NK].unsqueeze(2), [128, NK, NK]),
                            in1=bcast(halves[p][:, PH + h, 0:NK].unsqueeze(1), [128, NK, NK]),
                            op=ALU.mult).then_inc(s_pr, 1)
                for p in range(SLOTS):
                    pool.wait_ge(s_v, SLOTS * i + p + 1)
                    nc.gpsimd.tensor_tensor(out=rstd[:, p:p + 1], in0=veps[:, p:p + 1],
                                            in1=c["neg_half"][:, 0:1], op=ALU.pow).then_inc(s_r, 1)

        @block.vector
        def _(dve):
            V = nc.vector
            n = [0]

            def link(ins):
                n[0] += 1
                ins.then_inc(s_mid, 1)
                dve.wait_ge(s_mid, n[0])

            link(V.tensor_scalar(covn[:], cov[:], 1.0 / N, None, ALU.mult))
            V.memset(veps[:], 1.0).then_inc(s_mean, 1)
            dve.wait_ge(s_meanT, 1)
            V.tensor_copy(mean_row[:], ps[0:1, 7, 0:128]).then_inc(s_mrow, 1)
            dve.wait_ge(s_outer, 1)
            V.tensor_tensor(covn[:, 0:128], covn[:, 0:128], ps[:, 7, 0:128], ALU.subtract).then_inc(s_covc, 1)
            dve.wait_ge(s_u, 1)
            V.tensor_tensor(wu[:].rearrange("d (b r) k -> d b (r k)", b=4), ps[:, 0:4, :],
                            c["w_q"][:].rearrange("d (b r) k -> d b (r k)", b=4), ALU.mult).then_inc(s_wu, 1)
            dve.wait_ge(s_vm, 1)
            link(V.tensor_copy(means[:], ps[:, 7, 16:32]))
            V.tensor_scalar(fold[:, 0, :], ps[:, 7, 0:16], BN_EPS, None, ALU.add).then_inc(s_veps, 1)
            dve.wait_ge(s_root, 1)
            link(V.tensor_tensor(fold[:, 2, :], fold[:, 1, :], cols[:, R_GAMMA:R_GAMMA + 16], ALU.mult))
            link(V.tensor_tensor(fold[:, 3, :], means[:], fold[:, 2, :], ALU.mult))
            link(V.tensor_tensor(fold[:, 3, :], cols[:, R_BETA:R_BETA + 16], fold[:, 3, :], ALU.subtract))
            dve.wait_ge(s_turned, 1)
            link(V.tensor_tensor(keys_s[:], keysT[:], bcast(fold[:, 2, :].unsqueeze(2), [128, 2 * PH, NK]), ALU.mult))
            V.tensor_tensor(keys_b[:], keysT[:], bcast(fold[:, 3, :].unsqueeze(2), [128, 2 * PH, NK]),
                            ALU.mult).then_inc(s_ks, 1)
            dve.wait_ge(s_fold, 1)
            V.tensor_copy(w_sim[:], ps[:, 5, :])
            V.tensor_copy(b_sim[:], ps[:, 6, :]).then_inc(s_folded, 1)
            for p in range(SLOTS):
                V.memset(z[p][:, 0:1], 0.0).then_inc(s_used, 1)
                V.memset(best[p][:, 0:1, 0:1], 0.0).then_inc(s_out[p], 16)
            dve.wait_ge(s_folded, 1)
            dve.wait_ge(s_g, B + SLOTS)

            LINKS = FINAL_LINKS
            state = {}

            def settle():
                V.memset(spare[:], 0.0)

            def chain(ins):
                state["links"] += 1
                ins.then_inc(s_ch, 1)
                dve.wait_ge(s_ch, LINKS * state["i"] + state["links"])

            with dve.Fori(0, ROUNDS) as i:
                state.update(i=i, links=0)
                for p in range(SLOTS):
                    u1 = SLOTS * i + p + 1
                    dve.wait_ge(s_sim, u1)
                    hv = halves[p]
                    chain(V.tensor_tensor(hv[:, :, 0:NK], ps[:, 4 * p, :].rearrange("t (r k) -> t r k", k=NK),
                                          b_sim[:].rearrange("t (r k) -> t r k", k=NK), ALU.add))
                    settle()
                    for r in range(2 * PH):
                        ins = V.max(hv[:, r, NK:SEG], hv[:, r, 0:NK])
                    chain(ins)
                    chain(V.tensor_copy(mxs[p][:], hv[:, :, NK]))
                    V.tensor_tensor(hv[:], hv[:], bcast(mxs[p][:].unsqueeze(2), [128, 2 * PH, SEG]),
                                    ALU.subtract).then_inc(s_simc, 1)
                for p in range(SLOTS):
                    u1 = SLOTS * i + p + 1
                    dve.wait_ge(s_exp, u1)
                    hv = halves[p]
                    chain(V.tensor_tensor(cand[p][:].rearrange("t h (a b) -> t h a b", a=TOP),
                                          bcast(hv[:, 0:PH, NK:SEG].unsqueeze(3), [128, PH, TOP, TOP]),
                                          bcast(hv[:, PH:2 * PH, NK:SEG].unsqueeze(2), [128, PH, TOP, TOP]), ALU.mult))
                    settle()
                    for h in range(PH):
                        ins = V.max(best[p][:, h, :], cand[p][:, h, :])
                    chain(ins)
                    chain(V.tensor_reduce(total[p][:], best[p][:], AX.X, ALU.add))
                    V.reciprocal(inv[p][:], total[p][:]).then_inc(s_cut, 1)
                for p in range(SLOTS):
                    u1 = SLOTS * i + p + 1
                    dve.wait_ge(s_cut, u1)
                    for h in range(PH):
                        dve.wait_ge(s_pr, PH * (SLOTS * i + p) + h + 1)
                        o = outer[0][h % 2][:]
                        ins = V.scalar_tensor_tensor(out=kept[:], in0=o, scalar=best[p][:, h, TOP - 1:TOP], in1=o,
                                                     op0=ALU.is_ge, op1=ALU.mult)
                        ins.then_inc(s_used, 1)
                        dve.wait_ge(s_used, PH * (SLOTS * i + p) + h + 1 + SLOTS)
                        if h == 0:
                            chain(V.tensor_scalar(mix[p][:], kept[:], inv[p][:, 0:1], None, ALU.mult))
                        else:
                            chain(V.scalar_tensor_tensor(out=mix[p][:], in0=kept[:], scalar=inv[p][:, h:h + 1],
                                                         in1=mix[p][:], op0=ALU.mult, op1=ALU.add))
                    u = SLOTS * i + p
                    V.tensor_tensor(mix[p][:].unsqueeze(1), mix[p][:].unsqueeze(1), act_all[:, bass.ds(u, 1), :],
                                    ALU.mult).then_inc(s_mix, 1)
                for p in range(SLOTS):
                    u = SLOTS * i + p
                    dve.wait_ge(s_y, u + 1)
                    chain(V.tensor_tensor(z[p][:].unsqueeze(1), ps[:, 4 * p + 3:4 * p + 4, 0:128],
                                          x5[:, bass.ds(u, 1), :], ALU.add))
                    chain(V.bn_stats(stats[:, p, :], z[p][:]))
                    settle()
                    chain(V.bn_aggr(mv[:, p, :], stats[:, p, :]))
                    V.tensor_scalar(veps[:, p:p + 1], mv[:, p, 1:2], LN_EPS, None, ALU.add).then_inc(s_v, 1)
                for p in range(SLOTS):
                    u = SLOTS * i + p
                    dve.wait_ge(s_r, u + 1)
                    dve.wait_ge(s_out[p], 16 * i + 16)
                    V.tensor_scalar(y[p][:], z[p][:], mv[:, p, 0:1], rstd[:, p:p + 1], ALU.subtract,
                                    ALU.mult).then_inc(s_fin, 1)
                assert state["links"] == LINKS, state["links"]


INPUTS = (
    "x", "ctx_2048", "mask_BxS2_if0", "L0_attn_W_qkv", "L0_attn_b_qkv", "L0_attn_W_proj", "L0_attn_b_proj",
    "L0_xattn_Wq", "L0_xattn_Wkv", "L0_xattn_null_kv", "L0_xattn_Wout", "L0_xattn_ln_scale",
    "L0_xattn_ln_bias", "L0_ffn_Wr", "L0_ffn_br", "L0_ffn_W1", "L0_ffn_b1", "L0_ffn_W2", "L0_ffn_b2",
    "L1_attn_Wq", "L1_attn_bq", "L1_attn_Wk", "L1_attn_bk", "L1_attn_Wv", "L1_attn_bv", "L1_attn_Wo",
    "L1_attn_bo", "L1_xattn_W_in", "L1_xattn_b_in", "L1_xattn_g_res", "L1_xattn_g_init", "L1_ffn_w_q",
    "L1_ffn_bn_gamma", "L1_ffn_bn_beta", "L1_ffn_keys", "L1_ffn_down_embed", "L1_ffn_up_embed")


def kernel(**inputs):
    import concourse.bacc as bacc
    from concourse.bass_utils import run_bass_kernel_spmd

    nc = bacc.Bacc("TRN2", target_bir_lowering=False, num_devices=1)
    arrays, args = {}, {}
    laid = {name: np.ascontiguousarray(inputs[name]) for name in INPUTS}
    laid["rel_rev"] = np.ascontiguousarray(np.asarray(inputs["L1_attn_rel_table"])[::-1].T)
    for name, arr in laid.items():
        arrays[f"in_{name}"] = arr
        args[name] = nc.dram_tensor(f"in_{name}", arr.shape, mybir.dt.from_np(arr.dtype),
                                    kind="ExternalInput").ap()
    result = nc.dram_tensor("result", [B, T, D], F32, kind="ExternalOutput").ap()
    build(nc, args, result)
    r = run_bass_kernel_spmd(nc, [arrays], core_ids=[0])
    return r.results[0]["result"]
```

```python
from contextlib import ExitStack

import numpy as np

import concourse.bass as bass
from concourse import mybir

ALU = mybir.AluOpType
ACT = mybir.ActivationFunctionType
AX = mybir.AxisListType
F32 = mybir.dt.float32
BF16 = mybir.dt.bfloat16
I32 = mybir.dt.int32
U32 = mybir.dt.uint32

B, T, D = 16, 128, 128
SLOTS = 2
ROUNDS = B // SLOTS
HEADS, DH = 16, 8
XH, XDH = 16, 64
XC = XH * XDH // 128
M, CTX = 77, 256
MK = M + 1
E, HID = 8, 256
HC = HID // 128
PH, KD, NK = 8, 128, 32
TOP = 8
NE = NK * NK
LN_EPS = 1e-5
XLN_EPS = 1e-6
RMS_EPS = 1e-5
BN_EPS = 1e-5
MASKED = -1e30
LOGP = -0.001
DT = float(-np.log(-np.expm1(np.float32(LOGP))))
BCOEF = float(np.exp(np.float32(LOGP)))

FIRST_LINKS = 22
SECOND_LINKS = 27
PREP_LINKS = 5
TAIL_LINKS = 3
R_B1, R_GAMMA, R_BETA = 0, 16, 32
R_BQK0, R_BQK1, R_GRES, R_NULLK = 48, 50, 52, 53
NROWS = 54

ROOT_1, ROOT_X, ROOT_2, ROOT_ROWS, ROOT_3, ROOT_4, ROOT_IN, ROOT_5 = range(8)
RSTDS = 8
ROOTS_OF_HALF = (3, 5)

NCH = 4
ORDER = "SF" * 13 + "FF"


HALVES = ("F", "S", ORDER)
LAST_ORDER = "MTMPTMPMPTMPMPMPMPP"


def weave(order, **parts):
    for which in order:
        if parts[which] is not None:
            next(parts[which])


def steps(engine, order, first, second, begin=lambda step: None):
    f, g = order[0], order[1]
    both = order[2]
    begin(0)
    weave(both, **{f: first(0, 0), g: None})
    with engine.Fori(0, ROUNDS - 1) as i:
        begin(SLOTS * i + 1)
        weave(both, **{f: first(SLOTS * i + 1, 1), g: second(SLOTS * i, 0)})
        begin(SLOTS * i + 2)
        weave(both, **{f: first(SLOTS * i + 2, 0), g: second(SLOTS * i + 1, 1)})
    begin(B - 1)
    weave(both, **{f: first(B - 1, 1), g: second(B - 2, 0)})
    begin(B)
    weave(both, **{f: None, g: second(B - 1, 1)})


def last_steps(engine, prepare, mix, tail, begin=lambda step: None):
    def step(u, p, t, m, e):
        begin(u)
        weave(LAST_ORDER, P=prepare(u, p) if t else None, M=mix(u - 1, 1 - p) if m else None,
              T=tail(u - 2, p) if e else None)

    step(0, 0, True, False, False)
    step(1, 1, True, True, False)
    with engine.Fori(0, ROUNDS - 1) as i:
        for p in range(SLOTS):
            step(SLOTS * i + SLOTS + p, p, True, True, True)
    step(B, 0, False, True, True)
    step(B + 1, 1, False, False, True)


def bcast(ap, shape):
    return ap.broadcast_to(shape)


def build(nc, a, out):
    with ExitStack() as ctx:
        def sb(name, shape, dt=F32, where=ctx):
            return where.enter_context(nc.sbuf_tensor(name, shape, dt))

        def sem(name):
            return ctx.enter_context(nc.semaphore(name))

        ps = ctx.enter_context(nc.psum_tensor("ps", [128, 8, 512], F32))

        ident = sb("ident", [128, 128])
        neg_half = sb("neg_half", [128, 16])
        ones_col = sb("ones_col", [128, 128])
        cols = sb("cols", [128, NROWS])
        spare = sb("spare", [1, 1])
        x5 = sb("x5", [128, B, 128])
        x5T = sb("x5T", [128, B, 128])
        cov = sb("cov", [128, 129])
        pk_wq = sb("pk_wq", [128, 2 * PH, KD])
        pk_keys = sb("pk_keys", [128, 2, 2 * KD])
        pk_down = sb("pk_down", [128, NE // 128, 128])
        pk_up = sb("pk_up", [128, NE // 128, 128])

        loop1 = ctx.enter_context(ExitStack())

        def sb1(name, shape, dt=F32):
            return sb(name, shape, dt, loop1)

        ident16 = sb1("ident16", [128, 128], BF16)
        causal16 = sb1("causal16", [128, 4, 128], BF16)
        head_mask = sb1("head_mask", [128, HEADS])
        iota8 = sb1("iota8", [128, E])
        iota_col = sb1("iota_col", [128, 1])

        w_qkv = [sb1(f"w_qkv{l}", [128, 3, 128]) for l in range(2)]
        w_proj = [sb1(f"w_proj{l}", [128, 128]) for l in range(2)]
        b_v = [sb1(f"b_v{l}", [128, 128]) for l in range(2)]
        b_proj = [sb1(f"b_proj{l}", [128, 128]) for l in range(2)]
        rel_bias = sb1("rel_bias", [128, HEADS, 128])
        xw_q = sb1("xw_q", [128, XC * 128])
        xw_kv = sb1("xw_kv", [128, 2, 2 * XC * 128])
        xw_out = sb1("xw_out", [128, XC, 128])
        x_scale = sb1("x_scale", [128, 128])
        x_bias = sb1("x_bias", [128, 128])
        w_r = sb1("w_r", [128, E])
        b_r = sb1("b_r", [128, E])
        w_1 = sb1("w_1", [128, E, HID])
        w_2 = sb1("w_2", [128, E, HC, 128])
        b_2 = sb1("b_2", [E, 128])
        w_inT = sb1("w_inT", [128, 128])
        b_in = sb1("b_in", [128, 128])
        g_init = sb1("g_init", [128, 128])
        plug_T = sb1("plug_T", [M, B, 128])


        rel_dram = nc.dram_tensor("rel_scratch", [HEADS, 256], F32, kind="Internal").ap()
        plug_dram = nc.dram_tensor("plug_scratch", [B, 128], F32, kind="Internal").ap()

        s_w0 = sem("first_attention_weights_loaded")
        s_wx = sem("cross_attention_weights_loaded")
        s_we = sem("expert_weights_loaded")
        s_w1 = sem("second_attention_weights_loaded")
        s_wp = sem("patch_weights_loaded")
        s_rows = sem("rows_loaded")
        s_pk = sem("product_key_weights_loaded")
        s_rel = sem("relative_table_loaded")
        s_rel_ext = sem("relative_table_extended")
        s_rel_out = sem("relative_table_stored")
        s_rel_in = sem("relative_bias_loaded")
        s_rel_fl = sem("relative_bias_flipped")
        s_plen = sem("patch_lengths_loaded")
        s_plug = sem("plug_ready")
        s_plug_out = sem("plug_stored")
        s_plug_in = sem("plug_spread")
        s_const = sem("pool_constants_ready")
        s_zero = sem("vector_constants_ready")
        s_setup = sem("vector_setup_chain")
        s_pchain = sem("pool_chain")
        s_rowsT = sem("rows_turned")
        s_cols = sem("columns_ready")
        s_winT = sem("w_in_turned")
        s_setup_done = sem("vector_setup_done")
        s_ev = sem("plug_exp_ready")
        s_nullv = sem("null_value_loaded")
        s_vz = sem("value_zeros_ready")

        def pair(name, shape, dt=F32):
            return [sb(f"{name}{p}", shape, dt, loop1) for p in range(SLOTS)]

        x_in = pair("x_in", [128, 128])
        c_in = pair("c_in", [M, CTX])
        wide_a = pair("wide_a", [128, 2048])
        wide_p = pair("wide_p", [128, 2048])
        wide_t = pair("wide_t", [128, 2048])
        v_exp = pair("v_exp", [128, HEADS, 128])
        v_z = pair("v_z", [MK, XH, 128])
        k_exp = pair("k_exp", [128, XC, 2, MK])
        c_T = pair("c_T", [128, 2, M])
        x_T = pair("x_T", [128, 128])
        k_T = pair("k_T", [128, 128])
        att_T = pair("att_T", [128, 128])
        mx = pair("mx", [128, 16])
        sums = pair("sums", [128, 16])
        rsum = pair("rsum", [128, 16])
        z = pair("z", [128, 128])
        z2 = pair("z2", [128, 128])
        x_1 = pair("x_1", [128, 128])
        x_2 = pair("x_2", [128, 128])
        x_3 = pair("x_3", [128, 128])
        x_5 = pair("x_5", [128, 129])
        logit = pair("logit", [128, E])
        logit_e = pair("logit_e", [128, E])
        top8 = pair("top8", [128, 8])
        top8i = pair("top8i", [128, 8], U32)
        sm = pair("sm", [128, 8])
        w_one = pair("w_one", [128, E])
        w_oneT = pair("w_oneT", [E, 128])
        stats = sb("stats", [128, SLOTS * RSTDS, 6], F32, loop1)
        mv = sb("mv", [128, SLOTS * RSTDS, 2], F32, loop1)
        veps = sb("veps", [128, SLOTS * RSTDS], F32, loop1)
        rstd = sb("rstd", [128, SLOTS * RSTDS], F32, loop1)

        r_z = [wide_a[p][0:64, 0:256].rearrange("d (g q) -> d g q", g=2) for p in range(SLOTS)]
        x_4 = x_1
        squares = [wide_t[p][:, 1024:1024 + CTX] for p in range(SLOTS)]
        plug_now = [wide_t[p][0:M, 1536:1664] for p in range(SLOTS)]
        plen_i = wide_t[0][0:B, 1152:1152 + M].bitcast(I32)
        flip = wide_t[1][:, 128:256]
        w_in = wide_t[1][:, 256:384]
        rows = wide_t[1][0:NROWS, 384:512]

        s_x = [sem(f"x{p}_loaded") for p in range(SLOTS)]
        s_c = [sem(f"context{p}_loaded") for p in range(SLOTS)]
        s_slot = sem("slot_free")
        A = [{n: sem(f"attention{l}_{n}") for n in (
            "x_turned", "xT_ready", "qkv_ready", "masked_q_ready", "v_ready", "scores_ready",
            "shifted", "probs_ready", "probs_turned", "probsT_ready", "mixed", "mixed_ready",
            "residual_ready", "projected")} for l in range(2)]
        X = {n: sem(f"cross_{n}") for n in (
            "c_turned", "cT_ready", "k_ready", "k_copied", "v_ready", "v_copied",
            "x_turned", "xT_ready", "q_ready", "q_copied", "scores_ready", "shifted", "probs_ready",
            "normalized", "probs_turned", "probsT_ready", "mixed", "mixed_copied", "residual_ready",
            "projected")}
        F = {n: sem(f"experts_{n}") for n in (
            "x_turned", "xT_ready", "logits_ready", "max_ready", "exp_ready", "gate_ready",
            "gate_turned", "gateT_ready", "hidden_ready", "relu_even", "relu_odd", "outputs_ready",
            "weighted")}
        G = {n: sem(f"patch_{n}") for n in (
            "x_turned", "xT_ready", "row_squares", "x_squares", "rows_scaled", "rows_ready",
            "plug_taken", "row_product", "input_product", "residual_ready", "x5_kept", "summed")}
        s_x1 = sem("x1_ready")
        s_x2 = sem("x2_ready")
        s_x3 = sem("x3_ready")
        s_x4 = sem("x4_ready")
        s_x5 = sem("x5_ready")
        s_x5T = sem("x5_turned")
        s_x5T_ready = sem("x5T_stored")
        s_var = [sem(f"variance_ready_in_{h}_half") for h in ("first", "second")]
        s_rstd = [sem(f"rstd_ready_in_{h}_half") for h in ("first", "second")]
        s_chain = sem("vector_chain")
        s_cov = sem("covariance_summed")

        def v_blocks(p):
            base = v_exp[p][:]
            return bass.AP(tensor=base.tensor, offset=base.offset,
                           ap=[base.ap[0], [8 * 128, 2], [128 + DH, 8], [1, DH]])

        bank = lambda p, k: ps[:, 4 * p + k, :]
        banks = lambda p: ps[:, 4 * p:4 * p + 4, :]
        half_of = lambda k: int(k >= ROOTS_OF_HALF[0])
        root_count = lambda k, u: ROOTS_OF_HALF[half_of(k)] * u + k - ROOTS_OF_HALF[0] * half_of(k) + 1
        one = lambda tile, u: tile[:, bass.ds(u, 1), :]

        def weights_dma(q, names):
            for dst, src, s in names:
                q.dma_start(dst, src).then_inc(s, 16)

        def pbc(ap1d, n=128):
            return ap1d.partition_broadcast(n)

        row_sources = [
            (R_B1, 16, a["L0_ffn_b1"].rearrange("e (j h) -> (e j) h", h=128)),
            (R_GAMMA, 16, a["L1_ffn_bn_gamma"].rearrange("(r d) -> r d", d=128)),
            (R_BETA, 16, a["L1_ffn_bn_beta"].rearrange("(r d) -> r d", d=128)),
            (R_BQK0, 2, a["L0_attn_b_qkv"].rearrange("(r d) -> r d", d=128)[0:2]),
            (R_BQK1, 1, a["L1_attn_bq"].unsqueeze(0)),
            (R_BQK1 + 1, 1, a["L1_attn_bk"].unsqueeze(0)),
            (R_GRES, 1, a["L1_xattn_g_res"].unsqueeze(0)),
        ]
        N_ROWS_DMA = len(row_sources) + 2

        first = ctx.enter_context(ExitStack())
        block = first.enter_context(nc.Block())

        @block.sync
        def _(sp):
            for p in range(SLOTS):
                sp.dma_start(x_in[p][:], a["x"][p]).then_inc(s_x[p], 16)
                sp.dma_start(c_in[p][:], a["ctx_2048"][p]).then_inc(s_c[p], 16)
            weights_dma(sp, [
                (w_qkv[0][:], a["L0_attn_W_qkv"].rearrange("k (t n) -> k t n", t=3), s_w0),
                (w_proj[0][:], a["L0_attn_W_proj"], s_w0),
                (b_v[0][:], pbc(a["L0_attn_b_qkv"][2 * D:3 * D]), s_w0),
                (b_proj[0][:], pbc(a["L0_attn_b_proj"]), s_w0),
            ])
            for r, n, src in row_sources:
                sp.dma_start(rows[r:r + n, :], src).then_inc(s_rows, 16)
            for j in range(2):
                sp.dma_start(rows[R_NULLK:R_NULLK + 1, 64 * j:64 * j + 64],
                             a["L0_xattn_null_kv"][0:1, :]).then_inc(s_rows, 16)
            weights_dma(sp, [
                (xw_q[:], a["L0_xattn_Wq"], s_wx),
                (xw_kv[:], a["L0_xattn_Wkv"].rearrange("(c k) n -> k c n", k=128), s_wx),
                (xw_out[:], a["L0_xattn_Wout"].rearrange("(c k) n -> k c n", k=128), s_wx),
                (x_scale[:], pbc(a["L0_xattn_ln_scale"]), s_wx),
                (x_bias[:], pbc(a["L0_xattn_ln_bias"]), s_wx),
            ])
            for p in range(SLOTS):
                sp.wait_ge(s_vz, p + 1)
                for hp in range(2):
                    sp.dma_start(
                        v_z[p][M:M + 1].rearrange("k (c g) d -> k c g d", g=2)[:, :, hp, 64 * hp:64 * hp + 64],
                        a["L0_xattn_null_kv"][1:2, :].unsqueeze(1).broadcast_to([1, XC, 64]),
                    ).then_inc(s_nullv, 16)
            sp.wait_ge(s_rel_ext, 1)
            sp.dma_start(rel_dram[:, 0:255], wide_p[0][0:HEADS, 0:255]).then_inc(s_rel_out, 16)
            sp.wait_ge(s_rel_out, 16)
            sp.dma_start(wide_p[1][:].rearrange("i (h j) -> i h j", h=HEADS),
                         bass.AP(tensor=rel_dram.tensor, offset=0, ap=[[1, 128], [256, HEADS], [1, 128]])
                         ).then_inc(s_rel_in, 16)
            sp.wait_ge(s_plug, 1)
            sp.dma_start(plug_dram, wide_t[0][0:B, 0:128]).then_inc(s_plug_out, 16)
            sp.wait_ge(s_plug_out, 16)
            sp.dma_start(plug_T[:], plug_dram.partition_broadcast(M)).then_inc(s_plug_in, 16)

            weights_dma(sp, [
                (pk_wq[:], a["L1_ffn_w_q"].rearrange("k (r d) -> k r d", d=KD), s_pk),
                (pk_keys[:], a["L1_ffn_keys"].rearrange("(t h) k p d -> (h k) t (p d)", t=2), s_pk),
                (pk_down[:], a["L1_ffn_down_embed"].rearrange("(c k) n -> k c n", k=128), s_pk),
                (pk_up[:], a["L1_ffn_up_embed"].rearrange("(c k) n -> k c n", k=128), s_pk),
            ])
            with sp.Fori(0, ROUNDS - 1) as i:
                for p in range(SLOTS):
                    u = SLOTS * i + p
                    sp.wait_ge(A[0]["x_turned"], u + 1)
                    sp.wait_ge(A[0]["residual_ready"], u + 1)
                    sp.dma_start(x_in[p][:], a["x"][bass.ds(u + SLOTS, 1)].rearrange("o t d -> t (o d)")
                                 ).then_inc(s_x[p], 16)
                    sp.wait_ge(G["row_product"], u + 1)
                    sp.dma_start(c_in[p][:], a["ctx_2048"][bass.ds(u + SLOTS, 1)].rearrange("o t d -> t (o d)")
                                 ).then_inc(s_c[p], 16)

        @block.gpsimd
        def _(pool):
            n = [0]

            def link(ins):
                n[0] += 1
                ins.then_inc(s_pchain, 1)
                pool.wait_ge(s_pchain, n[0])

            link(nc.gpsimd.memset(ident[:], 1.0))
            link(nc.gpsimd.affine_select(out=ident[:], in_=ident[:], compare_op=ALU.is_equal, fill=0.0,
                                         base=0, pattern=[[-1, 128]], channel_multiplier=1))
            link(nc.gpsimd.memset(flip[:], 1.0))
            link(nc.gpsimd.affine_select(out=flip[:], in_=flip[:], compare_op=ALU.is_equal, fill=0.0,
                                         base=-127, pattern=[[1, 128]], channel_multiplier=1))
            link(nc.gpsimd.tensor_copy(ident16[:], ident[:]))
            link(nc.gpsimd.memset(causal16[:], 0.0))
            link(nc.gpsimd.affine_select(out=causal16[:], in_=causal16[:], compare_op=ALU.is_ge, fill=MASKED,
                                         base=0, pattern=[[0, 4], [-1, 128]], channel_multiplier=1))
            link(nc.gpsimd.memset(head_mask[:], float(DH) ** -0.5))
            link(nc.gpsimd.affine_select(out=head_mask[:], in_=head_mask[:], compare_op=ALU.is_ge, fill=0.0,
                                         base=0, pattern=[[-DH, HEADS]], channel_multiplier=1))
            link(nc.gpsimd.affine_select(out=head_mask[:], in_=head_mask[:], compare_op=ALU.is_ge, fill=0.0,
                                         base=DH - 1, pattern=[[DH, HEADS]], channel_multiplier=-1))
            link(nc.gpsimd.iota(iota8[:], pattern=[[1, E]], base=0, channel_multiplier=0,
                                allow_small_or_imprecise_dtypes=True))
            link(nc.gpsimd.iota(iota_col[:], pattern=[[1, 1]], base=0, channel_multiplier=1,
                                allow_small_or_imprecise_dtypes=True))
            link(nc.gpsimd.memset(neg_half[:], -0.5))
            nc.gpsimd.memset(ones_col[:], 1.0).then_inc(s_const, 1)

            pool.wait_ge(s_setup_done, 1)

            def root(k, u, p):
                pool.wait_ge(s_var[half_of(k)], root_count(k, u))
                c = RSTDS * p + k
                nc.gpsimd.tensor_tensor(out=rstd[:, c:c + 1], in0=veps[:, c:c + 1],
                                        in1=neg_half[:, 0:1], op=ALU.pow).then_inc(s_rstd[half_of(k)], 1)

            def first_half(u, p):
                pool.wait_ge(s_slot, u + 1)
                pool.wait_ge(s_x[p], 8 * (u - p) + 16)
                nc.gpsimd.tensor_tensor(out=z2[p][:], in0=x_in[p][:], in1=b_proj[0][:], op=ALU.add
                                        ).then_inc(A[0]["residual_ready"], 1)
                for _ in range(6):
                    yield
                root(ROOT_1, u, p)
                yield
                pool.wait_ge(s_x1, u + 1)
                nc.gpsimd.tensor_tensor(out=z2[p][:], in0=x_1[p][:], in1=x_bias[:], op=ALU.add
                                        ).then_inc(X["residual_ready"], 1)
                for _ in range(6):
                    yield
                root(ROOT_X, u, p)
                yield
                root(ROOT_2, u, p)
                yield

            def second_half(u, p):
                for _ in range(3):
                    yield
                root(ROOT_ROWS, u, p)
                pool.wait_ge(s_rstd[1], root_count(ROOT_ROWS, u))
                k = RSTDS * p + ROOT_ROWS
                nc.gpsimd.tensor_tensor(out=c_in[p][:, 0:128], in0=c_in[p][:, 0:128],
                                        in1=bcast(rstd[0:M, k:k + 1], [M, 128]), op=ALU.mult
                                        ).then_inc(G["rows_scaled"], 1)
                pool.wait_ge(G["rows_scaled"], u + 1)
                nc.gpsimd.tensor_tensor(out=c_in[p][:, 0:128], in0=c_in[p][:, 0:128],
                                        in1=g_init[0:M, :], op=ALU.mult).then_inc(G["rows_ready"], 1)
                root(ROOT_3, u, p)
                yield
                pool.wait_ge(s_x3, u + 1)
                nc.gpsimd.tensor_tensor(out=z2[p][:], in0=x_3[p][:], in1=b_proj[1][:], op=ALU.add
                                        ).then_inc(A[1]["residual_ready"], 1)
                for _ in range(5):
                    yield
                root(ROOT_4, u, p)
                yield
                pool.wait_ge(s_x4, u + 1)
                nc.gpsimd.tensor_copy(plug_now[p].unsqueeze(1), one(plug_T, u)).then_inc(G["plug_taken"], 1)
                nc.gpsimd.tensor_tensor(out=z2[p][:], in0=x_4[p][:], in1=b_in[:], op=ALU.add
                                        ).then_inc(G["residual_ready"], 1)
                root(ROOT_IN, u, p)
                yield
                root(ROOT_5, u, p)
                yield
                pool.wait_ge(s_x5, u + 1)
                nc.gpsimd.tensor_copy(one(x5, u), x_5[p][:, 0:128].unsqueeze(1)).then_inc(G["x5_kept"], 1)
                yield

            steps(pool, HALVES, first_half, second_half)

        @block.tensor
        def _(pe):
            pe.wait_ge(s_const, 1)
            pe.wait_ge(s_rows, 16 * N_ROWS_DMA)
            nc.tensor.transpose(ps[:, 0, 0:NROWS], rows[:], ident[0:NROWS, 0:NROWS]).then_inc(s_rowsT, 1)
            pe.wait_ge(s_wp, 16 * 3)
            nc.tensor.transpose(ps[:, 1, 0:128], w_in[:], ident[:]).then_inc(s_winT, 1)
            pe.wait_ge(s_rel_in, 16)
            for c in range(4):
                mm = nc.tensor.matmul(ps[:, 4 + c, :], flip[:], wide_p[1][:, 512 * c:512 * c + 512],
                                      start=True, stop=True)
            mm.then_inc(s_rel_fl, 1)
            pe.wait_ge(s_w0, 16 * 4)
            pe.wait_ge(s_wx, 16 * 5)
            pe.wait_ge(s_we, 16 * 5)
            pe.wait_ge(s_w1, 16 * 6)
            pe.wait_ge(s_setup_done, 1)
            pe.wait_ge(s_nullv, 64)

            def turn(src, p, done):
                nc.tensor.transpose(bank(p, 0)[:, 0:128], src[:], ident[:]).then_inc(done, 1)

            def project_qkv(l, u, p):
                S = A[l]
                pe.wait_ge(S["xT_ready"], u + 1)
                nc.tensor.matmul(bank(p, 3)[:, 128:256], w_qkv[l][:, 1, :], x_T[p][:], start=True, stop=True)
                nc.tensor.matmul(bank(p, 3)[:, 0:128], w_qkv[l][:, 0, :], x_T[p][:], start=True, stop=True)
                nc.tensor.matmul(bank(p, 3)[:, 256:384], x_T[p][:], w_qkv[l][:, 2, :], start=True,
                                 stop=True).then_inc(S["qkv_ready"], 1)

            def scores(l, u, p):
                S = A[l]
                q = wide_a[p][:].rearrange("d (h t) -> d h t", h=HEADS)
                for c in range(NCH):
                    if l == 0 and c == 1:
                        pe.wait_ge(X["v_copied"], u + 1)
                    if c == NCH - 1:
                        pe.wait_ge(S["v_ready"], u + 1)
                    pe.wait_ge(S["masked_q_ready"], NCH * u + c + 1)
                    if l == 0:
                        nc.tensor.matmul(bank(p, c), ident16[:], causal16[:].rearrange("k h j -> k (h j)"),
                                         start=True, stop=False, skip_group_check=True)
                    for k in range(4):
                        mm = nc.tensor.matmul(bank(p, c)[:, 128 * k:128 * k + 128], q[:, 4 * c + k, :], k_T[p][:],
                                              start=(l == 1), stop=True, skip_group_check=True)
                    mm.then_inc(S["scores_ready"], 1)

            def turn_probs(l, u, p):
                S = A[l]
                pr = wide_p[p][:].rearrange("q (h k) -> q h k", h=HEADS)
                for c in range(NCH):
                    pe.wait_ge(S["probs_ready"], NCH * u + c + 1)
                    for k in range(4):
                        mm = nc.tensor.transpose(bank(p, c)[:, 128 * k:128 * k + 128], pr[:, 4 * c + k, :], ident[:])
                    mm.then_inc(S["probs_turned"], 1)

            def mix(l, u, p):
                S = A[l]
                pt = wide_t[p][:].rearrange("k (h q) -> k h q", h=HEADS)
                for c in range(NCH):
                    pe.wait_ge(S["probsT_ready"], NCH * u + c + 1)
                    for h in range(4 * c, 4 * c + 4):
                        mm = nc.tensor.matmul(bank(p, 0)[:, 128 * (h // 8):128 * (h // 8) + 128], v_exp[p][:, h, :],
                                              pt[:, h, :], start=(h % 8 == 0), stop=(h % 8 == 7),
                                              skip_group_check=True)
                mm.then_inc(S["mixed"], 1)

            def project(l, u, p):
                S = A[l]
                pe.wait_ge(S["mixed_ready"], u + 1)
                nc.tensor.matmul(bank(p, 1)[:, 0:128], att_T[p][:], w_proj[l][:], start=True,
                                 stop=True).then_inc(S["projected"], 1)

            def first_half(u, p):
                pe.wait_ge(s_slot, u + 1)
                pe.wait_ge(s_x[p], 8 * (u - p) + 16)
                turn(x_in[p], p, A[0]["x_turned"])
                pe.wait_ge(s_c[p], 8 * (u - p) + 16)
                for c in range(2):
                    mm = nc.tensor.transpose(bank(p, 3)[:, 128 * c:128 * c + M], c_in[p][:, 128 * c:128 * c + 128],
                                             ident[0:M, 0:M])
                mm.then_inc(X["c_turned"], 1)
                yield
                pe.wait_ge(X["cT_ready"], u + 1)
                project_qkv(0, u, p)
                for c in range(XC):
                    for k in range(2):
                        mm = nc.tensor.matmul(bank(p, 1 + c // 4)[:, 128 * (c % 4):128 * (c % 4) + M],
                                              xw_kv[:, k, 128 * c:128 * c + 128], c_T[p][:, k, :],
                                              start=(k == 0), stop=(k == 1))
                mm.then_inc(X["k_ready"], 1)
                yield
                pe.wait_ge(X["k_copied"], u + 1)
                for n in range(2):
                    for k in range(2):
                        mm = nc.tensor.matmul(bank(p, 1 + n)[0:M, :], c_T[p][:, k, :],
                                              xw_kv[:, k, 1024 + 512 * n:1536 + 512 * n],
                                              start=(k == 0), stop=(k == 1))
                mm.then_inc(X["v_ready"], 1)
                yield
                scores(0, u, p)
                yield
                turn_probs(0, u, p)
                yield
                mix(0, u, p)
                yield
                project(0, u, p)
                yield
                pe.wait_ge(s_x1, u + 1)
                turn(x_1[p], p, X["x_turned"])
                yield
                pe.wait_ge(X["xT_ready"], u + 1)
                for c in range(XC):
                    mm = nc.tensor.matmul(bank(p, c // 4)[:, 128 * (c % 4):128 * (c % 4) + 128],
                                          xw_q[:, 128 * c:128 * c + 128], x_T[p][:], start=True, stop=True)
                mm.then_inc(X["q_ready"], 1)
                yield
                pe.wait_ge(X["q_copied"], u + 1)
                for c in range(XC):
                    mm = nc.tensor.matmul(bank(p, c // 2)[:, 2 * MK * (c % 2):2 * MK * (c % 2 + 1)],
                                          wide_a[p][:, 128 * c:128 * c + 128],
                                          k_exp[p][:, c].rearrange("d g k -> d (g k)"), start=True, stop=True)
                    if c % 4 == 3:
                        mm.then_inc(X["scores_ready"], 1)
                yield
                yield
                pr = wide_p[p][:, 0:XH * MK].rearrange("q (h k) -> q h k", h=XH)
                for n in range(2):
                    pe.wait_ge(X["normalized"], 2 * u + n + 1)
                    for h in range(8 * n, 8 * n + 8):
                        mm = nc.tensor.transpose(bank(p, h // 4)[0:MK, 128 * (h % 4):128 * (h % 4) + 128],
                                                 pr[:, h, :], ident[:])
                    mm.then_inc(X["probs_turned"], 1)
                yield
                pt = wide_t[p][:].rearrange("k (h q) -> k h q", h=XH)
                for n in range(2):
                    pe.wait_ge(X["probsT_ready"], 2 * u + n + 1)
                    for c in range(4 * n, 4 * n + 4):
                        for g in range(2):
                            mm = nc.tensor.matmul(bank(p, c // 4)[:, 128 * (c % 4):128 * (c % 4) + 128],
                                                  v_z[p][:, 2 * c + g, :], pt[0:MK, 2 * c + g, :],
                                                  start=(g == 0), stop=(g == 1))
                    mm.then_inc(X["mixed"], 1)
                yield
                for n in range(2):
                    pe.wait_ge(X["mixed_copied"], 2 * u + n + 1)
                    for c in range(4 * n, 4 * n + 4):
                        mm = nc.tensor.matmul(bank(p, 2)[:, 0:128], wide_a[p][:, 128 * c:128 * c + 128],
                                              xw_out[:, c, :], start=(c == 0), stop=(c == XC - 1))
                mm.then_inc(X["projected"], 1)
                yield
                yield

            def second_half(u, p):
                pe.wait_ge(s_x2, u + 1)
                turn(x_2[p], p, F["x_turned"])
                yield
                pe.wait_ge(F["xT_ready"], u + 1)
                nc.tensor.matmul(bank(p, 3)[:, 0:E], x_T[p][:], w_r[:], start=True,
                                 stop=True).then_inc(F["logits_ready"], 1)
                for k in range(E * HC):
                    if k == 12:
                        pe.wait_ge(F["max_ready"], u + 1)
                    mm = nc.tensor.matmul(bank(p, k // 4)[:, 128 * (k % 4):128 * (k % 4) + 128],
                                          w_1[:, k // HC, 128 * (k % HC):128 * (k % HC) + 128], x_T[p][:],
                                          start=True, stop=True)
                    if k % 4 == 3:
                        mm.then_inc(F["hidden_ready"], 1)
                yield
                for e in range(E):
                    if e % 2 == 0:
                        pe.wait_ge(F["relu_odd" if e // 2 % 2 else "relu_even"], 2 * u + e // 4 + 1)
                    for j in range(HC):
                        mm = nc.tensor.matmul(bank(p, e // 4)[:, 128 * (e % 4):128 * (e % 4) + 128],
                                              wide_a[p][:, 128 * (HC * e + j):128 * (HC * e + j) + 128],
                                              w_2[:, e, j, :], start=(j == 0), stop=(j == HC - 1))
                    if e % 4 == 3:
                        mm.then_inc(F["outputs_ready"], 1)
                pe.wait_ge(F["gate_ready"], u + 1)
                nc.tensor.transpose(bank(p, 2)[0:E, 0:128], w_one[p][:], ident[:]).then_inc(F["gate_turned"], 1)
                yield
                pe.wait_ge(F["gateT_ready"], u + 1)
                nc.tensor.matmul(bank(p, 3)[:, 0:128], w_oneT[p][:], b_2[:], start=True,
                                 stop=True).then_inc(F["weighted"], 1)
                yield
                pe.wait_ge(s_x3, u + 1)
                turn(x_3[p], p, A[1]["x_turned"])
                yield
                project_qkv(1, u, p)
                yield
                scores(1, u, p)
                yield
                turn_probs(1, u, p)
                yield
                mix(1, u, p)
                yield
                project(1, u, p)
                yield
                pe.wait_ge(s_x4, u + 1)
                turn(x_4[p], p, G["x_turned"])
                pe.wait_ge(G["rows_ready"], u + 1)
                pe.wait_ge(G["plug_taken"], u + 1)
                nc.tensor.matmul(bank(p, 2)[:, 0:128], plug_now[p], c_in[p][:, 0:128], start=True,
                                 stop=True).then_inc(G["row_product"], 1)
                yield
                pe.wait_ge(G["xT_ready"], u + 1)
                nc.tensor.matmul(bank(p, 1)[:, 0:128], x_T[p][:], w_inT[:], start=True,
                                 stop=True).then_inc(G["input_product"], 1)
                yield
                pe.wait_ge(s_x5, u + 1)
                turn(x_5[p][:, 0:128], p, s_x5T)
                nc.tensor.matmul(bank(p, 3)[:, 0:129], x_5[p][:, 0:128], x_5[p][:], start=True,
                                 stop=True).then_inc(G["summed"], 1)
                yield

            steps(pe, HALVES, first_half, second_half)

        @block.scalar
        def _(act):
            weights_dma(act, [
                (w_in[:], a["L1_xattn_W_in"], s_wp),
                (b_in[:], pbc(a["L1_xattn_b_in"]), s_wp),
                (g_init[:], pbc(a["L1_xattn_g_init"][0:128]), s_wp),
                (w_r[:], a["L0_ffn_Wr"], s_we),
                (b_r[:], pbc(a["L0_ffn_br"]), s_we),
                (w_1[:], a["L0_ffn_W1"].rearrange("e k n -> k e n"), s_we),
                (w_2[:], a["L0_ffn_W2"].rearrange("e (j k) n -> k e j n", k=128), s_we),
                (b_2[:], a["L0_ffn_b2"], s_we),
                (w_qkv[1][:, 0, :], a["L1_attn_Wq"], s_w1),
                (w_qkv[1][:, 1, :], a["L1_attn_Wk"], s_w1),
                (w_qkv[1][:, 2, :], a["L1_attn_Wv"], s_w1),
                (w_proj[1][:], a["L1_attn_Wo"], s_w1),
                (b_v[1][:], pbc(a["L1_attn_bv"]), s_w1),
                (b_proj[1][:], pbc(a["L1_attn_bo"]), s_w1),
                (wide_p[0][0:HEADS, 128:255], a["rel_rev"], s_rel),
                (plen_i, a["mask_BxS2_if0"], s_plen),
            ])
            act.wait_ge(s_ev, 1)
            nc.scalar.activation(plug_T[:], plug_T[:], ACT.Exp, scale=-DT).then_inc(s_ev, 1)

            def copy_turned(u, p, ready, done):
                act.wait_ge(ready, u + 1)
                nc.scalar.copy(x_T[p][:], bank(p, 0)[:, 0:128]).then_inc(done, 1)

            def exponentials(l, u, p):
                for c in range(NCH):
                    act.wait_ge(A[l]["shifted"], NCH * u + c + 1)
                    nc.scalar.activation(wide_p[p][:, 512 * c:512 * c + 512], wide_p[p][:, 512 * c:512 * c + 512],
                                         ACT.Exp).then_inc(A[l]["probs_ready"], 1)

            def copy_probs(l, u, p):
                for c in range(NCH):
                    act.wait_ge(A[l]["probs_turned"], NCH * u + c + 1)
                    nc.scalar.copy(wide_t[p][:, 512 * c:512 * c + 512], bank(p, c)).then_inc(A[l]["probsT_ready"], 1)

            def first_half(u, p):
                copy_turned(u, p, A[0]["x_turned"], A[0]["xT_ready"])
                act.wait_ge(X["c_turned"], u + 1)
                nc.scalar.copy(c_T[p][:], bank(p, 3)[:, 0:256].rearrange("d (c k) -> d c k", c=2)[:, :, 0:M]
                               ).then_inc(X["cT_ready"], 1)
                yield
                act.wait_ge(X["k_ready"], u + 1)
                for hp in range(2):
                    r = slice(64 * hp, 64 * hp + 64)
                    ins = nc.scalar.copy(k_exp[p][r, :, hp, 0:M],
                                         ps[r, 4 * p + 1:4 * p + 3, :].rearrange("d b (c k) -> d (b c) k", k=128)
                                         [:, :, 0:M])
                ins.then_inc(X["k_copied"], 1)
                yield
                act.wait_ge(X["v_ready"], u + 1)
                for hp in range(2):
                    ins = nc.scalar.copy(
                        v_z[p][0:M].rearrange("k (c g) d -> k c g d", g=2)[:, :, hp, 64 * hp:64 * hp + 64],
                        ps[0:M, 4 * p + 1:4 * p + 3, :].rearrange("k b (c g d) -> k (b c) g d", g=2, d=64)[:, :, hp, :])
                ins.then_inc(X["v_copied"], 1)
                yield
                exponentials(0, u, p)
                yield
                copy_probs(0, u, p)
                yield
                yield
                yield
                copy_turned(u, p, X["x_turned"], X["xT_ready"])
                yield
                act.wait_ge(X["q_ready"], u + 1)
                nc.scalar.copy(wide_a[p][:, 0:1024].rearrange("d (b n) -> d b n", b=2),
                               ps[:, 4 * p:4 * p + 2, :]).then_inc(X["q_copied"], 1)
                yield
                half = XH * MK // 2
                for n in range(2):
                    act.wait_ge(X["shifted"], 2 * u + n + 1)
                    nc.scalar.activation(wide_p[p][:, half * n:half * n + half], wide_p[p][:, half * n:half * n + half],
                                         ACT.Exp, scale=float(XDH) ** -0.5).then_inc(X["probs_ready"], 1)
                yield
                yield
                for n in range(2):
                    act.wait_ge(X["probs_turned"], 2 * u + n + 1)
                    nc.scalar.copy(wide_t[p][0:MK, 1024 * n:1024 * n + 1024].rearrange("k (b n) -> k b n", b=2),
                                   ps[0:MK, 4 * p + 2 * n:4 * p + 2 * n + 2, :]).then_inc(X["probsT_ready"], 1)
                yield
                for n in range(2):
                    act.wait_ge(X["mixed"], 2 * u + n + 1)
                    nc.scalar.copy(wide_a[p][:, 512 * n:512 * n + 512], bank(p, n)).then_inc(X["mixed_copied"], 1)
                yield
                yield
                yield

            def second_half(u, p):
                copy_turned(u, p, F["x_turned"], F["xT_ready"])
                yield
                act.wait_ge(F["max_ready"], u + 1)
                nc.scalar.activation(logit_e[p][:], logit[p][:], ACT.Exp, bias=sm[p][:, 0:1],
                                     accum_out=sm[p][:, 1:2]).then_inc(F["exp_ready"], 1)
                for c in range(0, NCH, 2):
                    act.wait_ge(F["hidden_ready"], NCH * u + c + 1)
                    for k in range(4 * c, 4 * c + 4):
                        ins = nc.scalar.activation(wide_a[p][:, 128 * k:128 * k + 128],
                                                   bank(p, c)[:, 128 * (k % 4):128 * (k % 4) + 128], ACT.Relu,
                                                   bias=cols[:, R_B1 + k:R_B1 + k + 1])
                    ins.then_inc(F["relu_even"], 1)
                yield
                act.wait_ge(F["gate_turned"], u + 1)
                nc.scalar.copy(w_oneT[p][:], bank(p, 2)[0:E, 0:128]).then_inc(F["gateT_ready"], 1)
                nc.scalar.activation(squares[p][0:M, :], c_in[p][:], ACT.Square,
                                     accum_out=sm[p][0:M, 5:6]).then_inc(G["row_squares"], 1)
                yield
                yield
                copy_turned(u, p, A[1]["x_turned"], A[1]["xT_ready"])
                yield
                yield
                exponentials(1, u, p)
                yield
                copy_probs(1, u, p)
                yield
                yield
                yield
                act.wait_ge(s_x4, u + 1)
                nc.scalar.activation(squares[p][:, 0:128], x_4[p][:], ACT.Square,
                                     accum_out=sm[p][:, 4:5]).then_inc(G["x_squares"], 1)
                copy_turned(u, p, G["x_turned"], G["xT_ready"])
                yield
                yield
                act.wait_ge(s_x5T, u + 1)
                nc.scalar.copy(one(x5T, u), bank(p, 0)[:, 0:128].unsqueeze(1)).then_inc(s_x5T_ready, 1)
                yield

            steps(act, HALVES, first_half, second_half)

        @block.vector
        def _(dve):
            V = nc.vector
            n = [0]

            def link(ins):
                n[0] += 1
                ins.then_inc(s_setup, 1)
                dve.wait_ge(s_setup, n[0])

            for p in range(SLOTS):
                V.memset(v_z[p][:], 0.0).then_inc(s_vz, 1)
                link(V.memset(k_exp[p][:], 0.0))
                link(V.memset(v_exp[p][:], 0.0))
                for h in range(HEADS):
                    ins = V.memset(v_exp[p][:, h, 64 + DH * (h % 8):64 + DH * (h % 8) + DH], 1.0)
                link(ins)
                link(V.memset(x_5[p][:], 1.0))
            link(V.memset(cov[:], 0.0))
            link(V.memset(veps[:], 1.0))
            dve.wait_ge(s_const, 1)
            dve.wait_ge(s_rel, 16)
            link(V.tensor_copy(wide_p[0][0:HEADS, 0:128],
                               bcast(wide_p[0][0:HEADS, 128:129], [HEADS, 128])))
            V.tensor_copy(wide_t[1][0:HEADS, 0:8], wide_p[0][0:HEADS, 0:8]).then_inc(s_rel_ext, 1)
            dve.wait_ge(s_plen, 16)
            plen = wide_t[0][0:B, 256:256 + M]
            edge = wide_t[0][0:B, 384:384 + M]
            wrap = wide_t[0][0:B, 512:512 + M]
            hit = wide_t[0][0:B, 640:768]
            zero = wide_t[0][0:B, 768:1024]
            tok = wide_t[0][0:B, 1024:1152]
            link(V.memset(zero, 0.0))
            link(V.tensor_copy(plen, plen_i))
            link(V.tensor_tensor_scan(edge, plen, zero[:, 0:M], 0.0, ALU.add, ALU.add))
            link(V.tensor_scalar(edge, edge, 1.0, None, ALU.subtract))
            link(V.tensor_scalar(wrap, edge, 0.0, float(T), ALU.is_lt, ALU.mult))
            link(V.tensor_tensor(edge, edge, wrap, ALU.add))
            link(V.memset(tok, 1.0))
            link(V.tensor_tensor_scan(hit, tok, zero[:, 0:128], -1.0, ALU.add, ALU.add))
            link(V.tensor_copy(tok, hit))
            CH = 16
            for c in range(T // CH):
                cmp = wide_a[0][0:B, 0:CH * M].rearrange("b (t k) -> b t k", t=CH)
                link(V.tensor_tensor(cmp, bcast(edge.unsqueeze(1), [B, CH, M]),
                                     bcast(tok[:, CH * c:CH * c + CH].unsqueeze(2), [B, CH, M]), ALU.is_equal))
                link(V.tensor_reduce(hit[:, CH * c:CH * c + CH], cmp, AX.X, ALU.max))
            link(V.tensor_tensor_scan(tok, hit, zero[:, 0:128], -1.0, ALU.add, ALU.add))
            V.tensor_scalar(wide_t[0][0:B, 0:128], tok, 0.0, float(M - 1), ALU.max, ALU.min).then_inc(s_plug, 1)
            dve.wait_ge(s_plug_in, 16)
            flat = plug_T[:]
            sign = wide_a[1][0:M, :].rearrange("k (b t) -> k b t", b=B)
            link(V.tensor_scalar(flat, flat, iota_col[0:M, 0:1], None, ALU.subtract))
            link(V.tensor_scalar(sign, flat, 0.0, None, ALU.is_ge))
            V.tensor_scalar(flat, flat, 0.0, None, ALU.max).then_inc(s_ev, 1)
            dve.wait_ge(s_ev, 2)
            link(V.tensor_tensor(flat, flat, sign, ALU.mult))
            dve.wait_ge(s_rowsT, 1)
            link(V.tensor_copy(cols[:], ps[:, 0, 0:NROWS]))
            dve.wait_ge(s_winT, 1)
            link(V.tensor_scalar(w_inT[:], ps[:, 1, 0:128], cols[:, R_GRES:R_GRES + 1], None, ALU.mult))
            for p in range(SLOTS):
                for hp in range(2):
                    r = slice(64 * hp, 64 * hp + 64)
                    link(V.tensor_copy(k_exp[p][r, :, hp, M:MK],
                                       bcast(cols[r, R_NULLK:R_NULLK + 1].unsqueeze(1), [64, XC, 1])))
            dve.wait_ge(s_rel_fl, 1)
            link(V.tensor_copy(rel_bias[:].rearrange("i (b h) j -> i b (h j)", b=4), ps[:, 4:8, :]))
            dve.wait_ge(s_w0, 16 * 4)
            dve.wait_ge(s_wx, 16 * 5)
            dve.wait_ge(s_we, 16 * 5)
            dve.wait_ge(s_w1, 16 * 6)
            dve.wait_ge(s_wp, 16 * 3)
            dve.wait_ge(s_nullv, 64)
            link(V.tensor_scalar(g_init[:], g_init[:], BCOEF, None, ALU.mult))
            V.memset(z[0][:, 0:1], 0.0).then_inc(s_setup_done, 1)
            for p in range(SLOTS):
                V.memset(z2[p][:, 0:1], 0.0).then_inc(s_slot, 1)

            state = {}
            expected = [0, FIRST_LINKS] + 3 * [FIRST_LINKS + SECOND_LINKS]

            def settle():
                V.memset(spare[:], 0.0)

            def mark(ins):
                state["links"] += 1
                ins.then_inc(s_chain, 1)
                return state["base"] + state["links"]

            def chain(ins):
                count = mark(ins)
                dve.wait_ge(s_chain, count)

            def begin(step):
                assert state.get("links", expected[0]) == expected.pop(0), state["links"]
                state.update(base=0 if isinstance(step, int) and step == 0
                             else (FIRST_LINKS + SECOND_LINKS) * (step - 1) + FIRST_LINKS, links=0)

            def norm_begin(k, p, zp, eps):
                c = RSTDS * p + k
                chain(V.bn_stats(stats[:, c, :], zp))
                settle()
                chain(V.bn_aggr(mv[:, c, :], stats[:, c, :]))
                V.tensor_scalar(veps[:, c:c + 1], mv[:, c, 1:2], eps, None, ALU.add).then_inc(s_var[half_of(k)], 1)

            def norm_end(k, u, p, outp, zp):
                c = RSTDS * p + k
                dve.wait_ge(s_rstd[half_of(k)], root_count(k, u))
                return V.tensor_scalar(outp, zp, mv[:, c, 0:1], rstd[:, c:c + 1], ALU.subtract, ALU.mult)

            def take_qkv(l, u, p):
                S = A[l]
                bq = R_BQK0 if l == 0 else R_BQK1
                dve.wait_ge(S["qkv_ready"], u + 1)
                V.tensor_scalar(k_T[p][:], bank(p, 3)[:, 128:256], cols[:, bq + 1:bq + 2], None, ALU.add)
                for c in range(NCH):
                    V.scalar_tensor_tensor(
                        out=wide_a[p][:, 512 * c:512 * c + 512].rearrange("d (h t) -> d h t", h=4),
                        in0=bcast(bank(p, 3)[:, 0:128].unsqueeze(1), [128, 4, 128]),
                        scalar=cols[:, bq:bq + 1],
                        in1=bcast(head_mask[:, 4 * c:4 * c + 4].unsqueeze(2), [128, 4, 128]),
                        op0=ALU.add, op1=ALU.mult).then_inc(S["masked_q_ready"], 1)
                    if c == 0:
                        V.tensor_tensor(
                            v_blocks(p),
                            bank(p, 3)[:, 256:384].rearrange("k (g h d) -> k g h d", g=2, h=8),
                            b_v[l][:].rearrange("k (g h d) -> k g h d", g=2, h=8), ALU.add).then_inc(S["v_ready"], 1)

            def shift(l, u, p):
                S = A[l]

                def subtract(c, sc, count):
                    dve.wait_ge(s_chain, count)
                    V.tensor_tensor(wide_p[p][:, 512 * c:512 * c + 512].rearrange("q (h k) -> q h k", h=4), sc,
                                    bcast(mx[p][:, 4 * c:4 * c + 4].unsqueeze(2), [128, 4, 128]),
                                    ALU.subtract).then_inc(S["shifted"], 1)

                late = None
                for c in range(NCH):
                    dve.wait_ge(S["scores_ready"], NCH * u + c + 1)
                    sc = bank(p, c).rearrange("q (h k) -> q h k", h=4)
                    if l == 1:
                        pr = wide_p[p][:, 512 * c:512 * c + 512].rearrange("q (h k) -> q h k", h=4)
                        chain(V.tensor_tensor(pr, sc, rel_bias[:, 4 * c:4 * c + 4, :], ALU.add))
                        sc = pr
                    count = mark(V.tensor_reduce(mx[p][:, 4 * c:4 * c + 4], sc, AX.X, ALU.max))
                    if late:
                        subtract(*late)
                    late = (c, sc, count)
                subtract(*late)

            def divide(l, u, p):
                S = A[l]
                dve.wait_ge(S["mixed"], u + 1)
                chain(V.reciprocal(r_z[p][:], ps[64:128, 4 * p, 0:256].rearrange("d (g q) -> d g q", g=2)))
                for g in range(2):
                    ins = V.tensor_tensor(att_T[p][64 * g:64 * g + 64, :],
                                          ps[0:64, 4 * p, 128 * g:128 * g + 128], r_z[p][:, g, :], ALU.mult)
                ins.then_inc(S["mixed_ready"], 1)

            def add_residual(l, u, p, k):
                dve.wait_ge(A[l]["residual_ready"], u + 1)
                dve.wait_ge(A[l]["projected"], u + 1)
                chain(V.tensor_tensor(z[p][:], bank(p, 1)[:, 0:128], z2[p][:], ALU.add))
                norm_begin(k, p, z[p][:], LN_EPS)

            def first_half(u, p):
                yield
                dve.wait_ge(s_slot, u + 1)
                take_qkv(0, u, p)
                yield
                yield
                shift(0, u, p)
                yield
                yield
                divide(0, u, p)
                yield
                add_residual(0, u, p, ROOT_1)
                yield
                norm_end(ROOT_1, u, p, x_1[p][:], z[p][:]).then_inc(s_x1, 1)
                yield
                yield
                for n in range(2):
                    dve.wait_ge(X["scores_ready"], 2 * u + n + 1)
                    sc = ps[:, 4 * p + 2 * n:4 * p + 2 * n + 2, 0:4 * MK].rearrange("q b (h k) -> q b h k", h=4)
                    pr = wide_p[p][:, 8 * MK * n:8 * MK * (n + 1)].rearrange("q (b h k) -> q b h k", b=2, h=4)
                    m = mx[p][:, 8 * n:8 * n + 8].rearrange("q (b h) -> q b h", b=2)
                    chain(V.tensor_reduce(m, sc, AX.X, ALU.max))
                    V.tensor_tensor(pr, sc, bcast(m.unsqueeze(3), [128, 2, 4, MK]), ALU.subtract
                                    ).then_inc(X["shifted"], 1)
                yield
                for n in range(2):
                    dve.wait_ge(X["probs_ready"], 2 * u + n + 1)
                    pr = wide_p[p][:, 8 * MK * n:8 * MK * (n + 1)].rearrange("q (h k) -> q h k", h=8)
                    chain(V.tensor_reduce(sums[p][:, 8 * n:8 * n + 8], pr, AX.X, ALU.add))
                    chain(V.reciprocal(rsum[p][:, 8 * n:8 * n + 8], sums[p][:, 8 * n:8 * n + 8]))
                    V.tensor_tensor(pr, pr, bcast(rsum[p][:, 8 * n:8 * n + 8].unsqueeze(2), [128, 8, MK]),
                                    ALU.mult).then_inc(X["normalized"], 1)
                yield
                yield
                yield
                dve.wait_ge(X["projected"], u + 1)
                chain(V.tensor_copy(z[p][:], bank(p, 2)[:, 0:128]))
                norm_begin(ROOT_X, p, z[p][:], XLN_EPS)
                yield
                chain(norm_end(ROOT_X, u, p, z[p][:], z[p][:]))
                chain(V.tensor_tensor(z[p][:], z[p][:], x_scale[:], ALU.mult))
                dve.wait_ge(X["residual_ready"], u + 1)
                chain(V.tensor_tensor(z[p][:], z[p][:], z2[p][:], ALU.add))
                norm_begin(ROOT_2, p, z[p][:], LN_EPS)
                yield

            def second_half(u, p):
                norm_end(ROOT_2, u, p, x_2[p][:], z[p][:]).then_inc(s_x2, 1)
                yield
                dve.wait_ge(F["logits_ready"], u + 1)
                chain(V.tensor_tensor(logit[p][:], bank(p, 3)[:, 0:E], b_r[:], ALU.add))
                settle()
                chain(V.max(top8[p][:], logit[p][:]))
                settle()
                V.max_index(top8i[p][:], top8[p][:], logit[p][:])
                V.tensor_scalar(sm[p][:, 0:1], top8[p][:, 0:1], -1.0, None, ALU.mult).then_inc(F["max_ready"], 1)
                for c in range(1, NCH, 2):
                    dve.wait_ge(F["hidden_ready"], NCH * u + c + 1)
                    for k in range(4 * c, 4 * c + 4):
                        ins = V.tensor_scalar(wide_a[p][:, 128 * k:128 * k + 128],
                                              bank(p, c)[:, 128 * (k % 4):128 * (k % 4) + 128],
                                              cols[:, R_B1 + k:R_B1 + k + 1], 0.0, ALU.add, ALU.max)
                    ins.then_inc(F["relu_odd"], 1)
                dve.wait_ge(F["exp_ready"], u + 1)
                V.tensor_copy(sm[p][:, 2:3], top8i[p][:, 0:1])
                chain(V.reciprocal(sm[p][:, 3:4], sm[p][:, 1:2]))
                V.tensor_scalar(w_one[p][:], iota8[:], sm[p][:, 2:3], sm[p][:, 3:4], ALU.is_equal,
                                ALU.mult).then_inc(F["gate_ready"], 1)
                yield
                dve.wait_ge(F["gate_ready"], u + 1)
                for n in range(2):
                    dve.wait_ge(F["outputs_ready"], 2 * u + n + 1)
                    count = mark(V.tensor_tensor(
                        wide_p[p][:, 512 * n:512 * n + 512].rearrange("t (e d) -> t e d", e=4),
                        bank(p, n).rearrange("t (e d) -> t e d", e=4),
                        bcast(w_one[p][:, 4 * n:4 * n + 4].unsqueeze(2), [128, 4, 128]), ALU.mult))
                dve.wait_ge(s_chain, count)
                chain(V.tensor_reduce(z[p][:], wide_p[p][:, 0:1024].rearrange("t (e d) -> t d e", e=E), AX.X, ALU.add))
                chain(V.tensor_tensor(z[p][:], z[p][:], x_2[p][:], ALU.add))
                yield
                dve.wait_ge(G["row_squares"], u + 1)
                k = RSTDS * p + ROOT_ROWS
                V.tensor_scalar(veps[0:M, k:k + 1], sm[p][0:M, 5:6], 1.0 / CTX, RMS_EPS, ALU.mult,
                                ALU.add).then_inc(s_var[1], 1)
                dve.wait_ge(F["weighted"], u + 1)
                chain(V.tensor_tensor(z[p][:], bank(p, 3)[:, 0:128], z[p][:], ALU.add))
                norm_begin(ROOT_3, p, z[p][:], LN_EPS)
                yield
                norm_end(ROOT_3, u, p, x_3[p][:], z[p][:]).then_inc(s_x3, 1)
                yield
                take_qkv(1, u, p)
                yield
                shift(1, u, p)
                yield
                yield
                divide(1, u, p)
                yield
                add_residual(1, u, p, ROOT_4)
                yield
                norm_end(ROOT_4, u, p, x_4[p][:], z[p][:]).then_inc(s_x4, 1)
                dve.wait_ge(G["x_squares"], u + 1)
                k = RSTDS * p + ROOT_IN
                V.tensor_scalar(veps[:, k:k + 1], sm[p][:, 4:5], 1.0 / D, RMS_EPS, ALU.mult,
                                ALU.add).then_inc(s_var[1], 1)
                dve.wait_ge(G["residual_ready"], u + 1)
                dve.wait_ge(G["row_product"], u + 1)
                chain(V.tensor_tensor(z[p][:], bank(p, 2)[:, 0:128], z2[p][:], ALU.add))
                yield
                dve.wait_ge(G["input_product"], u + 1)
                dve.wait_ge(s_rstd[1], root_count(ROOT_IN, u))
                chain(V.scalar_tensor_tensor(out=z[p][:], in0=bank(p, 1)[:, 0:128], scalar=rstd[:, k:k + 1],
                                             in1=z[p][:], op0=ALU.mult, op1=ALU.add))
                norm_begin(ROOT_5, p, z[p][:], LN_EPS)
                yield
                norm_end(ROOT_5, u, p, x_5[p][:, 0:128], z[p][:]).then_inc(s_x5, 1)
                dve.wait_ge(G["summed"], u + 1)
                chain(V.tensor_tensor(cov[:], cov[:], bank(p, 3)[:, 0:129], ALU.add))
                dve.wait_ge(s_x5T_ready, u + 1)
                dve.wait_ge(G["x5_kept"], u + 1)
                V.memset(sums[p][:, 0:1], 0.0).then_inc(s_slot, 1)
                yield

            steps(dve, HALVES, first_half, second_half, begin)

        first.close()
        loop1.close()
        product_keys(nc, ctx, ps, out, dict(
            ident=ident, ones=ones_col, neg_half=neg_half, cols=cols, spare=spare, x5=x5, x5T=x5T, cov=cov,
            w_q=pk_wq, keys=pk_keys, down=pk_down, up=pk_up, loaded=s_pk))


def product_keys(nc, ctx, ps, out, c):
    ident, ones, cols, x5, x5T, cov = c["ident"], c["ones"], c["cols"], c["x5"], c["x5T"], c["cov"]
    spare = c["spare"]
    N = B * T
    SEG = NK + TOP
    BUFS = 4
    MIX, GELU, SIM, OUT = 0, 4, 6, 7

    def sb(name, shape, dt=F32):
        return ctx.enter_context(nc.sbuf_tensor(name, shape, dt))

    def pair(name, shape, dt=F32):
        return [sb(f"{name}{p}", shape, dt) for p in range(SLOTS)]

    def sem(name):
        return ctx.enter_context(nc.semaphore(name))

    wqT = sb("wqT", [128, 2 * PH, 128])
    keysT = sb("keysT", [128, 2 * PH, NK])
    downT = sb("downT", [128, NE])
    covn = sb("covn", [128, 129])
    mean_row = sb("mean_row", [1, 128])
    wu = sb("wu", [128, 2 * PH, KD])
    fold = sb("fold", [128, 4, 2 * PH])
    means = sb("means", [128, 2 * PH])
    keys_s = sb("keys_s", [128, 2 * PH, NK])
    keys_b = sb("keys_b", [128, 2 * PH, NK])
    w_sim = sb("w_sim", [128, 512])
    b_sim = sb("b_sim", [128, 512])
    xs = pair("xs", [128, 128])
    act_T = pair("act_T", [128, NE])
    halves = pair("halves", [128, 2 * PH, SEG])
    cand = pair("cand", [128, PH, TOP * TOP])
    mxs = pair("mxs", [128, 2 * PH])
    best = pair("best", [128, PH, TOP])
    total = pair("total", [128, PH])
    inv = pair("inv", [128, PH])
    diag = pair("diag", [128, PH, 128])
    outer = [sb(f"outer{k}", [128, NE]) for k in range(BUFS)]
    kept = [sb(f"kept{k}", [128, NE]) for k in range(BUFS)]
    mixT = pair("mixT", [128, NE])
    z = pair("fz", [128, 128])
    y = pair("fy", [128, 128])
    stats = sb("fstats", [128, SLOTS, 6])
    mv = sb("fmv", [128, SLOTS, 2])
    veps = sb("fveps", [128, SLOTS])
    rstd = sb("frstd", [128, SLOTS])

    s_turn = sem("pk_weights_turned")
    s_turned = sem("pk_turned_copied")
    s_mean = sem("pk_mean_ready")
    s_meanT = sem("pk_mean_turned")
    s_mrow = sem("pk_mean_row_ready")
    s_outer = sem("pk_mean_product_ready")
    s_covc = sem("pk_covariance_ready")
    s_u = sem("pk_covariance_times_weights")
    s_wu = sem("pk_squares_ready")
    s_vm = sem("pk_variance_and_mean_ready")
    s_veps = sem("pk_variance_copied")
    s_root = sem("pk_root_ready")
    s_ks = sem("pk_scaled_keys_ready")
    s_fold = sem("pk_folded_weights_ready")
    s_folded = sem("pk_folded_weights_copied")
    s_mid = sem("pk_fold_chain")
    s_xs = sem("score_x_copied")
    s_sim = sem("half_scores_ready")
    s_biased = sem("half_scores_taken")
    s_gp = sem("expert_products_ready")
    s_g = sem("gelu_ready")
    s_simc = sem("half_scores_shifted")
    s_exp = sem("half_exps_ready")
    s_cut = sem("cut_ready")
    s_diag = sem("diagonals_ready")
    s_pr = sem("outer_product_ready")
    s_kept = sem("largest_kept")
    s_mixed = sem("kept_products_used")
    s_mixT = sem("mix_ready")
    s_y = sem("experts_summed")
    s_v = sem("final_variance_ready")
    s_r = sem("final_root_ready")
    s_fin = sem("result_ready")
    s_out = [sem(f"result{p}_stored") for p in range(SLOTS)]
    s_ch = sem("final_vector_chain")

    with nc.Block() as block:

        @block.sync
        def _(sp):
            with sp.Fori(0, ROUNDS) as i:
                for p in range(SLOTS):
                    u = SLOTS * i + p
                    sp.wait_ge(s_fin, u + 1)
                    sp.dma_start(out[bass.ds(u, 1)].rearrange("o t d -> t (o d)"), y[p][:]).then_inc(s_out[p], 16)
            for p in range(SLOTS):
                sp.wait_ge(s_out[p], 16 * (ROUNDS + 1))

        @block.tensor
        def _(pe):
            pe.wait_ge(c["loaded"], 64)
            for k in range(2 * PH):
                nc.tensor.transpose(ps[:, k // 4, 128 * (k % 4):128 * (k % 4) + 128], c["w_q"][:, k, :], ident[:])
            for half in range(2):
                for t in range(2):
                    nc.tensor.transpose(ps[:, 4, 256 * half + 128 * t:256 * half + 128 * t + 128],
                                        c["keys"][:, t, KD * half:KD * half + KD], ident[:])
            for k in range(NE // 128):
                mm = nc.tensor.transpose(ps[:, 5 + k // 4, 128 * (k % 4):128 * (k % 4) + 128],
                                         c["down"][:, k, :], ident[:])
            mm.then_inc(s_turn, 1)
            pe.wait_ge(s_mean, 1)
            nc.tensor.transpose(ps[0:1, 7, 0:128], covn[:, 128:129], ident[:]).then_inc(s_meanT, 1)
            pe.wait_ge(s_mrow, 1)
            nc.tensor.matmul(ps[:, 7, 0:128], mean_row[:], mean_row[:], start=True, stop=True).then_inc(s_outer, 1)
            pe.wait_ge(s_covc, 1)
            pe.wait_ge(s_turned, 1)
            for k in range(4):
                mm = nc.tensor.matmul(ps[:, k, :], covn[:, 0:128],
                                      c["w_q"][:, 4 * k:4 * k + 4, :].rearrange("k r d -> k (r d)"),
                                      start=True, stop=True)
            mm.then_inc(s_u, 1)
            pe.wait_ge(s_wu, 1)
            for k in range(2 * PH):
                nc.tensor.matmul(ps[:, 7, k:k + 1], wu[:, k, :], ones[:, 0:1], start=True, stop=True)
                mm = nc.tensor.matmul(ps[:, 7, 16 + k:17 + k], c["w_q"][:, k, :], covn[:, 128:129],
                                      start=True, stop=True)
            mm.then_inc(s_vm, 1)
            pe.wait_ge(s_ks, 1)
            for k in range(2 * PH):
                nc.tensor.matmul(ps[:, 5, NK * k:NK * k + NK], wqT[:, k, :], keys_s[:, k, :], start=True, stop=True)
            nc.tensor.matmul(ps[:, 6, :], ones[:], keys_b[:].rearrange("d r k -> d (r k)"), start=True,
                             stop=True).then_inc(s_fold, 1)

            pe.wait_ge(s_folded, 1)

            def prepare(u, p):
                pe.wait_ge(s_xs, u + 1)
                pe.wait_ge(s_biased, u + 1)
                nc.tensor.matmul(ps[:, SIM, :], xs[p][:], w_sim[:], start=True, stop=True).then_inc(s_sim, 1)
                yield
                pe.wait_ge(s_g, u + 1)
                for k in range(NE // 128):
                    mm = nc.tensor.matmul(ps[:, GELU + k // 4, 128 * (k % 4):128 * (k % 4) + 128],
                                          downT[:, 128 * k:128 * k + 128], xs[p][:], start=True, stop=True)
                mm.then_inc(s_gp, 1)
                for _ in range(7):
                    yield

            def mix(u, p):
                for h in range(PH):
                    if h == 0:
                        pe.wait_ge(s_diag, u + 1)
                    pe.wait_ge(s_kept, PH * u + h + 1 + BUFS)
                    for k in range(NE // 128):
                        mm = nc.tensor.matmul(ps[:, MIX + 2 * p + k // 4, 128 * (k % 4):128 * (k % 4) + 128],
                                              kept[h % BUFS][:, 128 * k:128 * k + 128], diag[p][:, h, :],
                                              start=(h == 0 and k % 4 == 0), stop=(h == PH - 1),
                                              skip_group_check=True)
                    mm.then_inc(s_mixed, 1)
                    yield

            def tail(u, p):
                pe.wait_ge(s_mixT, u + 1 + SLOTS)
                for k in range(NE // 128):
                    mm = nc.tensor.matmul(ps[:, OUT, 0:128], mixT[p][:, 128 * k:128 * k + 128],
                                          c["up"][:, k, :], start=(k == 0), stop=(k == NE // 128 - 1))
                mm.then_inc(s_y, 1)
                yield
                yield
                yield

            last_steps(pe, prepare, mix, tail)

        @block.scalar
        def _(act):
            act.wait_ge(s_turn, 1)
            nc.scalar.copy(wqT[:].rearrange("d (b r) k -> d b (r k)", b=4), ps[:, 0:4, :])
            nc.scalar.copy(keysT[:].rearrange("d r k -> d (r k)"), ps[:, 4, :])
            nc.scalar.copy(downT[:].rearrange("d (b n) -> d b n", b=2), ps[:, 5:7, :]).then_inc(s_turned, 1)

            def prepare(u, p):
                nc.scalar.copy(xs[p][:].unsqueeze(1), x5T[:, bass.ds(u, 1), :]).then_inc(s_xs, 1)
                yield
                yield
                act.wait_ge(s_gp, u + 1)
                act.wait_ge(s_mixT, u + 1)
                nc.scalar.activation(act_T[p][:].rearrange("e (b n) -> e b n", b=2), ps[:, GELU:GELU + 2, :],
                                     ACT.Gelu_apprx_tanh).then_inc(s_g, 1)
                yield
                yield
                act.wait_ge(s_simc, u + 1)
                nc.scalar.activation(halves[p][:], halves[p][:], ACT.Exp).then_inc(s_exp, 1)
                yield
                yield
                yield
                act.wait_ge(s_cut, u + 1)
                for h in range(PH):
                    ins = nc.scalar.mul(diag[p][:, h, :], ident[:], inv[p][:, h:h + 1])
                ins.then_inc(s_diag, 1)
                yield

            def mix(u, p):
                for _ in range(PH):
                    yield

            def tail(u, p):
                for _ in range(3):
                    yield

            last_steps(act, prepare, mix, tail)

        @block.gpsimd
        def _(pool):
            pool.wait_ge(s_veps, 1)
            nc.gpsimd.tensor_tensor(out=fold[:, 1, :], in0=fold[:, 0, :], in1=c["neg_half"][:], op=ALU.pow
                                    ).then_inc(s_root, 1)

            def prepare(u, p):
                for _ in range(8):
                    yield

            def mix(u, p):
                for h in range(PH):
                    if h == 0:
                        pool.wait_ge(s_exp, u + 1)
                    pool.wait_ge(s_kept, PH * u + h + 1)
                    nc.gpsimd.tensor_tensor(
                        out=outer[h % BUFS][:].rearrange("t (a b) -> t a b", a=NK),
                        in0=bcast(halves[p][:, h, 0:NK].unsqueeze(2), [128, NK, NK]),
                        in1=bcast(halves[p][:, PH + h, 0:NK].unsqueeze(1), [128, NK, NK]),
                        op=ALU.mult).then_inc(s_pr, 1)
                    yield

            def tail(u, p):
                yield
                pool.wait_ge(s_v, u + 1)
                nc.gpsimd.tensor_tensor(out=rstd[:, p:p + 1], in0=veps[:, p:p + 1],
                                        in1=c["neg_half"][:, 0:1], op=ALU.pow).then_inc(s_r, 1)
                yield
                yield

            last_steps(pool, prepare, mix, tail)

        @block.vector
        def _(dve):
            V = nc.vector
            n = [0]

            def link(ins):
                n[0] += 1
                ins.then_inc(s_mid, 1)
                dve.wait_ge(s_mid, n[0])

            link(V.tensor_scalar(covn[:], cov[:], 1.0 / N, None, ALU.mult))
            V.memset(veps[:], 1.0).then_inc(s_mean, 1)
            dve.wait_ge(s_meanT, 1)
            V.tensor_copy(mean_row[:], ps[0:1, 7, 0:128]).then_inc(s_mrow, 1)
            dve.wait_ge(s_outer, 1)
            V.tensor_tensor(covn[:, 0:128], covn[:, 0:128], ps[:, 7, 0:128], ALU.subtract).then_inc(s_covc, 1)
            dve.wait_ge(s_u, 1)
            V.tensor_tensor(wu[:].rearrange("d (b r) k -> d b (r k)", b=4), ps[:, 0:4, :],
                            c["w_q"][:].rearrange("d (b r) k -> d b (r k)", b=4), ALU.mult).then_inc(s_wu, 1)
            dve.wait_ge(s_vm, 1)
            link(V.tensor_copy(means[:], ps[:, 7, 16:32]))
            V.tensor_scalar(fold[:, 0, :], ps[:, 7, 0:16], BN_EPS, None, ALU.add).then_inc(s_veps, 1)
            dve.wait_ge(s_root, 1)
            link(V.tensor_tensor(fold[:, 2, :], fold[:, 1, :], cols[:, R_GAMMA:R_GAMMA + 16], ALU.mult))
            link(V.tensor_tensor(fold[:, 3, :], means[:], fold[:, 2, :], ALU.mult))
            link(V.tensor_tensor(fold[:, 3, :], cols[:, R_BETA:R_BETA + 16], fold[:, 3, :], ALU.subtract))
            dve.wait_ge(s_turned, 1)
            link(V.tensor_tensor(keys_s[:], keysT[:], bcast(fold[:, 2, :].unsqueeze(2), [128, 2 * PH, NK]), ALU.mult))
            V.tensor_tensor(keys_b[:], keysT[:], bcast(fold[:, 3, :].unsqueeze(2), [128, 2 * PH, NK]),
                            ALU.mult).then_inc(s_ks, 1)
            dve.wait_ge(s_fold, 1)
            V.tensor_copy(w_sim[:], ps[:, 5, :])
            V.tensor_copy(b_sim[:], ps[:, 6, :]).then_inc(s_folded, 1)
            for k in range(BUFS):
                V.memset(outer[k][:, 0:1], 0.0).then_inc(s_kept, 1)
                V.memset(kept[k][:, 0:1], 0.0).then_inc(s_mixed, 1)
            V.memset(halves[0][:, 0, 0:1], 0.0).then_inc(s_biased, 1)
            V.memset(act_T[0][:, 0:1], 0.0).then_inc(s_g, 1)
            for p in range(SLOTS):
                V.memset(mixT[p][:, 0:1], 0.0).then_inc(s_mixT, 1)
                V.memset(y[p][:, 0:1], 0.0).then_inc(s_out[p], 16)
            dve.wait_ge(s_folded, 1)

            state = {}
            expected = [0, PREP_LINKS, PREP_LINKS] + 2 * [PREP_LINKS + TAIL_LINKS] + [TAIL_LINKS]

            def settle():
                V.memset(spare[:], 0.0)

            def chain(ins):
                state["links"] += 1
                ins.then_inc(s_ch, 1)
                dve.wait_ge(s_ch, state["base"] + state["links"])

            def begin(step):
                assert state.get("links", 0) == expected.pop(0), state["links"]
                tails = 0 if isinstance(step, int) and step < SLOTS else TAIL_LINKS * (step - SLOTS)
                prepared = min(step, B) if isinstance(step, int) else step
                state.update(base=PREP_LINKS * prepared + tails, links=0)

            def prepare(u, p):
                hv = halves[p]
                yield
                dve.wait_ge(s_sim, u + 1)
                V.tensor_tensor(hv[:, :, 0:NK], ps[:, SIM, :].rearrange("t (r k) -> t r k", k=NK),
                                b_sim[:].rearrange("t (r k) -> t r k", k=NK), ALU.add).then_inc(s_biased, 1)
                yield
                dve.wait_ge(s_biased, u + 2)
                settle()
                for r in range(2 * PH):
                    ins = V.max(hv[:, r, NK:SEG], hv[:, r, 0:NK])
                chain(ins)
                yield
                chain(V.tensor_copy(mxs[p][:], hv[:, :, NK]))
                V.tensor_tensor(hv[:], hv[:], bcast(mxs[p][:].unsqueeze(2), [128, 2 * PH, SEG]),
                                ALU.subtract).then_inc(s_simc, 1)
                yield
                yield
                dve.wait_ge(s_exp, u + 1)
                chain(V.tensor_tensor(cand[p][:].rearrange("t h (a b) -> t h a b", a=TOP),
                                      bcast(hv[:, 0:PH, NK:SEG].unsqueeze(3), [128, PH, TOP, TOP]),
                                      bcast(hv[:, PH:2 * PH, NK:SEG].unsqueeze(2), [128, PH, TOP, TOP]), ALU.mult))
                yield
                settle()
                for h in range(PH):
                    ins = V.max(best[p][:, h, :], cand[p][:, h, :])
                chain(ins)
                chain(V.tensor_reduce(total[p][:], best[p][:], AX.X, ALU.add))
                V.reciprocal(inv[p][:], total[p][:]).then_inc(s_cut, 1)
                yield
                yield

            def mix(u, p):
                for h in range(PH):
                    dve.wait_ge(s_pr, PH * u + h + 1)
                    dve.wait_ge(s_mixed, PH * u + h + 1)
                    o = outer[h % BUFS][:]
                    V.scalar_tensor_tensor(out=kept[h % BUFS][:], in0=o, scalar=best[p][:, h, TOP - 1:TOP],
                                           in1=o, op0=ALU.is_ge, op1=ALU.mult).then_inc(s_kept, 1)
                    yield

            def tail(u, p):
                dve.wait_ge(s_mixed, PH * u + PH + BUFS)
                dve.wait_ge(s_g, u + 2)
                V.tensor_tensor(mixT[p][:].rearrange("e (b n) -> e b n", b=2), ps[:, MIX + 2 * p:MIX + 2 * p + 2, :],
                                act_T[p][:].rearrange("e (b n) -> e b n", b=2), ALU.mult).then_inc(s_mixT, 1)
                yield
                dve.wait_ge(s_y, u + 1)
                chain(V.tensor_tensor(z[p][:].unsqueeze(1), ps[:, OUT:OUT + 1, 0:128], x5[:, bass.ds(u, 1), :], ALU.add))
                chain(V.bn_stats(stats[:, p, :], z[p][:]))
                settle()
                chain(V.bn_aggr(mv[:, p, :], stats[:, p, :]))
                V.tensor_scalar(veps[:, p:p + 1], mv[:, p, 1:2], LN_EPS, None, ALU.add).then_inc(s_v, 1)
                yield
                dve.wait_ge(s_r, u + 1)
                dve.wait_ge(s_out[p], 8 * (u - p) + 16)
                V.tensor_scalar(y[p][:], z[p][:], mv[:, p, 0:1], rstd[:, p:p + 1], ALU.subtract,
                                ALU.mult).then_inc(s_fin, 1)
                yield

            last_steps(dve, prepare, mix, tail, begin)


INPUTS = (
    "x", "ctx_2048", "mask_BxS2_if0", "L0_attn_W_qkv", "L0_attn_b_qkv", "L0_attn_W_proj", "L0_attn_b_proj",
    "L0_xattn_Wq", "L0_xattn_Wkv", "L0_xattn_null_kv", "L0_xattn_Wout", "L0_xattn_ln_scale",
    "L0_xattn_ln_bias", "L0_ffn_Wr", "L0_ffn_br", "L0_ffn_W1", "L0_ffn_b1", "L0_ffn_W2", "L0_ffn_b2",
    "L1_attn_Wq", "L1_attn_bq", "L1_attn_Wk", "L1_attn_bk", "L1_attn_Wv", "L1_attn_bv", "L1_attn_Wo",
    "L1_attn_bo", "L1_xattn_W_in", "L1_xattn_b_in", "L1_xattn_g_res", "L1_xattn_g_init", "L1_ffn_w_q",
    "L1_ffn_bn_gamma", "L1_ffn_bn_beta", "L1_ffn_keys", "L1_ffn_down_embed", "L1_ffn_up_embed")


def kernel(**inputs):
    import concourse.bacc as bacc
    from concourse.bass_utils import run_bass_kernel_spmd

    nc = bacc.Bacc("TRN2", target_bir_lowering=False, num_devices=1)
    arrays, args = {}, {}
    laid = {name: np.ascontiguousarray(inputs[name]) for name in INPUTS}
    laid["rel_rev"] = np.ascontiguousarray(np.asarray(inputs["L1_attn_rel_table"])[::-1].T)
    for name, arr in laid.items():
        arrays[f"in_{name}"] = arr
        args[name] = nc.dram_tensor(f"in_{name}", arr.shape, mybir.dt.from_np(arr.dtype),
                                    kind="ExternalInput").ap()
    result = nc.dram_tensor("result", [B, T, D], F32, kind="ExternalOutput").ap()
    build(nc, args, result)
    r = run_bass_kernel_spmd(nc, [arrays], core_ids=[0])
    return r.results[0]["result"]
```

```python
from contextlib import ExitStack

import numpy as np

import concourse.bass as bass
from concourse import mybir

ALU = mybir.AluOpType
ACT = mybir.ActivationFunctionType
AX = mybir.AxisListType
F32 = mybir.dt.float32
BF16 = mybir.dt.bfloat16
I32 = mybir.dt.int32
U32 = mybir.dt.uint32

B, T, D = 16, 128, 128
SLOTS = 2
ROUNDS = B // SLOTS
HEADS, DH = 16, 8
XH, XDH = 16, 64
XC = XH * XDH // 128
M, CTX = 77, 256
MK = M + 1
E, HID = 8, 256
HC = HID // 128
PH, KD, NK = 8, 128, 32
TOP = 8
NE = NK * NK
LN_EPS = 1e-5
XLN_EPS = 1e-6
RMS_EPS = 1e-5
BN_EPS = 1e-5
MASKED = -1e30
LOGP = -0.001
DT = float(-np.log(-np.expm1(np.float32(LOGP))))
BCOEF = float(np.exp(np.float32(LOGP)))

FIRST_LINKS = 23
SECOND_LINKS = 27
PREP_LINKS = 5
TAIL_LINKS = 3
R_B1, R_GAMMA, R_BETA = 0, 16, 32
R_BQK0, R_BQK1, R_GRES, R_NULLK = 48, 50, 52, 53
NROWS = 54

ROOT_1, ROOT_X, ROOT_2, ROOT_ROWS, ROOT_3, ROOT_4, ROOT_IN, ROOT_5 = range(8)
RSTDS = 8
ROOTS_OF_HALF = (3, 5)

NCH = 4
PE_ORDER = "FFSSFFSFSFFFSFSSFFSFFSSFSCFSCFFSFSFSFCS"
DVE_ORDER = "FSFSFFSFSFFCSFFSFSFSFSSFSCFFFSSFFSFCSFS"
ACT_ORDER = "FFSSFFSFFSFFFSFFSSSSSFSCFFFFFCSFSFFSSSC"
POOL_ORDER = "FSFSSFFSFFFFCSFSFSSFFSSFSFCFFSSFFSFCSFS"
PE_FIRST_ORDER = "FFDSSFFDSFSFDFFSFSSFFSFFSSFSCFSCFFSFSFSFCS"
DVE_FIRST_ORDER = "FSFDSFFDSFSFDFCSFFSFFSSFSSFSCFFFSSFFSFCSFS"
ACT_FIRST_ORDER = "FFDSSFFDSFDSFFFFSFFSSSSFSCSFFFFFCSFSFFSSSC"
POOL_FIRST_ORDER = "FSFDSSFFDSFFDFFCSFSFSSFFSSFSFCFFSSFFSFCSFS"
PE_LAST_ORDER = "PPTMMPMMPMMMMTPTPPP"
DVE_LAST_ORDER = "MMPMTPMPPMPTMPMMPPT"
ACT_LAST_ORDER = "PPTMMPMMPMMMMTPTPPP"
POOL_LAST_ORDER = "PPTMMPMMMMMPTMPTPPP"


def weave(order, **parts):
    for which in order:
        if parts[which] is not None:
            next(parts[which])


def steps(engine, first_order, order, context, first, second, late_setup, turn_weights, begin=lambda step: None):
    def step(u, p, f, s, c):
        begin(u)
        weave(order, F=first(u, p) if f else None, S=second(u - 1, 1 - p) if s else None,
              C=context(u + 1, 1 - p) if c else None)

    begin(0)
    weave(first_order, F=first(0, 0), S=late_setup(), C=context(1, 1), D=context(0, 0, 1))
    with engine.Fori(0, ROUNDS - 1) as i:
        for p in (1, 0):
            step(SLOTS * i + SLOTS - p, p, True, True, True)
    step(B - 1, 1, True, True, False)
    begin(B)
    weave(order, F=turn_weights(), S=second(B - 1, 1), C=None)


def last_steps(engine, order, prepare, mix, tail, begin=lambda step: None):
    def step(u, p, t, m, e):
        begin(u)
        weave(order, P=prepare(u, p) if t else None, M=mix(u - 1, 1 - p) if m else None,
              T=tail(u - 2, p) if e else None)

    step(0, 0, True, False, False)
    step(1, 1, True, True, False)
    with engine.Fori(0, ROUNDS - 1) as i:
        for p in range(SLOTS):
            step(SLOTS * i + SLOTS + p, p, True, True, True)
    step(B, 0, False, True, True)
    step(B + 1, 1, False, False, True)


def bcast(ap, shape):
    return ap.broadcast_to(shape)


def build(nc, a, out):
    with ExitStack() as ctx:
        def sb(name, shape, dt=F32, where=ctx):
            return where.enter_context(nc.sbuf_tensor(name, shape, dt))

        def sem(name):
            return ctx.enter_context(nc.semaphore(name))

        ps = ctx.enter_context(nc.psum_tensor("ps", [128, 8, 512], F32))

        ident = sb("ident", [128, 128])
        neg_half = sb("neg_half", [128, 16])
        ones_col = sb("ones_col", [128, 128])
        cols = sb("cols", [128, NROWS])
        spare = sb("spare", [1, 1])
        x5 = sb("x5", [128, B, 128])
        x5T = sb("x5T", [128, B, 128])
        cov = sb("cov", [128, 129])
        pk_wq = sb("pk_wq", [128, 2 * PH, KD])
        pk_keys = sb("pk_keys", [128, 2, 2 * KD])
        pk_down = sb("pk_down", [128, NE // 128, 128])
        pk_up = sb("pk_up", [128, NE // 128, 128])

        wqT = sb("wqT", [128, 2 * PH, 128])
        keys_downT = sb("keys_downT", [128, 2048])

        loop1 = ctx.enter_context(ExitStack())

        def sb1(name, shape, dt=F32):
            return sb(name, shape, dt, loop1)

        ident16 = sb1("ident16", [128, 128], BF16)
        causal16 = sb1("causal16", [128, 4, 128], BF16)
        head_mask = sb1("head_mask", [128, HEADS])
        iota8 = sb1("iota8", [128, E])
        iota_col = sb1("iota_col", [128, 1])

        w_qkv = [sb1(f"w_qkv{l}", [128, 3, 128]) for l in range(2)]
        w_proj = [sb1(f"w_proj{l}", [128, 128]) for l in range(2)]
        b_v = [sb1(f"b_v{l}", [128, 128]) for l in range(2)]
        b_proj = [sb1(f"b_proj{l}", [128, 128]) for l in range(2)]
        rel_bias = sb1("rel_bias", [128, HEADS, 128])
        xw_q = sb1("xw_q", [128, XC * 128])
        xw_kv = sb1("xw_kv", [128, 2, 2 * XC * 128])
        xw_out = sb1("xw_out", [128, XC, 128])
        x_scale = sb1("x_scale", [128, 128])
        x_bias = sb1("x_bias", [128, 128])
        w_r = sb1("w_r", [128, E])
        b_r = sb1("b_r", [128, E])
        w_1 = sb1("w_1", [128, E, HID])
        w_2 = sb1("w_2", [128, E, HC, 128])
        b_2 = sb1("b_2", [E, 128])
        w_inT = sb1("w_inT", [128, 128])
        b_in = sb1("b_in", [128, 128])
        g_init = sb1("g_init", [128, 128])
        plug_T = sb1("plug_T", [M, B, 128])


        rel_dram = nc.dram_tensor("rel_scratch", [HEADS, 256], F32, kind="Internal").ap()
        plug_dram = nc.dram_tensor("plug_scratch", [B, M], F32, kind="Internal").ap()

        s_w0 = sem("first_attention_weights_loaded")
        s_wkv = sem("context_weights_loaded")
        s_wx = sem("cross_attention_weights_loaded")
        s_we = sem("expert_weights_loaded")
        s_w1 = sem("second_attention_weights_loaded")
        s_wp = sem("patch_weights_loaded")
        s_rows = sem("rows_loaded")
        s_pk = sem("product_key_weights_loaded")
        s_rel = sem("relative_table_loaded")
        s_rel_ext = sem("relative_table_extended")
        s_rel_out = sem("relative_table_stored")
        s_rel_in = sem("relative_bias_loaded")
        s_rel_fl = sem("relative_bias_flipped")
        s_plen = sem("patch_lengths_loaded")
        s_plug = sem("patch_ends_ready")
        s_plug_out = sem("patch_ends_stored")
        s_plug_in = sem("patch_ends_spread")
        s_hits = sem("boundaries_ready")
        s_counts_taken = sem("boundary_counts_taken")
        s_rel_taken = sem("relative_bias_taken")
        s_plug_rows = sem("boundary_counts_ready")
        s_const = sem("pool_constants_ready")
        s_zero = sem("vector_constants_ready")
        s_setup = sem("vector_setup_chain")
        s_pchain = sem("pool_chain")
        s_rowsT = sem("rows_turned")
        s_winT = sem("w_in_turned")
        s_setup_done = sem("setup_for_first_halves_done")
        s_late_done = sem("setup_for_second_halves_done")
        s_ev = sem("plug_exp_ready")
        s_nullv = sem("null_value_loaded")
        s_vz = sem("value_zeros_ready")

        def pair(name, shape, dt=F32, where=loop1):
            return [sb(f"{name}{p}", shape, dt, where) for p in range(SLOTS)]

        x_in = pair("x_in", [128, 128])
        c_in = pair("c_in", [M, CTX])
        wide_a = pair("wide_a", [128, 2048])
        wide_p = [wqT[:].rearrange("q r k -> q (r k)"), sb1("wide_p1", [128, 2048])[:]]
        wide_t = [keys_downT[:], sb1("wide_t1", [128, 2048])[:]]
        v_exp = pair("v_exp", [128, HEADS, 128])
        v_z = pair("v_z", [MK, XH, 128])
        k_exp = pair("k_exp", [128, XC, 2, MK])
        c_T = pair("c_T", [128, 2, M])
        x_T = pair("x_T", [128, 128])
        k_T = pair("k_T", [128, 128])
        att_T = pair("att_T", [128, 128])
        mx = pair("mx", [128, 16])
        sums = pair("sums", [128, 16])
        rsum = pair("rsum", [128, 16])
        z = pair("z", [128, 128])
        z2 = pair("z2", [128, 128])
        x_1 = pair("x_1", [128, 128])
        x_2 = pair("x_2", [128, 128])
        x_3 = pair("x_3", [128, 128])
        x_5 = pair("x_5", [128, 129])
        scan = pair("scan", [128, 128])
        logit = pair("logit", [128, E])
        logit_e = pair("logit_e", [128, E])
        top8 = pair("top8", [128, 8])
        top8i = pair("top8i", [128, 8], U32)
        sm = pair("sm", [128, 8])
        w_one = pair("w_one", [128, E])
        stats = sb("stats", [128, SLOTS * RSTDS, 6], F32, loop1)
        mv = sb("mv", [128, SLOTS * RSTDS, 2], F32, loop1)
        veps = sb("veps", [128, SLOTS * RSTDS], F32, loop1)
        rstd = sb("rstd", [128, SLOTS * RSTDS], F32, loop1)

        r_z = [wide_a[p][0:64, 0:256].rearrange("d (g q) -> d g q", g=2) for p in range(SLOTS)]
        x_4 = x_1
        w_oneT = [k_T[p][0:E, :] for p in range(SLOTS)]
        squares = [wide_t[p][:, 1024:1024 + CTX] for p in range(SLOTS)]
        plug_now = [wide_t[p][0:M, 1536:1664] for p in range(SLOTS)]
        plen_i = wide_t[1][0:B, 640:640 + M].bitcast(I32)
        edge = wide_t[1][0:B, 720:720 + M]
        hits = wide_a[1][:, 0:B * M]
        rel_ext = wide_a[1][0:HEADS, 1280:1536]
        upto = wide_t[1][:, 512:640]
        flip = wide_t[1][:, 128:256]
        w_in = wide_t[1][:, 256:384]
        rows = wide_t[1][0:NROWS, 384:512]

        s_x = [sem(f"x{p}_loaded") for p in range(SLOTS)]
        s_c = [sem(f"context{p}_loaded") for p in range(SLOTS)]
        s_slot = sem("slot_free")
        A = [{n: sem(f"attention{l}_{n}") for n in (
            "x_turned", "xT_ready", "qkv_ready", "masked_q_ready", "v_ready", "scores_ready",
            "shifted", "probs_ready", "probs_turned", "probsT_ready", "mixed", "mixed_ready",
            "residual_ready", "projected")} for l in range(2)]
        X = {n: sem(f"cross_{n}") for n in (
            "c_turned", "cT_ready", "k_ready", "k_copied", "v_ready", "v_copied",
            "x_turned", "xT_ready", "q_ready", "q_copied", "scores_ready", "shifted", "probs_ready",
            "normalized", "probs_turned", "probsT_ready", "mixed", "mixed_copied", "residual_ready",
            "projected")}
        F = {n: sem(f"experts_{n}") for n in (
            "x_turned", "xT_ready", "logits_ready", "max_ready", "exp_ready", "gate_ready",
            "gate_turned", "gateT_ready", "hidden_ready", "relu_even", "relu_odd", "outputs_ready",
            "weighted")}
        G = {n: sem(f"patch_{n}") for n in (
            "x_turned", "xT_ready", "row_squares", "x_squares", "rows_scaled", "rows_ready",
            "plug_taken", "row_product", "scan_taken", "scan_ready", "input_product", "residual_ready", "x5_kept", "summed")}
        s_x1 = sem("x1_ready")
        s_x2 = sem("x2_ready")
        s_x3 = sem("x3_ready")
        s_x4 = sem("x4_ready")
        s_x5 = sem("x5_ready")
        s_x5T = sem("x5_turned")
        s_x5T_ready = sem("x5T_stored")
        s_var = [sem(f"variance_ready_in_{h}_half") for h in ("first", "second")]
        s_rstd = [sem(f"rstd_ready_in_{h}_half") for h in ("first", "second")]
        s_chain = sem("vector_chain")
        s_turn = sem("last_weights_turned")

        def v_blocks(p):
            base = v_exp[p][:]
            return bass.AP(tensor=base.tensor, offset=base.offset,
                           ap=[base.ap[0], [8 * 128, 2], [128 + DH, 8], [1, DH]])

        bank = lambda p, k: ps[:, 4 * p + k, :]
        banks = lambda p: ps[:, 4 * p:4 * p + 4, :]
        half_of = lambda k: int(k >= ROOTS_OF_HALF[0])
        root_count = lambda k, u: ROOTS_OF_HALF[half_of(k)] * u + k - ROOTS_OF_HALF[0] * half_of(k) + 1
        one = lambda tile, u: tile[:, bass.ds(u, 1), :]

        def weights_dma(q, names):
            for dst, src, s in names:
                q.dma_start(dst, src).then_inc(s, 16)

        def pbc(ap1d, n=128):
            return ap1d.partition_broadcast(n)

        row_sources = [
            (R_B1, 16, a["L0_ffn_b1"].rearrange("e (j h) -> (e j) h", h=128)),
            (R_GAMMA, 16, a["L1_ffn_bn_gamma"].rearrange("(r d) -> r d", d=128)),
            (R_BETA, 16, a["L1_ffn_bn_beta"].rearrange("(r d) -> r d", d=128)),
            (R_BQK0, 2, a["L0_attn_b_qkv"].rearrange("(r d) -> r d", d=128)[0:2]),
            (R_BQK1, 1, a["L1_attn_bq"].unsqueeze(0)),
            (R_BQK1 + 1, 1, a["L1_attn_bk"].unsqueeze(0)),
            (R_GRES, 1, a["L1_xattn_g_res"].unsqueeze(0)),
        ]
        N_ROWS_DMA = len(row_sources) + 2

        first = ctx.enter_context(ExitStack())
        block = first.enter_context(nc.Block())

        @block.sync
        def _(sp):
            sp.dma_start(x_in[0][:], a["x"][0]).then_inc(s_x[0], 16)
            weights_dma(sp, [
                (w_qkv[0][:], a["L0_attn_W_qkv"].rearrange("k (t n) -> k t n", t=3), s_w0),
                (w_proj[0][:], a["L0_attn_W_proj"], s_w0),
                (b_v[0][:], pbc(a["L0_attn_b_qkv"][2 * D:3 * D]), s_w0),
                (b_proj[0][:], pbc(a["L0_attn_b_proj"]), s_w0),
            ])
            for r, n, src in row_sources:
                sp.dma_start(rows[r:r + n, :], src).then_inc(s_rows, 16)
            for j in range(2):
                sp.dma_start(rows[R_NULLK:R_NULLK + 1, 64 * j:64 * j + 64],
                             a["L0_xattn_null_kv"][0:1, :]).then_inc(s_rows, 16)
            sp.dma_start(c_in[0][:], a["ctx_2048"][0]).then_inc(s_c[0], 16)
            weights_dma(sp, [
                (xw_kv[:], a["L0_xattn_Wkv"].rearrange("(c k) n -> k c n", k=128), s_wkv),
                (xw_q[:], a["L0_xattn_Wq"], s_wx),
                (xw_out[:], a["L0_xattn_Wout"].rearrange("(c k) n -> k c n", k=128), s_wx),
                (x_scale[:], pbc(a["L0_xattn_ln_scale"]), s_wx),
                (x_bias[:], pbc(a["L0_xattn_ln_bias"]), s_wx),
            ])
            sp.dma_start(x_in[1][:], a["x"][1]).then_inc(s_x[1], 16)
            sp.dma_start(c_in[1][:], a["ctx_2048"][1]).then_inc(s_c[1], 16)
            for p in range(SLOTS):
                sp.wait_ge(s_vz, p + 1)
                for hp in range(2):
                    sp.dma_start(
                        v_z[p][M:M + 1].rearrange("k (c g) d -> k c g d", g=2)[:, :, hp, 64 * hp:64 * hp + 64],
                        a["L0_xattn_null_kv"][1:2, :].unsqueeze(1).broadcast_to([1, XC, 64]),
                    ).then_inc(s_nullv, 16)
            sp.wait_ge(s_rel_ext, 1)
            sp.dma_start(rel_dram[:, 0:255], rel_ext[:, 0:255]).then_inc(s_rel_out, 16)
            sp.wait_ge(s_plug, 1)
            sp.dma_start(plug_dram, edge).then_inc(s_plug_out, 16)
            sp.wait_ge(s_rel_out, 16)
            sp.dma_start(wide_p[1][:].rearrange("i (h j) -> i h j", h=HEADS),
                         bass.AP(tensor=rel_dram.tensor, offset=0, ap=[[1, 128], [256, HEADS], [1, 128]])
                         ).then_inc(s_rel_in, 16)
            sp.wait_ge(s_plug_out, 16)
            sp.dma_start(hits, plug_dram.rearrange("b m -> (b m)").partition_broadcast(128)
                         ).then_inc(s_plug_in, 16)
            weights_dma(sp, [
                (w_r[:], a["L0_ffn_Wr"], s_we),
                (b_r[:], pbc(a["L0_ffn_br"]), s_we),
                (w_1[:], a["L0_ffn_W1"].rearrange("e k n -> k e n"), s_we),
                (w_2[:], a["L0_ffn_W2"].rearrange("e (j k) n -> k e j n", k=128), s_we),
                (b_2[:], a["L0_ffn_b2"], s_we),
                (w_qkv[1][:, 0, :], a["L1_attn_Wq"], s_w1),
                (w_qkv[1][:, 1, :], a["L1_attn_Wk"], s_w1),
                (w_qkv[1][:, 2, :], a["L1_attn_Wv"], s_w1),
                (w_proj[1][:], a["L1_attn_Wo"], s_w1),
                (b_v[1][:], pbc(a["L1_attn_bv"]), s_w1),
                (b_proj[1][:], pbc(a["L1_attn_bo"]), s_w1),
            ])
            weights_dma(sp, [
                (pk_wq[:], a["L1_ffn_w_q"].rearrange("k (r d) -> k r d", d=KD), s_pk),
                (pk_keys[:], a["L1_ffn_keys"].rearrange("(t h) k p d -> (h k) t (p d)", t=2), s_pk),
                (pk_down[:], a["L1_ffn_down_embed"].rearrange("(c k) n -> k c n", k=128), s_pk),
                (pk_up[:], a["L1_ffn_up_embed"].rearrange("(c k) n -> k c n", k=128), s_pk),
            ])
            with sp.Fori(0, ROUNDS - 1) as i:
                for p in range(SLOTS):
                    u = SLOTS * i + p
                    sp.wait_ge(A[0]["x_turned"], u + 1)
                    sp.wait_ge(A[0]["residual_ready"], u + 1)
                    sp.dma_start(x_in[p][:], a["x"][bass.ds(u + SLOTS, 1)].rearrange("o t d -> t (o d)")
                                 ).then_inc(s_x[p], 16)
                    sp.wait_ge(G["row_product"], u + 1)
                    sp.dma_start(c_in[p][:], a["ctx_2048"][bass.ds(u + SLOTS, 1)].rearrange("o t d -> t (o d)")
                                 ).then_inc(s_c[p], 16)

        @block.gpsimd
        def _(pool):
            n = [0]

            def link(ins):
                n[0] += 1
                ins.then_inc(s_pchain, 1)
                pool.wait_ge(s_pchain, n[0])

            link(nc.gpsimd.memset(ident[:], 1.0))
            link(nc.gpsimd.affine_select(out=ident[:], in_=ident[:], compare_op=ALU.is_equal, fill=0.0,
                                         base=0, pattern=[[-1, 128]], channel_multiplier=1))
            nc.gpsimd.memset(ones_col[:], 1.0).then_inc(s_const, 1)
            link(nc.gpsimd.tensor_copy(ident16[:], ident[:]))
            link(nc.gpsimd.memset(causal16[:], 0.0))
            link(nc.gpsimd.affine_select(out=causal16[:], in_=causal16[:], compare_op=ALU.is_ge, fill=MASKED,
                                         base=0, pattern=[[0, 4], [-1, 128]], channel_multiplier=1))
            link(nc.gpsimd.memset(head_mask[:], float(DH) ** -0.5))
            link(nc.gpsimd.affine_select(out=head_mask[:], in_=head_mask[:], compare_op=ALU.is_ge, fill=0.0,
                                         base=0, pattern=[[-DH, HEADS]], channel_multiplier=1))
            link(nc.gpsimd.affine_select(out=head_mask[:], in_=head_mask[:], compare_op=ALU.is_ge, fill=0.0,
                                         base=DH - 1, pattern=[[DH, HEADS]], channel_multiplier=-1))
            nc.gpsimd.memset(neg_half[:], -0.5).then_inc(s_const, 1)
            link(nc.gpsimd.memset(flip[:], 1.0))
            link(nc.gpsimd.affine_select(out=flip[:], in_=flip[:], compare_op=ALU.is_equal, fill=0.0,
                                         base=-127, pattern=[[1, 128]], channel_multiplier=1))
            link(nc.gpsimd.memset(upto[:], 1.0))
            link(nc.gpsimd.affine_select(out=upto[:], in_=upto[:], compare_op=ALU.is_ge, fill=0.0,
                                         base=0, pattern=[[1, 128]], channel_multiplier=-1))
            link(nc.gpsimd.iota(iota8[:], pattern=[[1, E]], base=0, channel_multiplier=0,
                                allow_small_or_imprecise_dtypes=True))
            nc.gpsimd.iota(iota_col[:], pattern=[[1, 1]], base=0, channel_multiplier=1,
                                allow_small_or_imprecise_dtypes=True).then_inc(s_const, 1)

            pool.wait_ge(s_setup_done, 1)

            def late_setup():
                for _ in range(15):
                    yield
                pool.wait_ge(s_late_done, 1)
                yield

            def root(k, u, p):
                pool.wait_ge(s_var[half_of(k)], root_count(k, u))
                c = RSTDS * p + k
                nc.gpsimd.tensor_tensor(out=rstd[:, c:c + 1], in0=veps[:, c:c + 1],
                                        in1=neg_half[:, 0:1], op=ALU.pow).then_inc(s_rstd[half_of(k)], 1)

            def context(u, p, q=None):
                for _ in range(3):
                    yield

            def first_half(u, p):
                pool.wait_ge(s_slot, u + 1)
                pool.wait_ge(s_x[p], 8 * (u - p) + 16)
                nc.gpsimd.tensor_tensor(out=z2[p][:], in0=x_in[p][:], in1=b_proj[0][:], op=ALU.add
                                        ).then_inc(A[0]["residual_ready"], 1)
                for _ in range(8):
                    yield
                root(ROOT_1, u, p)
                yield
                if isinstance(u, int) and u == 0:
                    pool.wait_ge(s_wx, 16 * 4)
                pool.wait_ge(s_x1, u + 1)
                nc.gpsimd.tensor_tensor(out=z2[p][:], in0=x_1[p][:], in1=x_bias[:], op=ALU.add
                                        ).then_inc(X["residual_ready"], 1)
                for _ in range(9):
                    yield
                root(ROOT_X, u, p)
                yield
                root(ROOT_2, u, p)
                yield

            def second_half(u, p):
                for _ in range(2):
                    yield
                nc.gpsimd.tensor_copy(plug_now[p].unsqueeze(1), one(plug_T, u)).then_inc(G["plug_taken"], 1)
                root(ROOT_ROWS, u, p)
                pool.wait_ge(s_rstd[1], root_count(ROOT_ROWS, u))
                k = RSTDS * p + ROOT_ROWS
                nc.gpsimd.tensor_tensor(out=c_in[p][:, 0:128], in0=c_in[p][:, 0:128],
                                        in1=bcast(rstd[0:M, k:k + 1], [M, 128]), op=ALU.mult
                                        ).then_inc(G["rows_scaled"], 1)
                pool.wait_ge(G["rows_scaled"], u + 1)
                nc.gpsimd.tensor_tensor(out=c_in[p][:, 0:128], in0=c_in[p][:, 0:128],
                                        in1=g_init[0:M, :], op=ALU.mult).then_inc(G["rows_ready"], 1)
                yield
                root(ROOT_3, u, p)
                yield
                pool.wait_ge(s_x3, u + 1)
                nc.gpsimd.tensor_tensor(out=z2[p][:], in0=x_3[p][:], in1=b_proj[1][:], op=ALU.add
                                        ).then_inc(A[1]["residual_ready"], 1)
                yield
                pool.wait_ge(G["scan_taken"], u + 1)
                nc.gpsimd.tensor_tensor(out=scan[p][:], in0=scan[p][:], in1=b_in[:], op=ALU.add
                                        ).then_inc(G["scan_ready"], 1)
                for _ in range(7):
                    yield
                root(ROOT_4, u, p)
                yield
                pool.wait_ge(s_x4, u + 1)
                pool.wait_ge(G["scan_ready"], u + 1)
                nc.gpsimd.tensor_tensor(out=z2[p][:], in0=x_4[p][:], in1=scan[p][:], op=ALU.add
                                        ).then_inc(G["residual_ready"], 1)
                root(ROOT_IN, u, p)
                yield
                root(ROOT_5, u, p)
                yield
                pool.wait_ge(s_x5, u + 1)
                nc.gpsimd.tensor_copy(one(x5, u), x_5[p][:, 0:128].unsqueeze(1)).then_inc(G["x5_kept"], 1)
                yield

            def turn_weights():
                while True:
                    yield

            steps(pool, POOL_FIRST_ORDER, POOL_ORDER, context, first_half, second_half, late_setup, turn_weights)

        @block.tensor
        def _(pe):
            pe.wait_ge(s_const, 1)
            pe.wait_ge(s_rows, 16 * N_ROWS_DMA)
            nc.tensor.transpose(ps[:, 0, 0:NROWS], rows[:], ident[0:NROWS, 0:NROWS]).then_inc(s_rowsT, 1)
            pe.wait_ge(s_wp, 16 * 3)
            nc.tensor.transpose(ps[:, 1, 0:128], w_in[:], ident[:]).then_inc(s_winT, 1)
            pe.wait_ge(s_w0, 16 * 4)
            pe.wait_ge(s_const, 2)
            pe.wait_ge(s_setup_done, 1)

            def late_setup():
                for _ in range(4):
                    yield
                pe.wait_ge(s_const, 3)
                pe.wait_ge(s_rel_in, 16)
                for n in range(2):
                    if n == 1:
                        pe.wait_ge(s_rel_taken, 1)
                    for c in range(2):
                        mm = nc.tensor.matmul(bank(1, c), flip[:], wide_p[1][:, 512 * (2 * n + c):512 * (2 * n + c) + 512],
                                              start=True, stop=True)
                    mm.then_inc(s_rel_fl, 1)
                    yield
                yield
                pe.wait_ge(s_hits, 1)
                for n in range(2):
                    if n == 1:
                        pe.wait_ge(s_counts_taken, 1)
                    for b in range(8):
                        mm = nc.tensor.matmul(bank(1, b // 4)[0:M, 128 * (b % 4):128 * (b % 4) + 128],
                                              hits[:, M * (8 * n + b):M * (8 * n + b + 1)], upto[:], start=True, stop=True)
                    mm.then_inc(s_plug_rows, 1)
                    yield
                for _ in range(6):
                    yield
                pe.wait_ge(s_we, 16 * 5)
                pe.wait_ge(s_w1, 16 * 6)
                pe.wait_ge(s_late_done, 1)
                yield

            def turn(src, p, done):
                nc.tensor.transpose(bank(p, 0)[:, 0:128], src[:], ident[:]).then_inc(done, 1)

            def project_qkv(l, u, p):
                S = A[l]
                pe.wait_ge(S["xT_ready"], u + 1)
                nc.tensor.matmul(bank(p, 3)[:, 128:256], w_qkv[l][:, 1, :], x_T[p][:], start=True, stop=True)
                nc.tensor.matmul(bank(p, 3)[:, 0:128], w_qkv[l][:, 0, :], x_T[p][:], start=True, stop=True)
                nc.tensor.matmul(bank(p, 3)[:, 256:384], x_T[p][:], w_qkv[l][:, 2, :], start=True,
                                 stop=True).then_inc(S["qkv_ready"], 1)

            def scores(l, u, p, chunks):
                S = A[l]
                q = wide_a[p][:].rearrange("d (h t) -> d h t", h=HEADS)
                for c in chunks:
                    if c == NCH - 1:
                        pe.wait_ge(S["v_ready"], u + 1)
                    pe.wait_ge(S["masked_q_ready"], NCH * u + c + 1)
                    if l == 0:
                        nc.tensor.matmul(bank(p, c), ident16[:], causal16[:].rearrange("k h j -> k (h j)"),
                                         start=True, stop=False, skip_group_check=True)
                    for k in range(4):
                        mm = nc.tensor.matmul(bank(p, c)[:, 128 * k:128 * k + 128], q[:, 4 * c + k, :], k_T[p][:],
                                              start=(l == 1), stop=True, skip_group_check=True)
                    mm.then_inc(S["scores_ready"], 1)

            def turn_probs(l, u, p, chunks):
                S = A[l]
                pr = wide_p[p][:].rearrange("q (h k) -> q h k", h=HEADS)
                for c in chunks:
                    pe.wait_ge(S["probs_ready"], NCH * u + c + 1)
                    for k in range(4):
                        mm = nc.tensor.transpose(bank(p, c)[:, 128 * k:128 * k + 128], pr[:, 4 * c + k, :], ident[:])
                    mm.then_inc(S["probs_turned"], 1)

            def mix(l, u, p, g):
                S = A[l]
                pt = wide_t[p][:].rearrange("k (h q) -> k h q", h=HEADS)
                for c in (2 * g, 2 * g + 1):
                    pe.wait_ge(S["probsT_ready"], NCH * u + c + 1)
                    for h in range(4 * c, 4 * c + 4):
                        mm = nc.tensor.matmul(bank(p, g)[:, 0:128], v_exp[p][:, h, :], pt[:, h, :],
                                              start=(h % 8 == 0), stop=(h % 8 == 7))
                mm.then_inc(S["mixed"], 1)

            def attend(l, u, p):
                scores(l, u, p, (0, 1))
                yield
                scores(l, u, p, (2, 3))
                yield
                turn_probs(l, u, p, (0, 1))
                yield
                turn_probs(l, u, p, (2, 3))
                yield
                mix(l, u, p, 0)
                yield
                mix(l, u, p, 1)
                yield
                project(l, u, p)
                yield

            def context(u, p, q=None):
                q = p if q is None else q
                if isinstance(u, int) and u == 0:
                    pe.wait_ge(s_wkv, 16)
                elif isinstance(u, int) and u == 1:
                    pe.wait_ge(X["v_copied"], 1)
                else:
                    pe.wait_ge(A[1]["probsT_ready"], NCH * (u - SLOTS) + NCH)
                pe.wait_ge(s_c[p], 8 * (u - p) + 16)
                for c in range(2):
                    mm = nc.tensor.transpose(bank(q, 3)[:, 128 * c:128 * c + M], c_in[p][:, 128 * c:128 * c + 128],
                                             ident[0:M, 0:M])
                mm.then_inc(X["c_turned"], 1)
                yield
                pe.wait_ge(X["cT_ready"], u + 1)
                for c in range(XC):
                    for k in range(2):
                        mm = nc.tensor.matmul(bank(q, 2 + c // 4)[:, 128 * (c % 4):128 * (c % 4) + M],
                                              xw_kv[:, k, 128 * c:128 * c + 128], c_T[p][:, k, :],
                                              start=(k == 0), stop=(k == 1))
                mm.then_inc(X["k_ready"], 1)
                yield
                pe.wait_ge(X["k_copied"], u + 1)
                for n in range(2):
                    for k in range(2):
                        mm = nc.tensor.matmul(bank(q, 2 + n)[0:M, :], c_T[p][:, k, :],
                                              xw_kv[:, k, 1024 + 512 * n:1536 + 512 * n],
                                              start=(k == 0), stop=(k == 1))
                mm.then_inc(X["v_ready"], 1)
                yield

            def project(l, u, p):
                S = A[l]
                pe.wait_ge(S["mixed_ready"], 2 * u + 2)
                nc.tensor.matmul(bank(p, 1)[:, 0:128], att_T[p][:], w_proj[l][:], start=True,
                                 stop=True).then_inc(S["projected"], 1)

            def first_half(u, p):
                pe.wait_ge(s_slot, u + 1)
                pe.wait_ge(s_x[p], 8 * (u - p) + 16)
                turn(x_in[p], p, A[0]["x_turned"])
                yield
                if not (isinstance(u, int) and u == 0):
                    pe.wait_ge(X["v_copied"], u + 1)
                project_qkv(0, u, p)
                yield
                yield from attend(0, u, p)
                pe.wait_ge(s_x1, u + 1)
                turn(x_1[p], p, X["x_turned"])
                yield
                if isinstance(u, int) and u == 0:
                    pe.wait_ge(s_wx, 16 * 4)
                    pe.wait_ge(s_nullv, 64)
                    pe.wait_ge(X["v_copied"], 1)
                pe.wait_ge(X["xT_ready"], u + 1)
                for c in range(XC):
                    mm = nc.tensor.matmul(bank(p, c // 4)[:, 128 * (c % 4):128 * (c % 4) + 128],
                                          xw_q[:, 128 * c:128 * c + 128], x_T[p][:], start=True, stop=True)
                mm.then_inc(X["q_ready"], 1)
                yield
                pe.wait_ge(X["q_copied"], u + 1)
                for c in range(XC):
                    mm = nc.tensor.matmul(bank(p, c // 2)[:, 2 * MK * (c % 2):2 * MK * (c % 2 + 1)],
                                          wide_a[p][:, 128 * c:128 * c + 128],
                                          k_exp[p][:, c].rearrange("d g k -> d (g k)"), start=True, stop=True)
                    if c % 4 == 3:
                        mm.then_inc(X["scores_ready"], 1)
                        yield
                yield
                yield
                pr = wide_p[p][:, 0:XH * MK].rearrange("q (h k) -> q h k", h=XH)
                for n in range(2):
                    pe.wait_ge(X["normalized"], 2 * u + n + 1)
                    for h in range(8 * n, 8 * n + 8):
                        mm = nc.tensor.transpose(bank(p, h // 4)[0:MK, 128 * (h % 4):128 * (h % 4) + 128],
                                                 pr[:, h, :], ident[:])
                    mm.then_inc(X["probs_turned"], 1)
                    yield
                pt = wide_t[p][:].rearrange("k (h q) -> k h q", h=XH)
                for n in range(2):
                    pe.wait_ge(X["probsT_ready"], 2 * u + n + 1)
                    for c in range(4 * n, 4 * n + 4):
                        for g in range(2):
                            mm = nc.tensor.matmul(bank(p, c // 4)[:, 128 * (c % 4):128 * (c % 4) + 128],
                                                  v_z[p][:, 2 * c + g, :], pt[0:MK, 2 * c + g, :],
                                                  start=(g == 0), stop=(g == 1))
                    mm.then_inc(X["mixed"], 1)
                yield
                for n in range(2):
                    pe.wait_ge(X["mixed_copied"], 2 * u + n + 1)
                    for c in range(4 * n, 4 * n + 4):
                        mm = nc.tensor.matmul(bank(p, 2)[:, 0:128], wide_a[p][:, 128 * c:128 * c + 128],
                                              xw_out[:, c, :], start=(c == 0), stop=(c == XC - 1))
                mm.then_inc(X["projected"], 1)
                yield
                yield

            def second_half(u, p):
                pe.wait_ge(s_x2, u + 1)
                turn(x_2[p], p, F["x_turned"])
                yield
                pe.wait_ge(F["xT_ready"], u + 1)
                nc.tensor.matmul(bank(p, 3)[:, 0:E], x_T[p][:], w_r[:], start=True,
                                 stop=True).then_inc(F["logits_ready"], 1)
                for k in range(E * HC):
                    if k == 12:
                        pe.wait_ge(F["max_ready"], u + 1)
                    mm = nc.tensor.matmul(bank(p, k // 4)[:, 128 * (k % 4):128 * (k % 4) + 128],
                                          w_1[:, k // HC, 128 * (k % HC):128 * (k % HC) + 128], x_T[p][:],
                                          start=True, stop=True)
                    if k % 4 == 3:
                        mm.then_inc(F["hidden_ready"], 1)
                yield
                for e in range(E):
                    if e % 2 == 0:
                        pe.wait_ge(F["relu_odd" if e // 2 % 2 else "relu_even"], 2 * u + e // 4 + 1)
                    for j in range(HC):
                        mm = nc.tensor.matmul(bank(p, e // 4)[:, 128 * (e % 4):128 * (e % 4) + 128],
                                              wide_a[p][:, 128 * (HC * e + j):128 * (HC * e + j) + 128],
                                              w_2[:, e, j, :], start=(j == 0), stop=(j == HC - 1))
                    if e % 4 == 3:
                        mm.then_inc(F["outputs_ready"], 1)
                pe.wait_ge(F["gate_ready"], u + 1)
                nc.tensor.transpose(bank(p, 2)[0:E, 0:128], w_one[p][:], ident[:]).then_inc(F["gate_turned"], 1)
                yield
                pe.wait_ge(F["gateT_ready"], u + 1)
                nc.tensor.matmul(bank(p, 3)[:, 0:128], w_oneT[p][:], b_2[:], start=True,
                                 stop=True).then_inc(F["weighted"], 1)
                yield
                pe.wait_ge(G["rows_ready"], u + 1)
                pe.wait_ge(G["plug_taken"], u + 1)
                nc.tensor.matmul(bank(p, 2)[:, 0:128], plug_now[p], c_in[p][:, 0:128], start=True,
                                 stop=True).then_inc(G["row_product"], 1)
                pe.wait_ge(s_x3, u + 1)
                turn(x_3[p], p, A[1]["x_turned"])
                yield
                project_qkv(1, u, p)
                yield
                pe.wait_ge(G["scan_taken"], u + 1)
                yield from attend(1, u, p)
                pe.wait_ge(s_x4, u + 1)
                turn(x_4[p], p, G["x_turned"])
                yield
                pe.wait_ge(G["xT_ready"], u + 1)
                nc.tensor.matmul(bank(p, 1)[:, 0:128], x_T[p][:], w_inT[:], start=True,
                                 stop=True).then_inc(G["input_product"], 1)
                yield
                pe.wait_ge(s_x5, u + 1)
                turn(x_5[p][:, 0:128], p, s_x5T)
                nc.tensor.matmul(bank(p, 1)[:, 0:129], x_5[p][:, 0:128], x_5[p][:], start=True,
                                 stop=True).then_inc(G["summed"], 1)
                yield

            def turn_weights():
                pe.wait_ge(s_pk, 64)
                pe.wait_ge(s_slot, B + 1)
                yield
                for k in range(2 * PH):
                    mm = nc.tensor.transpose(bank(0, k // 4)[:, 128 * (k % 4):128 * (k % 4) + 128], pk_wq[:, k, :],
                                             ident[:])
                mm.then_inc(s_turn, 1)
                for _ in range(3):
                    yield
                pe.wait_ge(s_turn, 2)
                for half in range(2):
                    for t in range(2):
                        nc.tensor.transpose(bank(0, 0)[:, 256 * half + 128 * t:256 * half + 128 * t + 128],
                                            pk_keys[:, t, KD * half:KD * half + KD], ident[:])
                for k in range(NE // 128):
                    mm = nc.tensor.transpose(bank(0, 1 + k // 4)[:, 128 * (k % 4):128 * (k % 4) + 128],
                                             pk_down[:, k, :], ident[:])
                mm.then_inc(s_turn, 1)
                while True:
                    yield

            steps(pe, PE_FIRST_ORDER, PE_ORDER, context, first_half, second_half, late_setup, turn_weights)

        @block.scalar
        def _(act):
            weights_dma(act, [
                (rel_ext[:, 128:255], a["rel_rev"], s_rel),
                (plen_i, a["mask_BxS2_if0"], s_plen),
                (w_in[:], a["L1_xattn_W_in"], s_wp),
                (b_in[:], pbc(a["L1_xattn_b_in"]), s_wp),
                (g_init[:], pbc(a["L1_xattn_g_init"][0:128]), s_wp),
            ])
            def late_setup():
                for _ in range(9):
                    yield
                act.wait_ge(s_ev, 1)
                nc.scalar.activation(plug_T[:], plug_T[:], ACT.Exp, scale=-DT).then_inc(s_ev, 1)
                for _ in range(6):
                    yield
                act.wait_ge(s_late_done, 1)
                yield

            def copy_turned(u, p, ready, done):
                act.wait_ge(ready, u + 1)
                nc.scalar.copy(x_T[p][:], bank(p, 0)[:, 0:128]).then_inc(done, 1)

            def exponentials(l, u, p, chunks):
                for c in chunks:
                    act.wait_ge(A[l]["shifted"], NCH * u + c + 1)
                    nc.scalar.activation(wide_p[p][:, 512 * c:512 * c + 512], wide_p[p][:, 512 * c:512 * c + 512],
                                         ACT.Exp).then_inc(A[l]["probs_ready"], 1)

            def copy_probs(l, u, p, chunks):
                for c in chunks:
                    act.wait_ge(A[l]["probs_turned"], NCH * u + c + 1)
                    nc.scalar.copy(wide_t[p][:, 512 * c:512 * c + 512], bank(p, c)).then_inc(A[l]["probsT_ready"], 1)

            def attend(l, u, p):
                exponentials(l, u, p, (0, 1))
                yield
                exponentials(l, u, p, (2, 3))
                yield
                copy_probs(l, u, p, (0, 1))
                yield
                copy_probs(l, u, p, (2, 3))
                yield
                yield
                yield
                yield

            def context(u, p, q=None):
                q = p if q is None else q
                if isinstance(u, int) and u == 1:
                    act.wait_ge(s_setup_done, 2)
                act.wait_ge(X["c_turned"], u + 1)
                nc.scalar.copy(c_T[p][:], bank(q, 3)[:, 0:256].rearrange("d (c k) -> d c k", c=2)[:, :, 0:M]
                               ).then_inc(X["cT_ready"], 1)
                yield
                act.wait_ge(X["k_ready"], u + 1)
                for hp in range(2):
                    r = slice(64 * hp, 64 * hp + 64)
                    ins = nc.scalar.copy(k_exp[p][r, :, hp, 0:M],
                                         ps[r, 4 * q + 2:4 * q + 4, :].rearrange("d b (c k) -> d (b c) k", k=128)
                                         [:, :, 0:M])
                ins.then_inc(X["k_copied"], 1)
                yield
                act.wait_ge(X["v_ready"], u + 1)
                for hp in range(2):
                    ins = nc.scalar.copy(
                        v_z[p][0:M].rearrange("k (c g) d -> k c g d", g=2)[:, :, hp, 64 * hp:64 * hp + 64],
                        ps[0:M, 4 * q + 2:4 * q + 4, :].rearrange("k b (c g d) -> k (b c) g d", g=2, d=64)[:, :, hp, :])
                ins.then_inc(X["v_copied"], 1)
                yield

            def first_half(u, p):
                copy_turned(u, p, A[0]["x_turned"], A[0]["xT_ready"])
                yield
                yield
                yield from attend(0, u, p)
                copy_turned(u, p, X["x_turned"], X["xT_ready"])
                yield
                act.wait_ge(X["q_ready"], u + 1)
                nc.scalar.copy(wide_a[p][:, 0:1024].rearrange("d (b n) -> d b n", b=2),
                               ps[:, 4 * p:4 * p + 2, :]).then_inc(X["q_copied"], 1)
                yield
                half = XH * MK // 2
                for n in range(2):
                    act.wait_ge(X["shifted"], 2 * u + n + 1)
                    nc.scalar.activation(wide_p[p][:, half * n:half * n + half], wide_p[p][:, half * n:half * n + half],
                                         ACT.Exp, scale=float(XDH) ** -0.5).then_inc(X["probs_ready"], 1)
                    yield
                yield
                yield
                for n in range(2):
                    act.wait_ge(X["probs_turned"], 2 * u + n + 1)
                    nc.scalar.copy(wide_t[p][0:MK, 1024 * n:1024 * n + 1024].rearrange("k (b n) -> k b n", b=2),
                                   ps[0:MK, 4 * p + 2 * n:4 * p + 2 * n + 2, :]).then_inc(X["probsT_ready"], 1)
                    yield
                for n in range(2):
                    act.wait_ge(X["mixed"], 2 * u + n + 1)
                    nc.scalar.copy(wide_a[p][:, 512 * n:512 * n + 512], bank(p, n)).then_inc(X["mixed_copied"], 1)
                yield
                yield
                yield

            def second_half(u, p):
                copy_turned(u, p, F["x_turned"], F["xT_ready"])
                nc.scalar.activation(squares[p][0:M, :], c_in[p][:], ACT.Square,
                                     accum_out=sm[p][0:M, 5:6]).then_inc(G["row_squares"], 1)
                yield
                act.wait_ge(F["max_ready"], u + 1)
                nc.scalar.activation(logit_e[p][:], logit[p][:], ACT.Exp, bias=sm[p][:, 0:1],
                                     accum_out=sm[p][:, 1:2]).then_inc(F["exp_ready"], 1)
                for c in range(0, NCH, 2):
                    act.wait_ge(F["hidden_ready"], NCH * u + c + 1)
                    for k in range(4 * c, 4 * c + 4):
                        ins = nc.scalar.activation(wide_a[p][:, 128 * k:128 * k + 128],
                                                   bank(p, c)[:, 128 * (k % 4):128 * (k % 4) + 128], ACT.Relu,
                                                   bias=cols[:, R_B1 + k:R_B1 + k + 1])
                    ins.then_inc(F["relu_even"], 1)
                yield
                act.wait_ge(F["gate_turned"], u + 1)
                nc.scalar.copy(w_oneT[p][:], bank(p, 2)[0:E, 0:128]).then_inc(F["gateT_ready"], 1)
                yield
                yield
                act.wait_ge(G["row_product"], u + 1)
                nc.scalar.copy(scan[p][:], bank(p, 2)[:, 0:128]).then_inc(G["scan_taken"], 1)
                copy_turned(u, p, A[1]["x_turned"], A[1]["xT_ready"])
                yield
                yield
                yield from attend(1, u, p)
                act.wait_ge(s_x4, u + 1)
                nc.scalar.activation(squares[p][:, 0:128], x_4[p][:], ACT.Square,
                                     accum_out=sm[p][:, 4:5]).then_inc(G["x_squares"], 1)
                copy_turned(u, p, G["x_turned"], G["xT_ready"])
                yield
                yield
                act.wait_ge(s_x5T, u + 1)
                nc.scalar.copy(one(x5T, u), bank(p, 0)[:, 0:128].unsqueeze(1)).then_inc(s_x5T_ready, 1)
                yield

            def turn_weights():
                yield
                act.wait_ge(s_turn, 1)
                nc.scalar.copy(wide_p[0].rearrange("d (b n) -> d b n", b=4), banks(0)).then_inc(s_turn, 1)
                for _ in range(3):
                    yield
                act.wait_ge(s_turn, 3)
                nc.scalar.copy(wide_t[0][:, 0:1536].rearrange("d (b n) -> d b n", b=3), banks(0)[:, 0:3, :])
                while True:
                    yield

            steps(act, ACT_FIRST_ORDER, ACT_ORDER, context, first_half, second_half, late_setup, turn_weights)

        @block.vector
        def _(dve):
            V = nc.vector
            n = [0]

            def link(ins):
                n[0] += 1
                ins.then_inc(s_setup, 1)
                dve.wait_ge(s_setup, n[0])

            def zeros_and_ones(p):
                V.memset(k_exp[p][:], 0.0)
                link(V.memset(v_exp[p][:], 0.0))
                for h in range(HEADS):
                    V.memset(v_exp[p][:, h, 64 + DH * (h % 8):64 + DH * (h % 8) + DH], 1.0)
                V.memset(x_5[p][:], 1.0)

            def null_keys(p):
                for hp in range(2):
                    r = slice(64 * hp, 64 * hp + 64)
                    link(V.tensor_copy(k_exp[p][r, :, hp, M:MK],
                                       bcast(cols[r, R_NULLK:R_NULLK + 1].unsqueeze(1), [64, XC, 1])))

            V.memset(v_z[0][:], 0.0).then_inc(s_vz, 1)
            zeros_and_ones(0)
            dve.wait_ge(s_rel, 16)
            V.tensor_copy(rel_ext[:, 0:128], bcast(rel_ext[:, 128:129], [HEADS, 128])).then_inc(s_rel_ext, 1)
            dve.wait_ge(s_plen, 16)
            plen = wide_t[1][0:B, 800:800 + M]
            wrap = wide_t[1][0:B, 880:880 + M]
            zero = wide_t[1][0:B, 960:960 + M]
            V.memset(zero, 0.0)
            link(V.tensor_copy(plen, plen_i))
            link(V.tensor_tensor_scan(edge, plen, zero, 0.0, ALU.add, ALU.add))
            link(V.tensor_scalar(edge, edge, 1.0, None, ALU.subtract))
            link(V.tensor_scalar(wrap, edge, 0.0, float(T), ALU.is_lt, ALU.mult))
            V.tensor_tensor(edge, edge, wrap, ALU.add).then_inc(s_plug, 1)
            V.memset(v_z[1][:], 0.0).then_inc(s_vz, 1)
            V.memset(cov[:], 0.0)
            link(V.memset(veps[:], 1.0))
            dve.wait_ge(s_rowsT, 1)
            link(V.tensor_copy(cols[:], ps[:, 0, 0:NROWS]))
            dve.wait_ge(s_winT, 1)
            link(V.tensor_scalar(w_inT[:], ps[:, 1, 0:128], cols[:, R_GRES:R_GRES + 1], None, ALU.mult))
            null_keys(0)
            dve.wait_ge(s_w0, 16 * 4)
            dve.wait_ge(s_const, 2)
            V.memset(z[0][:, 0:1], 0.0).then_inc(s_setup_done, 1)
            for p in range(SLOTS):
                V.memset(z2[p][:, 0:1], 0.0).then_inc(s_slot, 1)

            def late_setup():
                for _ in range(2):
                    yield
                zeros_and_ones(1)
                yield
                null_keys(1)
                V.memset(z[1][:, 0:1], 0.0).then_inc(s_setup_done, 1)
                yield
                for n in range(2):
                    dve.wait_ge(s_rel_fl, n + 1)
                    V.tensor_copy(rel_bias[:, 8 * n:8 * n + 8, :].rearrange("i (b h) j -> i b (h j)", b=2),
                                  ps[:, 4:6, :]).then_inc(s_rel_taken, 1)
                    yield
                dve.wait_ge(s_const, 3)
                dve.wait_ge(s_plug_in, 16)
                link(V.tensor_scalar(hits, hits, iota_col[:, 0:1], None, ALU.is_equal))
                found = sums[1][:, 0:B]
                link(V.tensor_reduce(found, hits.rearrange("t (b m) -> t b m", b=B), AX.X, ALU.max))
                V.tensor_copy(hits.rearrange("t (b m) -> t b m", b=B), bcast(found.unsqueeze(2), [128, B, M])
                              ).then_inc(s_hits, 1)
                yield
                flat = plug_T[:].rearrange("k (c b) t -> k c (b t)", c=4)
                sign = wide_p[1][0:M, :].rearrange("k (c n) -> k c n", c=4)
                for n in range(2):
                    dve.wait_ge(s_plug_rows, n + 1)
                    V.tensor_scalar(flat[:, 2 * n:2 * n + 2, :], ps[0:M, 4:6, :], 1.0, 0.0, ALU.subtract, ALU.max
                                    ).then_inc(s_counts_taken, 1)
                    yield
                dve.wait_ge(s_counts_taken, 2)
                link(V.tensor_scalar(flat, flat, float(M - 1), iota_col[0:M, 0:1], ALU.min, ALU.subtract))
                link(V.tensor_scalar(sign, flat, 0.0, None, ALU.is_ge))
                V.tensor_scalar(flat, flat, 0.0, None, ALU.max).then_inc(s_ev, 1)
                yield
                dve.wait_ge(s_ev, 2)
                V.tensor_tensor(flat, flat, sign, ALU.mult)
                for _ in range(5):
                    yield
                dve.wait_ge(s_we, 16 * 5)
                dve.wait_ge(s_w1, 16 * 6)
                dve.wait_ge(s_wp, 16 * 3)
                V.tensor_scalar(g_init[:], g_init[:], BCOEF, None, ALU.mult).then_inc(s_late_done, 1)
                yield

            state = {}
            expected = [0, FIRST_LINKS] + 3 * [FIRST_LINKS + SECOND_LINKS]

            def settle():
                V.memset(spare[:], 0.0)

            def mark(ins):
                state["links"] += 1
                ins.then_inc(s_chain, 1)
                return state["base"] + state["links"]

            def chain(ins):
                count = mark(ins)
                dve.wait_ge(s_chain, count)

            def begin(step):
                assert state.get("links", expected[0]) == expected.pop(0), state["links"]
                state.update(base=0 if isinstance(step, int) and step == 0
                             else (FIRST_LINKS + SECOND_LINKS) * (step - 1) + FIRST_LINKS, links=0)

            def norm_begin(k, p, zp, eps):
                c = RSTDS * p + k
                chain(V.bn_stats(stats[:, c, :], zp))
                settle()
                chain(V.bn_aggr(mv[:, c, :], stats[:, c, :]))
                V.tensor_scalar(veps[:, c:c + 1], mv[:, c, 1:2], eps, None, ALU.add).then_inc(s_var[half_of(k)], 1)

            def norm_end(k, u, p, outp, zp):
                c = RSTDS * p + k
                dve.wait_ge(s_rstd[half_of(k)], root_count(k, u))
                return V.tensor_scalar(outp, zp, mv[:, c, 0:1], rstd[:, c:c + 1], ALU.subtract, ALU.mult)

            def take_qkv(l, u, p):
                S = A[l]
                bq = R_BQK0 if l == 0 else R_BQK1
                dve.wait_ge(S["qkv_ready"], u + 1)
                V.tensor_scalar(k_T[p][:], bank(p, 3)[:, 128:256], cols[:, bq + 1:bq + 2], None, ALU.add)
                for c in range(NCH):
                    V.scalar_tensor_tensor(
                        out=wide_a[p][:, 512 * c:512 * c + 512].rearrange("d (h t) -> d h t", h=4),
                        in0=bcast(bank(p, 3)[:, 0:128].unsqueeze(1), [128, 4, 128]),
                        scalar=cols[:, bq:bq + 1],
                        in1=bcast(head_mask[:, 4 * c:4 * c + 4].unsqueeze(2), [128, 4, 128]),
                        op0=ALU.add, op1=ALU.mult).then_inc(S["masked_q_ready"], 1)
                    if c == 0:
                        V.tensor_tensor(
                            v_blocks(p),
                            bank(p, 3)[:, 256:384].rearrange("k (g h d) -> k g h d", g=2, h=8),
                            b_v[l][:].rearrange("k (g h d) -> k g h d", g=2, h=8), ALU.add).then_inc(S["v_ready"], 1)

            def shift(l, u, p, chunks):
                S = A[l]
                late = []
                for c in chunks:
                    dve.wait_ge(S["scores_ready"], NCH * u + c + 1)
                    sc = bank(p, c).rearrange("q (h k) -> q h k", h=4)
                    if l == 1:
                        pr = wide_p[p][:, 512 * c:512 * c + 512].rearrange("q (h k) -> q h k", h=4)
                        chain(V.tensor_tensor(pr, sc, rel_bias[:, 4 * c:4 * c + 4, :], ALU.add))
                        sc = pr
                    late.append((c, sc, mark(V.tensor_reduce(mx[p][:, 4 * c:4 * c + 4], sc, AX.X, ALU.max))))
                for c, sc, count in late:
                    dve.wait_ge(s_chain, count)
                    V.tensor_tensor(wide_p[p][:, 512 * c:512 * c + 512].rearrange("q (h k) -> q h k", h=4), sc,
                                    bcast(mx[p][:, 4 * c:4 * c + 4].unsqueeze(2), [128, 4, 128]),
                                    ALU.subtract).then_inc(S["shifted"], 1)

            def divide(l, u, p, g):
                S = A[l]
                dve.wait_ge(S["mixed"], 2 * u + g + 1)
                chain(V.reciprocal(r_z[p][:, g, :], ps[64:128, 4 * p + g, 0:128]))
                V.tensor_tensor(att_T[p][64 * g:64 * g + 64, :], ps[0:64, 4 * p + g, 0:128], r_z[p][:, g, :],
                                ALU.mult).then_inc(S["mixed_ready"], 1)

            def attend(l, u, p, k):
                shift(l, u, p, (0, 1))
                yield
                shift(l, u, p, (2, 3))
                yield
                yield
                yield
                divide(l, u, p, 0)
                yield
                divide(l, u, p, 1)
                yield
                add_residual(l, u, p, k)
                yield

            def context(u, p, q=None):
                for _ in range(3):
                    yield

            def add_residual(l, u, p, k):
                dve.wait_ge(A[l]["residual_ready"], u + 1)
                dve.wait_ge(A[l]["projected"], u + 1)
                chain(V.tensor_tensor(z[p][:], bank(p, 1)[:, 0:128], z2[p][:], ALU.add))
                norm_begin(k, p, z[p][:], LN_EPS)

            def first_half(u, p):
                yield
                dve.wait_ge(s_slot, u + 1)
                take_qkv(0, u, p)
                yield
                yield from attend(0, u, p, ROOT_1)
                norm_end(ROOT_1, u, p, x_1[p][:], z[p][:]).then_inc(s_x1, 1)
                yield
                yield
                for n in range(2):
                    dve.wait_ge(X["scores_ready"], 2 * u + n + 1)
                    sc = ps[:, 4 * p + 2 * n:4 * p + 2 * n + 2, 0:4 * MK].rearrange("q b (h k) -> q b h k", h=4)
                    pr = wide_p[p][:, 8 * MK * n:8 * MK * (n + 1)].rearrange("q (b h k) -> q b h k", b=2, h=4)
                    m = mx[p][:, 8 * n:8 * n + 8].rearrange("q (b h) -> q b h", b=2)
                    chain(V.tensor_reduce(m, sc, AX.X, ALU.max))
                    V.tensor_tensor(pr, sc, bcast(m.unsqueeze(3), [128, 2, 4, MK]), ALU.subtract
                                    ).then_inc(X["shifted"], 1)
                    yield
                for n in range(2):
                    dve.wait_ge(X["probs_ready"], 2 * u + n + 1)
                    pr = wide_p[p][:, 8 * MK * n:8 * MK * (n + 1)].rearrange("q (h k) -> q h k", h=8)
                    chain(V.tensor_reduce(sums[p][:, 8 * n:8 * n + 8], pr, AX.X, ALU.add))
                    chain(V.reciprocal(rsum[p][:, 8 * n:8 * n + 8], sums[p][:, 8 * n:8 * n + 8]))
                    V.tensor_tensor(pr, pr, bcast(rsum[p][:, 8 * n:8 * n + 8].unsqueeze(2), [128, 8, MK]),
                                    ALU.mult).then_inc(X["normalized"], 1)
                    yield
                yield
                yield
                yield
                dve.wait_ge(X["projected"], u + 1)
                chain(V.tensor_copy(z[p][:], bank(p, 2)[:, 0:128]))
                norm_begin(ROOT_X, p, z[p][:], XLN_EPS)
                yield
                if isinstance(u, int) and u == 0:
                    dve.wait_ge(s_wx, 16 * 4)
                chain(norm_end(ROOT_X, u, p, z[p][:], z[p][:]))
                chain(V.tensor_tensor(z[p][:], z[p][:], x_scale[:], ALU.mult))
                dve.wait_ge(X["residual_ready"], u + 1)
                chain(V.tensor_tensor(z[p][:], z[p][:], z2[p][:], ALU.add))
                norm_begin(ROOT_2, p, z[p][:], LN_EPS)
                yield

            def second_half(u, p):
                norm_end(ROOT_2, u, p, x_2[p][:], z[p][:]).then_inc(s_x2, 1)
                yield
                dve.wait_ge(F["logits_ready"], u + 1)
                chain(V.tensor_tensor(logit[p][:], bank(p, 3)[:, 0:E], b_r[:], ALU.add))
                settle()
                chain(V.max(top8[p][:], logit[p][:]))
                settle()
                V.max_index(top8i[p][:], top8[p][:], logit[p][:])
                V.tensor_scalar(sm[p][:, 0:1], top8[p][:, 0:1], -1.0, None, ALU.mult).then_inc(F["max_ready"], 1)
                for c in range(1, NCH, 2):
                    dve.wait_ge(F["hidden_ready"], NCH * u + c + 1)
                    for k in range(4 * c, 4 * c + 4):
                        ins = V.tensor_scalar(wide_a[p][:, 128 * k:128 * k + 128],
                                              bank(p, c)[:, 128 * (k % 4):128 * (k % 4) + 128],
                                              cols[:, R_B1 + k:R_B1 + k + 1], 0.0, ALU.add, ALU.max)
                    ins.then_inc(F["relu_odd"], 1)
                dve.wait_ge(G["row_squares"], u + 1)
                k = RSTDS * p + ROOT_ROWS
                V.tensor_scalar(veps[0:M, k:k + 1], sm[p][0:M, 5:6], 1.0 / CTX, RMS_EPS, ALU.mult,
                                ALU.add).then_inc(s_var[1], 1)
                dve.wait_ge(F["exp_ready"], u + 1)
                V.tensor_copy(sm[p][:, 2:3], top8i[p][:, 0:1])
                chain(V.reciprocal(sm[p][:, 3:4], sm[p][:, 1:2]))
                V.tensor_scalar(w_one[p][:], iota8[:], sm[p][:, 2:3], sm[p][:, 3:4], ALU.is_equal,
                                ALU.mult).then_inc(F["gate_ready"], 1)
                yield
                dve.wait_ge(F["gate_ready"], u + 1)
                for n in range(2):
                    dve.wait_ge(F["outputs_ready"], 2 * u + n + 1)
                    count = mark(V.tensor_tensor(
                        wide_p[p][:, 512 * n:512 * n + 512].rearrange("t (e d) -> t e d", e=4),
                        bank(p, n).rearrange("t (e d) -> t e d", e=4),
                        bcast(w_one[p][:, 4 * n:4 * n + 4].unsqueeze(2), [128, 4, 128]), ALU.mult))
                dve.wait_ge(s_chain, count)
                chain(V.tensor_reduce(z[p][:], wide_p[p][:, 0:1024].rearrange("t (e d) -> t d e", e=E), AX.X, ALU.add))
                chain(V.tensor_tensor(z[p][:], z[p][:], x_2[p][:], ALU.add))
                yield
                dve.wait_ge(F["weighted"], u + 1)
                chain(V.tensor_tensor(z[p][:], bank(p, 3)[:, 0:128], z[p][:], ALU.add))
                norm_begin(ROOT_3, p, z[p][:], LN_EPS)
                yield
                norm_end(ROOT_3, u, p, x_3[p][:], z[p][:]).then_inc(s_x3, 1)
                yield
                take_qkv(1, u, p)
                yield
                yield from attend(1, u, p, ROOT_4)
                norm_end(ROOT_4, u, p, x_4[p][:], z[p][:]).then_inc(s_x4, 1)
                dve.wait_ge(G["x_squares"], u + 1)
                k = RSTDS * p + ROOT_IN
                V.tensor_scalar(veps[:, k:k + 1], sm[p][:, 4:5], 1.0 / D, RMS_EPS, ALU.mult,
                                ALU.add).then_inc(s_var[1], 1)
                yield
                dve.wait_ge(G["residual_ready"], u + 1)
                dve.wait_ge(G["input_product"], u + 1)
                dve.wait_ge(s_rstd[1], root_count(ROOT_IN, u))
                chain(V.scalar_tensor_tensor(out=z[p][:], in0=bank(p, 1)[:, 0:128], scalar=rstd[:, k:k + 1],
                                             in1=z2[p][:], op0=ALU.mult, op1=ALU.add))
                norm_begin(ROOT_5, p, z[p][:], LN_EPS)
                yield
                norm_end(ROOT_5, u, p, x_5[p][:, 0:128], z[p][:]).then_inc(s_x5, 1)
                dve.wait_ge(G["summed"], u + 1)
                chain(V.tensor_tensor(cov[:], cov[:], bank(p, 1)[:, 0:129], ALU.add))
                dve.wait_ge(s_x5T_ready, u + 1)
                dve.wait_ge(G["x5_kept"], u + 1)
                V.memset(sums[p][:, 0:1], 0.0).then_inc(s_slot, 1)
                yield

            def turn_weights():
                while True:
                    yield

            steps(dve, DVE_FIRST_ORDER, DVE_ORDER, context, first_half, second_half, late_setup, turn_weights, begin)

        first.close()
        loop1.close()
        product_keys(nc, ctx, ps, out, dict(
            ident=ident, ones=ones_col, neg_half=neg_half, cols=cols, spare=spare, x5=x5, x5T=x5T, cov=cov,
            wqT=wqT, keys_downT=keys_downT,
            w_q=pk_wq, keys=pk_keys, down=pk_down, up=pk_up, loaded=s_pk))


def product_keys(nc, ctx, ps, out, c):
    ident, ones, cols, x5, x5T, cov = c["ident"], c["ones"], c["cols"], c["x5"], c["x5T"], c["cov"]
    spare = c["spare"]
    N = B * T
    SEG = NK + TOP
    BUFS = 4
    MIX, GELU, SIM, OUT = 0, 4, 6, 7
    FOLD_PARTS = [slice(0, 6), slice(6, 12), slice(12, 2 * PH)]
    FOLD_BANKS = [0, 1, 2, 3, 6, 7]

    def sb(name, shape, dt=F32):
        return ctx.enter_context(nc.sbuf_tensor(name, shape, dt))

    def pair(name, shape, dt=F32):
        return [sb(f"{name}{p}", shape, dt) for p in range(SLOTS)]

    def sem(name):
        return ctx.enter_context(nc.semaphore(name))

    wqT = c["wqT"]
    keysT = c["keys_downT"][:, 0:2 * PH * NK].rearrange("d (r k) -> d r k", k=NK)
    downT = c["keys_downT"][:, 2 * PH * NK:2 * PH * NK + NE]
    covn = sb("covn", [128, 129])
    mean_row = sb("mean_row", [1, 128])
    wu = sb("wu", [128, 2 * PH, KD])
    fold = sb("fold", [128, 4, 2 * PH])
    means = sb("means", [128, 2 * PH])
    keys_s = sb("keys_s", [128, 2 * PH, NK])
    keys_b = sb("keys_b", [128, 2 * PH, NK])
    w_sim = sb("w_sim", [128, 512])
    b_sim = sb("b_sim", [128, 512])
    xs = pair("xs", [128, 128])
    act_T = pair("act_T", [128, NE])
    halves = pair("halves", [128, 2 * PH, SEG])
    cand = pair("cand", [128, PH, TOP * TOP])
    mxs = pair("mxs", [128, 2 * PH])
    best = pair("best", [128, PH, TOP])
    total = pair("total", [128, PH])
    inv = pair("inv", [128, PH])
    diag = pair("diag", [128, PH, 128])
    outer = [sb(f"outer{k}", [128, NE]) for k in range(BUFS)]
    kept = [sb(f"kept{k}", [128, NE]) for k in range(BUFS)]
    mixT = pair("mixT", [128, NE])
    z = pair("fz", [128, 128])
    y = pair("fy", [128, 128])
    stats = sb("fstats", [128, SLOTS, 6])
    mv = sb("fmv", [128, SLOTS, 2])
    veps = sb("fveps", [128, SLOTS])
    rstd = sb("frstd", [128, SLOTS])

    s_mean = sem("pk_mean_ready")
    s_meanT = sem("pk_mean_turned")
    s_mrow = sem("pk_mean_row_ready")
    s_outer = sem("pk_mean_product_ready")
    s_covc = sem("pk_covariance_ready")
    s_u = sem("pk_covariance_times_weights")
    s_veps = sem("pk_variance_copied")
    s_root = sem("pk_root_ready")
    s_ks = sem("pk_scaled_keys_ready")
    s_fold = sem("pk_folded_weights_ready")
    s_folded = sem("pk_folded_weights_copied")
    s_mid = sem("pk_fold_chain")
    s_xs = sem("score_x_copied")
    s_sim = sem("half_scores_ready")
    s_biased = sem("half_scores_taken")
    s_gp = sem("expert_products_ready")
    s_g = sem("gelu_ready")
    s_simc = sem("half_scores_shifted")
    s_exp = sem("half_exps_ready")
    s_cut = sem("cut_ready")
    s_diag = sem("diagonals_ready")
    s_pr = sem("outer_product_ready")
    s_kept = sem("largest_kept")
    s_mixed = sem("kept_products_used")
    s_mixT = sem("mix_ready")
    s_y = sem("experts_summed")
    s_v = sem("final_variance_ready")
    s_r = sem("final_root_ready")
    s_fin = sem("result_ready")
    s_out = [sem(f"result{p}_stored") for p in range(SLOTS)]
    s_ch = sem("final_vector_chain")

    with nc.Block() as block:

        @block.sync
        def _(sp):
            with sp.Fori(0, ROUNDS) as i:
                for p in range(SLOTS):
                    u = SLOTS * i + p
                    sp.wait_ge(s_fin, u + 1)
                    sp.dma_start(out[bass.ds(u, 1)].rearrange("o t d -> t (o d)"), y[p][:]).then_inc(s_out[p], 16)
            for p in range(SLOTS):
                sp.wait_ge(s_out[p], 16 * (ROUNDS + 1))

        @block.tensor
        def _(pe):
            pe.wait_ge(s_mean, 1)
            nc.tensor.transpose(ps[0:1, 7, 0:128], covn[:, 128:129], ident[:]).then_inc(s_meanT, 1)
            pe.wait_ge(s_mrow, 1)
            nc.tensor.matmul(ps[:, 7, 0:128], mean_row[:], mean_row[:], start=True, stop=True).then_inc(s_outer, 1)
            pe.wait_ge(s_covc, 1)
            for k in range(2 * PH):
                mm = nc.tensor.matmul(ps[:, FOLD_BANKS[k // 3], 129 * (k % 3):129 * (k % 3) + 129], c["w_q"][:, k, :],
                                      covn[:], start=True, stop=True)
                if k + 1 in [part.stop for part in FOLD_PARTS]:
                    mm.then_inc(s_u, 1)

            def products(u, p):
                pe.wait_ge(s_xs, u + 1)
                pe.wait_ge(s_g, u + 1)
                for k in range(NE // 128):
                    mm = nc.tensor.matmul(ps[:, GELU + k // 4, 128 * (k % 4):128 * (k % 4) + 128],
                                          downT[:, 128 * k:128 * k + 128], xs[p][:], start=True, stop=True)
                mm.then_inc(s_gp, 1)

            products(0, 0)
            pe.wait_ge(s_ks, 1)
            for k in range(2 * PH):
                mm = nc.tensor.matmul(ps[:, 0, NK * k:NK * k + NK], wqT[:, k, :], keys_s[:, k, :],
                                      start=True, stop=True)
            mm.then_inc(s_fold, 1)
            pe.wait_ge(s_ks, 2)
            nc.tensor.matmul(ps[:, 1, :], ones[:], keys_b[:].rearrange("d r k -> d (r k)"), start=True,
                             stop=True).then_inc(s_fold, 1)

            pe.wait_ge(s_folded, 1)

            def prepare(u, p):
                pe.wait_ge(s_xs, u + 1)
                pe.wait_ge(s_biased, u + 1)
                nc.tensor.matmul(ps[:, SIM, :], xs[p][:], w_sim[:], start=True, stop=True).then_inc(s_sim, 1)
                yield
                if not (isinstance(u, int) and u == 0):
                    products(u, p)
                for _ in range(7):
                    yield

            def mix(u, p):
                for h in range(PH):
                    if h == 0:
                        pe.wait_ge(s_diag, u + 1)
                    pe.wait_ge(s_kept, PH * u + h + 1 + BUFS)
                    for k in range(NE // 128):
                        mm = nc.tensor.matmul(ps[:, MIX + 2 * p + k // 4, 128 * (k % 4):128 * (k % 4) + 128],
                                              kept[h % BUFS][:, 128 * k:128 * k + 128], diag[p][:, h, :],
                                              start=(h == 0 and k % 4 == 0), stop=(h == PH - 1),
                                              skip_group_check=True)
                    mm.then_inc(s_mixed, 1)
                    yield

            def tail(u, p):
                pe.wait_ge(s_mixT, u + 1 + SLOTS)
                for k in range(NE // 128):
                    mm = nc.tensor.matmul(ps[:, OUT, 0:128], mixT[p][:, 128 * k:128 * k + 128],
                                          c["up"][:, k, :], start=(k == 0), stop=(k == NE // 128 - 1))
                mm.then_inc(s_y, 1)
                yield
                yield
                yield

            last_steps(pe, PE_LAST_ORDER, prepare, mix, tail)

        @block.scalar
        def _(act):

            def prepare(u, p):
                nc.scalar.copy(xs[p][:].unsqueeze(1), x5T[:, bass.ds(u, 1), :]).then_inc(s_xs, 1)
                yield
                yield
                act.wait_ge(s_gp, u + 1)
                act.wait_ge(s_mixT, u + 1)
                nc.scalar.activation(act_T[p][:].rearrange("e (b n) -> e b n", b=2), ps[:, GELU:GELU + 2, :],
                                     ACT.Gelu_apprx_tanh).then_inc(s_g, 1)
                yield
                yield
                act.wait_ge(s_simc, u + 1)
                nc.scalar.activation(halves[p][:], halves[p][:], ACT.Exp).then_inc(s_exp, 1)
                yield
                yield
                yield
                act.wait_ge(s_cut, u + 1)
                for h in range(PH):
                    ins = nc.scalar.mul(diag[p][:, h, :], ident[:], inv[p][:, h:h + 1])
                ins.then_inc(s_diag, 1)
                yield

            def mix(u, p):
                for _ in range(PH):
                    yield

            def tail(u, p):
                for _ in range(3):
                    yield

            last_steps(act, ACT_LAST_ORDER, prepare, mix, tail)

        @block.gpsimd
        def _(pool):
            for i, part in enumerate(FOLD_PARTS):
                pool.wait_ge(s_veps, i + 1)
                nc.gpsimd.tensor_tensor(out=fold[:, 1, part], in0=fold[:, 0, part], in1=c["neg_half"][:, part],
                                        op=ALU.pow).then_inc(s_root, 1)

            def prepare(u, p):
                for _ in range(8):
                    yield

            def mix(u, p):
                for h in range(PH):
                    if h == 0:
                        pool.wait_ge(s_exp, u + 1)
                    pool.wait_ge(s_kept, PH * u + h + 1)
                    nc.gpsimd.tensor_tensor(
                        out=outer[h % BUFS][:].rearrange("t (a b) -> t a b", a=NK),
                        in0=bcast(halves[p][:, h, 0:NK].unsqueeze(2), [128, NK, NK]),
                        in1=bcast(halves[p][:, PH + h, 0:NK].unsqueeze(1), [128, NK, NK]),
                        op=ALU.mult).then_inc(s_pr, 1)
                    yield

            def tail(u, p):
                yield
                pool.wait_ge(s_v, u + 1)
                nc.gpsimd.tensor_tensor(out=rstd[:, p:p + 1], in0=veps[:, p:p + 1],
                                        in1=c["neg_half"][:, 0:1], op=ALU.pow).then_inc(s_r, 1)
                yield
                yield

            last_steps(pool, POOL_LAST_ORDER, prepare, mix, tail)

        @block.vector
        def _(dve):
            V = nc.vector
            n = [0]

            def link(ins):
                n[0] += 1
                ins.then_inc(s_mid, 1)
                dve.wait_ge(s_mid, n[0])

            link(V.tensor_scalar(covn[:], cov[:], 1.0 / N, None, ALU.mult))
            V.memset(veps[:], 1.0).then_inc(s_mean, 1)
            V.memset(act_T[0][:, 0:1], 0.0).then_inc(s_g, 1)
            for p in range(SLOTS):
                V.memset(mixT[p][:, 0:1], 0.0).then_inc(s_mixT, 1)
            dve.wait_ge(s_meanT, 1)
            V.tensor_copy(mean_row[:], ps[0:1, 7, 0:128]).then_inc(s_mrow, 1)
            dve.wait_ge(s_outer, 1)
            V.tensor_tensor(covn[:, 0:128], covn[:, 0:128], ps[:, 7, 0:128], ALU.subtract).then_inc(s_covc, 1)
            for i, part in enumerate(FOLD_PARTS):
                dve.wait_ge(s_u, i + 1)
                for k in range(part.start, part.stop, 3):
                    ks = slice(k, min(k + 3, part.stop))
                    m = ps[:, FOLD_BANKS[k // 3], 0:129 * (ks.stop - k)].rearrange("e (k n) -> e k n", n=129)
                    V.tensor_tensor(wu[:, ks, :], m[:, :, 0:128], wqT[:, ks, :], ALU.mult)
                    ins = V.tensor_copy(means[:, ks], m[:, :, 128])
                link(ins)
                link(V.tensor_reduce(fold[:, 0, part], wu[:, part, :], AX.X, ALU.add))
                V.tensor_scalar(fold[:, 0, part], fold[:, 0, part], BN_EPS, None, ALU.add).then_inc(s_veps, 1)
            for k in range(BUFS):
                V.memset(outer[k][:, 0:1], 0.0).then_inc(s_kept, 1)
                V.memset(kept[k][:, 0:1], 0.0).then_inc(s_mixed, 1)
            V.memset(halves[0][:, 0, 0:1], 0.0).then_inc(s_biased, 1)
            for p in range(SLOTS):
                V.memset(y[p][:, 0:1], 0.0).then_inc(s_out[p], 16)
            dve.wait_ge(s_root, len(FOLD_PARTS))
            link(V.tensor_tensor(fold[:, 2, :], fold[:, 1, :], cols[:, R_GAMMA:R_GAMMA + 16], ALU.mult))
            V.tensor_tensor(keys_s[:], keysT[:], bcast(fold[:, 2, :].unsqueeze(2), [128, 2 * PH, NK]),
                            ALU.mult).then_inc(s_ks, 1)
            link(V.tensor_tensor(fold[:, 3, :], means[:], fold[:, 2, :], ALU.mult))
            link(V.tensor_tensor(fold[:, 3, :], cols[:, R_BETA:R_BETA + 16], fold[:, 3, :], ALU.subtract))
            V.tensor_tensor(keys_b[:], keysT[:], bcast(fold[:, 3, :].unsqueeze(2), [128, 2 * PH, NK]),
                            ALU.mult).then_inc(s_ks, 1)
            dve.wait_ge(s_fold, 1)
            V.tensor_copy(w_sim[:], ps[:, 0, :]).then_inc(s_folded, 1)
            dve.wait_ge(s_fold, 2)
            V.tensor_copy(b_sim[:], ps[:, 1, :]).then_inc(s_folded, 1)
            dve.wait_ge(s_folded, 2)

            state = {}
            expected = [0, PREP_LINKS, PREP_LINKS] + 2 * [PREP_LINKS + TAIL_LINKS] + [TAIL_LINKS]

            def settle():
                V.memset(spare[:], 0.0)

            def chain(ins):
                state["links"] += 1
                ins.then_inc(s_ch, 1)
                dve.wait_ge(s_ch, state["base"] + state["links"])

            def begin(step):
                assert state.get("links", 0) == expected.pop(0), state["links"]
                tails = 0 if isinstance(step, int) and step < SLOTS else TAIL_LINKS * (step - SLOTS)
                prepared = min(step, B) if isinstance(step, int) else step
                state.update(base=PREP_LINKS * prepared + tails, links=0)

            def prepare(u, p):
                hv = halves[p]
                yield
                dve.wait_ge(s_sim, u + 1)
                V.tensor_tensor(hv[:, :, 0:NK], ps[:, SIM, :].rearrange("t (r k) -> t r k", k=NK),
                                b_sim[:].rearrange("t (r k) -> t r k", k=NK), ALU.add).then_inc(s_biased, 1)
                yield
                dve.wait_ge(s_biased, u + 2)
                settle()
                for r in range(2 * PH):
                    ins = V.max(hv[:, r, NK:SEG], hv[:, r, 0:NK])
                chain(ins)
                yield
                chain(V.tensor_copy(mxs[p][:], hv[:, :, NK]))
                V.tensor_tensor(hv[:], hv[:], bcast(mxs[p][:].unsqueeze(2), [128, 2 * PH, SEG]),
                                ALU.subtract).then_inc(s_simc, 1)
                yield
                yield
                dve.wait_ge(s_exp, u + 1)
                chain(V.tensor_tensor(cand[p][:].rearrange("t h (a b) -> t h a b", a=TOP),
                                      bcast(hv[:, 0:PH, NK:SEG].unsqueeze(3), [128, PH, TOP, TOP]),
                                      bcast(hv[:, PH:2 * PH, NK:SEG].unsqueeze(2), [128, PH, TOP, TOP]), ALU.mult))
                yield
                settle()
                for h in range(PH):
                    ins = V.max(best[p][:, h, :], cand[p][:, h, :])
                chain(ins)
                chain(V.tensor_reduce(total[p][:], best[p][:], AX.X, ALU.add))
                V.reciprocal(inv[p][:], total[p][:]).then_inc(s_cut, 1)
                yield
                yield

            def mix(u, p):
                for h in range(PH):
                    dve.wait_ge(s_pr, PH * u + h + 1)
                    dve.wait_ge(s_mixed, PH * u + h + 1)
                    o = outer[h % BUFS][:]
                    V.scalar_tensor_tensor(out=kept[h % BUFS][:], in0=o, scalar=best[p][:, h, TOP - 1:TOP],
                                           in1=o, op0=ALU.is_ge, op1=ALU.mult).then_inc(s_kept, 1)
                    yield

            def tail(u, p):
                dve.wait_ge(s_mixed, PH * u + PH + BUFS)
                dve.wait_ge(s_g, u + 2)
                V.tensor_tensor(mixT[p][:].rearrange("e (b n) -> e b n", b=2), ps[:, MIX + 2 * p:MIX + 2 * p + 2, :],
                                act_T[p][:].rearrange("e (b n) -> e b n", b=2), ALU.mult).then_inc(s_mixT, 1)
                yield
                dve.wait_ge(s_y, u + 1)
                chain(V.tensor_tensor(z[p][:].unsqueeze(1), ps[:, OUT:OUT + 1, 0:128], x5[:, bass.ds(u, 1), :], ALU.add))
                chain(V.bn_stats(stats[:, p, :], z[p][:]))
                settle()
                chain(V.bn_aggr(mv[:, p, :], stats[:, p, :]))
                V.tensor_scalar(veps[:, p:p + 1], mv[:, p, 1:2], LN_EPS, None, ALU.add).then_inc(s_v, 1)
                yield
                dve.wait_ge(s_r, u + 1)
                dve.wait_ge(s_out[p], 8 * (u - p) + 16)
                V.tensor_scalar(y[p][:], z[p][:], mv[:, p, 0:1], rstd[:, p:p + 1], ALU.subtract,
                                ALU.mult).then_inc(s_fin, 1)
                yield

            last_steps(dve, DVE_LAST_ORDER, prepare, mix, tail, begin)


INPUTS = (
    "x", "ctx_2048", "mask_BxS2_if0", "L0_attn_W_qkv", "L0_attn_b_qkv", "L0_attn_W_proj", "L0_attn_b_proj",
    "L0_xattn_Wq", "L0_xattn_Wkv", "L0_xattn_null_kv", "L0_xattn_Wout", "L0_xattn_ln_scale",
    "L0_xattn_ln_bias", "L0_ffn_Wr", "L0_ffn_br", "L0_ffn_W1", "L0_ffn_b1", "L0_ffn_W2", "L0_ffn_b2",
    "L1_attn_Wq", "L1_attn_bq", "L1_attn_Wk", "L1_attn_bk", "L1_attn_Wv", "L1_attn_bv", "L1_attn_Wo",
    "L1_attn_bo", "L1_xattn_W_in", "L1_xattn_b_in", "L1_xattn_g_res", "L1_xattn_g_init", "L1_ffn_w_q",
    "L1_ffn_bn_gamma", "L1_ffn_bn_beta", "L1_ffn_keys", "L1_ffn_down_embed", "L1_ffn_up_embed")


def kernel(**inputs):
    import concourse.bacc as bacc
    from concourse.bass_utils import run_bass_kernel_spmd

    nc = bacc.Bacc("TRN2", target_bir_lowering=False, num_devices=1)
    arrays, args = {}, {}
    laid = {name: np.ascontiguousarray(inputs[name]) for name in INPUTS}
    laid["rel_rev"] = np.ascontiguousarray(np.asarray(inputs["L1_attn_rel_table"])[::-1].T)
    for name, arr in laid.items():
        arrays[f"in_{name}"] = arr
        args[name] = nc.dram_tensor(f"in_{name}", arr.shape, mybir.dt.from_np(arr.dtype),
                                    kind="ExternalInput").ap()
    result = nc.dram_tensor("result", [B, T, D], F32, kind="ExternalOutput").ap()
    build(nc, args, result)
    r = run_bass_kernel_spmd(nc, [arrays], core_ids=[0])
    return r.results[0]["result"]
```
